# Optimizing a Trainium2 kernel written in Bass

```python
import numpy as np
import jax
import jax.numpy as jnp

def _softmax(x, axis=-1):
    return jax.nn.softmax(x, axis=axis)

def _gelu(x):
    return jax.nn.gelu(x, approximate=True)

def _silu(x):
    return jax.nn.silu(x)

def _sigmoid(x):
    return jax.nn.sigmoid(x)

def _layernorm(x, axis=-1, eps=1e-05):
    m = jnp.mean(x, axis=axis, keepdims=True)
    v = jnp.var(x, axis=axis, keepdims=True)
    return (x - m) / jnp.sqrt(v + eps)

def _scatter_add(tgt, idx, src, axis=0):
    return tgt.at[idx].add(src)

def _segment_sum(src, seg, n):
    return jax.ops.segment_sum(src, seg, n)
kernel_name = 'mk_gps_d1_gnn_r8_49f28c'

def setup_inputs(seed: int=0):
    np.random.seed(seed)
    _w = jnp.asarray

    def _rec_inputs():
        import jax
        import jax.numpy as jnp
        _gk = jax.random.key(seed)
        x = -6.415e-05 + 1 * jax.random.normal(jax.random.fold_in(_gk, 1), (1250, 512), jnp.float32)
        src = jax.random.randint(jax.random.fold_in(_gk, 2), (40000,), 0, 1250, jnp.int32)
        dst = jax.random.randint(jax.random.fold_in(_gk, 3), (40000,), 0, 1250, jnp.int32)
        _o = jnp.argsort(dst, stable=True)
        src = src[_o]
        dst = dst[_o]
        return (x, src, dst)
    x, src, dst = _rec_inputs()

    def _L0_gnn_setup():
        import jax, jax.numpy as jnp
        import numpy as np
        NEG_SLOPE = 0.2
        HEADS = 8

        def gat_conv(x, src, dst, W, att_src, att_dst, bias, heads, out_ch):
            N = x.shape[0]
            h = (x @ W).reshape(N, heads, out_ch)
            a_src = jnp.einsum('nhc,hc->nh', h, att_src)
            a_dst = jnp.einsum('nhc,hc->nh', h, att_dst)
            e = jax.nn.leaky_relu(a_src[src] + a_dst[dst], NEG_SLOPE)
            m = jax.ops.segment_max(e, dst, num_segments=N)
            m = jnp.where(jnp.isfinite(m), m, jnp.zeros_like(m))
            ex = jnp.exp(e - m[dst])
            s = jax.ops.segment_sum(ex, dst, num_segments=N)
            alpha = ex / (s[dst] + 1e-16)
            msg = h[src] * alpha[:, :, None]
            out = jax.ops.segment_sum(msg, dst, num_segments=N)
            return out.reshape(N, heads * out_ch) + bias
        key = jax.random.key(seed)
        ks = jax.random.split(key, 12)
        N, F_in, nhid, heads, ncls, E = (2500, 512, 128, HEADS, 64, 25000)
        x = jax.random.normal(ks[0], (N, F_in), dtype=jnp.float32)
        edge_index = jax.random.randint(ks[1], (2, E), 0, N, dtype=jnp.int32)

        def lin(k, fi, fo):
            return jax.random.normal(k, (fi, fo), dtype=jnp.float32) / np.sqrt(fi)
        W1 = lin(ks[2], F_in, heads * nhid)
        att_src1 = jax.random.normal(ks[3], (heads, nhid), dtype=jnp.float32) / np.sqrt(nhid)
        att_dst1 = jax.random.normal(ks[4], (heads, nhid), dtype=jnp.float32) / np.sqrt(nhid)
        b1 = jnp.zeros((heads * nhid,), dtype=jnp.float32)
        W2 = lin(ks[5], heads * nhid, heads * ncls)
        att_src2 = jax.random.normal(ks[6], (heads, ncls), dtype=jnp.float32) / np.sqrt(ncls)
        att_dst2 = jax.random.normal(ks[7], (heads, ncls), dtype=jnp.float32) / np.sqrt(ncls)
        b2 = jnp.zeros((heads * ncls,), dtype=jnp.float32)
        return {'x': x, 'edge_index': edge_index, 'W1': W1, 'att_src1': att_src1, 'att_dst1': att_dst1, 'b1': b1, 'W2': W2, 'att_src2': att_src2, 'att_dst2': att_dst2, 'b2': b2}
    _L0_gnn_all = _L0_gnn_setup()
    _L0_gnn_in = {k: v for k, v in _L0_gnn_all.items() if k in ('W1', 'att_src1', 'att_dst1', 'b1', 'W2', 'att_src2', 'att_dst2', 'b2')}
    del _L0_gnn_all

    def _L0_mix_setup():
        import jax, jax.numpy as jnp
        import numpy as np
        B, N, DIM = (2, 512, 512)
        HEADS, DIM_HEAD = (8, 64)
        INNER = HEADS * DIM_HEAD
        SCALE = DIM_HEAD ** (-0.5)
        LN_EPS = 1e-05

        def _layernorm(x, gamma, beta):
            mu = jnp.mean(x, axis=-1, keepdims=True)
            var = jnp.mean(jnp.square(x - mu), axis=-1, keepdims=True)
            return (x - mu) * jax.lax.rsqrt(var + LN_EPS) * gamma + beta
        key = jax.random.key(seed)
        ks = jax.random.split(key, 4)
        x = jax.random.normal(ks[0], (B, N, DIM), dtype=jnp.float32)
        w_qkv = jax.random.normal(ks[1], (DIM, 3 * INNER), dtype=jnp.float32) * DIM ** (-0.5)
        ln_gamma = jnp.ones((INNER,), dtype=jnp.float32)
        ln_beta = jnp.zeros((INNER,), dtype=jnp.float32)
        w_out = jax.random.normal(ks[2], (INNER, DIM), dtype=jnp.float32) * INNER ** (-0.5)
        b_out = jnp.zeros((DIM,), dtype=jnp.float32)
        return {'x': x, 'w_qkv': w_qkv, 'ln_gamma': ln_gamma, 'ln_beta': ln_beta, 'w_out': w_out, 'b_out': b_out}
    _L0_mix_all = _L0_mix_setup()
    _L0_mix_in = {k: v for k, v in _L0_mix_all.items() if k in ('w_qkv', 'ln_gamma', 'ln_beta', 'w_out', 'b_out')}
    del _L0_mix_all

    def _L0_ffn_setup():
        import jax, jax.numpy as jnp
        import numpy as np
        E = 64
        K = 2
        CAP = 512
        H = 512
        FFN = 256
        B, S = (8, 512)
        key = jax.random.key(seed)
        ks = jax.random.split(key, 6)
        hidden_states = jax.random.normal(ks[0], (B, S, H), dtype=jnp.float32)
        router_w = jax.random.normal(ks[1], (E, H), dtype=jnp.float32) * (0.01 / np.sqrt(H))
        w1 = jax.random.normal(ks[2], (FFN, H), dtype=jnp.float32) * (1.0 / np.sqrt(H))
        b1 = jnp.zeros((FFN,), dtype=jnp.float32)
        w2 = jax.random.normal(ks[3], (H, FFN), dtype=jnp.float32) * (1.0 / np.sqrt(FFN))
        b2 = jnp.zeros((H,), dtype=jnp.float32)
        return {'hidden_states': hidden_states, 'router_w': router_w, 'w1': w1, 'b1': b1, 'w2': w2, 'b2': b2}
    _L0_ffn_all = _L0_ffn_setup()
    _L0_ffn_in = {k: v for k, v in _L0_ffn_all.items() if k in ('router_w', 'w1', 'b1', 'w2', 'b2')}
    del _L0_ffn_all
    return {'x': x, 'src': src, 'dst': dst, 'L0_gnn_W1': _L0_gnn_in['W1'], 'L0_gnn_att_src1': _L0_gnn_in['att_src1'], 'L0_gnn_att_dst1': _L0_gnn_in['att_dst1'], 'L0_gnn_b1': _L0_gnn_in['b1'], 'L0_gnn_W2': _L0_gnn_in['W2'], 'L0_gnn_att_src2': _L0_gnn_in['att_src2'], 'L0_gnn_att_dst2': _L0_gnn_in['att_dst2'], 'L0_gnn_b2': _L0_gnn_in['b2'], 'L0_mix_w_qkv': _L0_mix_in['w_qkv'], 'L0_mix_ln_gamma': _L0_mix_in['ln_gamma'], 'L0_mix_ln_beta': _L0_mix_in['ln_beta'], 'L0_mix_w_out': _L0_mix_in['w_out'], 'L0_mix_b_out': _L0_mix_in['b_out'], 'L0_ffn_router_w': _L0_ffn_in['router_w'], 'L0_ffn_w1': _L0_ffn_in['w1'], 'L0_ffn_b1': _L0_ffn_in['b1'], 'L0_ffn_w2': _L0_ffn_in['w2'], 'L0_ffn_b2': _L0_ffn_in['b2']}

def reference(x, src, dst, L0_gnn_W1, L0_gnn_att_src1, L0_gnn_att_dst1, L0_gnn_b1, L0_gnn_W2, L0_gnn_att_src2, L0_gnn_att_dst2, L0_gnn_b2, L0_mix_w_qkv, L0_mix_ln_gamma, L0_mix_ln_beta, L0_mix_w_out, L0_mix_b_out, L0_ffn_router_w, L0_ffn_w1, L0_ffn_b1, L0_ffn_w2, L0_ffn_b2):
    import jax
    import jax.numpy as jnp

    def _L0_gnn_ref(x, edge_index, W1, att_src1, att_dst1, b1, W2, att_src2, att_dst2, b2):
        import jax, jax.numpy as jnp
        import numpy as np
        NEG_SLOPE = 0.2
        HEADS = 8

        def gat_conv(x, src, dst, W, att_src, att_dst, bias, heads, out_ch):
            N = x.shape[0]
            h = (x @ W).reshape(N, heads, out_ch)
            a_src = jnp.einsum('nhc,hc->nh', h, att_src)
            a_dst = jnp.einsum('nhc,hc->nh', h, att_dst)
            e = jax.nn.leaky_relu(a_src[src] + a_dst[dst], NEG_SLOPE)
            m = jax.ops.segment_max(e, dst, num_segments=N)
            m = jnp.where(jnp.isfinite(m), m, jnp.zeros_like(m))
            ex = jnp.exp(e - m[dst])
            s = jax.ops.segment_sum(ex, dst, num_segments=N)
            alpha = ex / (s[dst] + 1e-16)
            msg = h[src] * alpha[:, :, None]
            out = jax.ops.segment_sum(msg, dst, num_segments=N)
            return out.reshape(N, heads * out_ch) + bias
        N = x.shape[0]
        nhid = att_src1.shape[1]
        ncls = att_src2.shape[1]
        loop = jnp.arange(N, dtype=edge_index.dtype)
        src = jnp.concatenate([edge_index[0], loop])
        dst = jnp.concatenate([edge_index[1], loop])
        h = gat_conv(x, src, dst, W1, att_src1, att_dst1, b1, HEADS, nhid)
        h = jax.nn.relu(h)
        out = gat_conv(h, src, dst, W2, att_src2, att_dst2, b2, HEADS, ncls)
        return jax.nn.log_softmax(out, axis=1)

    def _L0_mix_ref(x, w_qkv, ln_gamma, ln_beta, w_out, b_out):
        import jax, jax.numpy as jnp
        import numpy as np
        B, N, DIM = (2, 512, 512)
        HEADS, DIM_HEAD = (8, 64)
        INNER = HEADS * DIM_HEAD
        SCALE = DIM_HEAD ** (-0.5)
        LN_EPS = 1e-05

        def _layernorm(x, gamma, beta):
            mu = jnp.mean(x, axis=-1, keepdims=True)
            var = jnp.mean(jnp.square(x - mu), axis=-1, keepdims=True)
            return (x - mu) * jax.lax.rsqrt(var + LN_EPS) * gamma + beta
        b, n, _ = x.shape
        qkv = x @ w_qkv
        q, k, v = jnp.split(qkv, 3, axis=-1)

        def to_heads(t):
            return t.reshape(b, n, HEADS, DIM_HEAD).transpose(0, 2, 1, 3)
        q, k, v = (to_heads(q), to_heads(k), to_heads(v))
        dots = jnp.einsum('bhid,bhjd->bhij', q, k) * SCALE
        attn = jax.nn.relu(dots)
        out = jnp.einsum('bhij,bhjd->bhid', attn, v)
        out = out.transpose(0, 2, 1, 3).reshape(b, n, INNER)
        out = _layernorm(out, ln_gamma, ln_beta)
        return out @ w_out + b_out

    def _L0_ffn_ref(hidden_states, router_w, w1, b1, w2, b2):
        import jax, jax.numpy as jnp
        import numpy as np
        E = 64
        K = 2
        CAP = 512
        H = 512
        FFN = 256
        B, S = (8, 512)
        orig_shape = hidden_states.shape
        x = hidden_states.reshape(-1, orig_shape[-1])
        T = x.shape[0]
        N = T * K
        logits = jnp.einsum('th,eh->te', x, router_w)
        probs_full = jax.nn.softmax(logits, axis=-1)
        probs, idx = jax.lax.top_k(probs_full, K)
        flat_e = idx.reshape(-1)
        flat_p = probs.reshape(-1)
        order = jnp.argsort(flat_e, stable=True)
        sorted_e = flat_e[order]
        counts = jnp.zeros((E,), jnp.int32).at[flat_e].add(1)
        offsets = jnp.concatenate([jnp.zeros((1,), jnp.int32), jnp.cumsum(counts)[:-1]])
        pos = jnp.arange(N, dtype=jnp.int32) - offsets[sorted_e]
        keep = pos < CAP
        slot = sorted_e * CAP + jnp.minimum(pos, CAP - 1)
        dest = jnp.where(keep, slot, E * CAP)
        tok = order // K
        buf = jnp.zeros((E * CAP + 1, x.shape[-1]), x.dtype).at[dest].set(x[tok])
        buf = buf[:-1]
        h = jax.nn.gelu(jnp.einsum('nh,fh->nf', buf, w1) + b1, approximate=False)
        y = jnp.einsum('nf,hf->nh', h, w2) + b2
        gate = jnp.where(keep, flat_p[order], 0.0)
        contrib = y[jnp.minimum(slot, E * CAP - 1)] * gate[:, None]
        out = jnp.zeros_like(x).at[tok].add(contrib)
        return out.reshape(orig_shape)
    edge_index = jnp.stack([src, dst])
    xn = _layernorm(x, axis=-1)
    x = x + _L0_gnn_ref(xn, edge_index, L0_gnn_W1, L0_gnn_att_src1, L0_gnn_att_dst1, L0_gnn_b1, L0_gnn_W2, L0_gnn_att_src2, L0_gnn_att_dst2, L0_gnn_b2) + _L0_mix_ref(xn[None], L0_mix_w_qkv, L0_mix_ln_gamma, L0_mix_ln_beta, L0_mix_w_out, L0_mix_b_out)[0]
    x = x + _L0_ffn_ref(_layernorm(x, axis=-1)[None], L0_ffn_router_w, L0_ffn_w1, L0_ffn_b1, L0_ffn_w2, L0_ffn_b2)[0]
    return x

_drawn_inputs = setup_inputs


def setup_inputs(seed=0):
    import zlib

    import numpy as np

    out = dict(_drawn_inputs(seed))
    spreads = {'L0_gnn_b1': (0.0, 0.8),
     'L0_gnn_b2': (0.0, 2.0),
     'L0_mix_ln_gamma': (1.0, 0.6),
     'L0_mix_ln_beta': (0.0, 2.0),
     'L0_mix_b_out': (0.0, 2.0),
     'L0_ffn_b1': (0.0, 2.0),
     'L0_ffn_b2': (0.0, 2.0)}
    factors = {'L0_gnn_W1': 8.0,
     'L0_gnn_att_src1': 8.0,
     'L0_gnn_att_dst1': 8.0,
     'L0_gnn_W2': 2.893,
     'L0_gnn_att_src2': 8.0,
     'L0_gnn_att_dst2': 120.091,
     'L0_ffn_router_w': 200.0,
     'L0_ffn_w1': 8.0,
     'L0_ffn_w2': 8.0,
     'L0_mix_w_qkv': 2.996}
    for name, (base, spread) in spreads.items():
        noise = np.random.default_rng([zlib.crc32(name.encode()), seed]).standard_normal(out[name].shape)
        drawn = base * np.exp(spread * noise) if base else spread * noise
        out[name] = jnp.asarray(drawn.astype(out[name].dtype))
    for name, factor in factors.items():
        out[name] = (out[name] * factor).astype(out[name].dtype)
    return out
```

```python
from contextlib import ExitStack

import concourse.bass as bass
from concourse import mybir

F32 = mybir.dt.float32
BF16 = mybir.dt.bfloat16
I32 = mybir.dt.int32
I16 = mybir.dt.int16
U16 = mybir.dt.uint16
U32 = mybir.dt.uint32
ALU = mybir.AluOpType
ACT = mybir.ActivationFunctionType
AX = mybir.AxisListType.X

R = 125
BANK = 512
BIG = 1.0e30
LN_EPS = 1e-5
SLOPE = 0.2
WIN = 40
MARGIN = 4
CAP = 512


def ds(i, n):
    return bass.ds(i, n)


class Semaphores:

    def __init__(self, nc):
        self.nc, self.held = nc, []

    def new(self, name):
        self.held.append(self.nc.alloc_semaphore(name))
        return self.held[-1]

    def start_over(self):
        self.nc.clear_and_free_semaphores(self.held)
        self.nc.all_engine_barrier()
        self.held = []


class Shapes:
    def __init__(self, nc, x, src, w1, att, att2, w_out, router, ffn_w1):
        self.sems = Semaphores(nc)
        self.N, self.D = x.shape
        self.T = self.N // R
        self.E = src.shape[0]
        self.ET = self.E // R
        self.H, self.C1 = att.shape
        self.C2 = att2.shape[1]
        self.HC = w1.shape[1]
        self.KC = self.D // 128
        self.NE = router.shape[0]
        self.F = ffn_w1.shape[0]
        assert self.N == self.T * R and self.E == self.ET * R and self.ET % self.T == 0
        assert self.ET // self.T + 2 * MARGIN == WIN


class Chain:

    def __init__(self, engine, sem, base=0):
        self.engine, self.sem, self.base, self.n = engine, sem, base, 0

    def at(self, base):
        self.base, self.n = base, 0

    def __call__(self, instruction):
        self.n += 1
        instruction.then_inc(self.sem, 1)
        self.engine.wait_ge(self.sem, self.base + self.n)


def one_over_sqrt(dve, link, std, ve, out, std_ready, value, scratch):
    dve.wait_ge(std_ready, value)
    link(dve.reciprocal(out, std))
    link(dve.tensor_tensor(scratch, out, out, ALU.mult))
    link(dve.tensor_tensor(scratch, scratch, ve, ALU.mult))
    link(dve.tensor_scalar(scratch, scratch, -0.5, 1.5, ALU.mult, ALU.add))
    link(dve.tensor_tensor(out, out, scratch, ALU.mult))


def project(nc, s, x, w1, wqkv, att_src1, att_dst1, RA, RB, h1, ident, adcol, rows_dram):
    T, KC, H, D, C1, HC, N = s.T, s.KC, s.H, s.D, s.C1, s.HC, s.N
    W1 = RA[:, 0:KC * HC].rearrange("p (k n) -> p k n", k=KC)
    WQKV = RA[:, KC * HC:KC * (HC + 3 * D)].rearrange("p (k n) -> p k n", k=KC)
    M = 2 * D // 128
    QK = RB[:, 0:M * N].rearrange("p (m n) -> p m n", m=M)
    V = RB[0:R, M * N:M * N + T * D].rearrange("p (t n) -> p t n", t=T)
    with ExitStack() as ctx:
        def sb(name, shape, dt=F32):
            return ctx.enter_context(nc.sbuf_tensor(name, shape, dt))

        def ps(name, shape, dt=F32):
            return ctx.enter_context(nc.psum_tensor(name, shape, dt))

        def sem(name):
            return s.sems.new(name)

        xs = [sb(f"x_in{i}", [R, D]) for i in range(2)]
        xn = [sb(f"xn{i}", [R, D]) for i in range(2)]
        xT = [sb(f"xnT{i}", [128, KC, R]) for i in range(2)]
        xT_all = sb("xnT_all", [128, KC, N])
        attb = sb("att1_rows", [128, 2, HC])
        watt = sb("w1_att", [128, KC, 2 * H])
        prod = sb("w1_att_prod", [128, HC])
        stat = sb("ln_stat", [R, T, 6])
        mv = sb("ln_mean_var", [R, T, 2])
        ve, std, rstd, scratch = (sb(f"ln_{n}", [R, T]) for n in ("var_eps", "std", "rstd", "scratch"))
        rows = sb("att1_scores", [2 * H, N])
        p_xT = ps("p_xT", [128, BANK])
        p_h1 = ps("p_h1", [R, 2 * BANK])
        p_v = ps("p_v", [R, BANK])
        p_qk = ps("p_qk", [128, 2, BANK])
        NB = 3
        CB = [(k * BANK, min(N - k * BANK, BANK)) for k in range(NB)]

        x_loaded = [sem(f"x_loaded{i}") for i in range(2)]
        w_loaded, wq_loaded, att_loaded = sem("w1_loaded"), sem("wqkv_loaded"), sem("att1_loaded")
        x_used, std_ready, var_ready = sem("x_used"), sem("std_ready"), sem("var_ready")
        xn_ready, ones_ready = sem("xn_ready"), sem("h1_ones_ready")
        xT_done, xT_copied, xT_kept = sem("xT_done"), sem("xT_copied"), sem("xT_kept")
        qk_done, qk_out, h1_done, h1_out = sem("qk_done"), sem("qk_out"), sem("h1_done"), sem("h1_out")
        v_done, v_out = sem("v_done"), sem("v_out")
        watt_ready, row_done, row_out = sem("watt_ready"), sem("row_done"), sem("row_out")
        col_done, col_out, rows_stored = sem("col_done"), sem("col_out"), sem("rows_stored")
        vec_chain, pool_chain = sem("p1_vec_chain"), sem("p1_pool_chain")
        p_row = [p_h1[0:2 * H, 0:BANK], p_h1[0:2 * H, BANK:2 * BANK], p_v[0:2 * H, :]]
        p_col = p_xT[0:R, 0:T * 2 * H]
        block = ctx.enter_context(nc.Block())

        @block.sync
        def _(sp):
            for i in range(2):
                sp.dma_start(xs[i][:, :], x[i * R:(i + 1) * R, :]).then_inc(x_loaded[i], 16)
            with sp.Fori(1, T // 2) as u:
                for i in range(2):
                    sp.wait_ge(x_used, 2 * u - 1 + i)
                    sp.dma_start(xs[i][:, :], x[ds((2 * u + i) * R, R), :]).then_inc(x_loaded[i], 16)
            with sp.Fori(0, T // 2) as u:
                for i in range(2):
                    sp.wait_ge(x_used, T + 2 * u - 1 + i)
                    sp.dma_start(xs[i][:, :], x[ds((2 * u + i) * R, R), :]).then_inc(x_loaded[i], 16)
            sp.wait_ge(row_out, NB)
            sp.dma_start(rows_dram, rows[0:H, :]).then_inc(rows_stored, 16)
            sp.wait_ge(rows_stored, 16)

        @block.gpsimd
        def _(pool):
            link = Chain(pool, pool_chain)
            prods = prod[:, :].rearrange("p (h c) -> p h c", h=H)
            pool.wait_ge(w_loaded, 16)
            pool.wait_ge(att_loaded, 32)
            for k in range(KC):
                for j in range(2):
                    link(pool.tensor_tensor(prod[:, :], W1[:, k, :], attb[:, j, :], ALU.mult))
                    c = C1 // 2
                    while c:
                        left, right = prods[:, :, 0:c], prods[:, :, c:2 * c]
                        to = left if c > 1 else watt[:, k, j * H:(j + 1) * H].rearrange("p (h c) -> p h c", c=1)
                        link(pool.tensor_tensor(to, left, right, ALU.add))
                        c //= 2
            pool.sem_inc(watt_ready, 1)

        @block.vector
        def _(dve):
            link = Chain(dve, vec_chain)
            dve.memset(h1[:, :, :, C1:C1 + 1], 1.0).then_inc(ones_ready, 1)
            with dve.Fori(0, T // 2) as u:
                for i in range(2):
                    t = 2 * u + i
                    dve.wait_ge(x_loaded[i], 16 * (u + 1))
                    dve.bn_stats(stat[:, ds(t, 1), :].rearrange("p a b -> p (a b)"), xs[i][:, :]).then_inc(x_used, 1)
            dve.wait_ge(x_used, T)
            for t in range(T):
                ins = dve.bn_aggr(mv[:, t, :], stat[:, t, :])
            link(ins)
            dve.tensor_scalar(ve[:, :], mv[:, :, 1], LN_EPS, None, ALU.add).then_inc(var_ready, 1)
            dve.wait_ge(var_ready, 1)
            one_over_sqrt(dve, link, std[:, :], ve[:, :], rstd[:, :], std_ready, 1, scratch[:, :])
            with dve.Fori(0, T // 2) as u:
                for i in range(2):
                    t = 2 * u + i
                    dve.wait_ge(x_loaded[i], 16 * (u + 1 + T // 2))
                    dve.wait_ge(xT_done, t)
                    dve.tensor_scalar(xn[i][:, :], xs[i][:, :], mv[:, ds(t, 1), 0], rstd[:, ds(t, 1)],
                                      ALU.subtract, ALU.mult).then_inc(x_used, 1)
                    dve.wait_ge(xT_copied, t + 1)
                    dve.tensor_copy(xT_all[:, :, ds(t * R, R)], xT[i][:, :, :])\
                       .then_inc(xT_kept, 1)
                    dve.wait_ge(qk_done, t + 1)
                    dve.tensor_copy(QK[:, :, ds(t * R, R)].rearrange("p (b m) r -> p b m r", b=2),
                                    p_qk[:, :, 0:4 * R].rearrange("p b (m r) -> p b m r", m=4)).then_inc(qk_out, 1)
            for k, (c0, w) in enumerate(CB):
                dve.wait_ge(row_done, k + 1)
                dve.tensor_copy(rows[:, c0:c0 + w], p_row[k][:, 0:w]).then_inc(row_out, 1)
            dve.wait_ge(col_done, 1)
            dve.tensor_copy(adcol[:, :, :], p_col.rearrange("p (t h) -> p t h", t=T)).then_inc(col_out, 1)
            dve.wait_ge(col_out, 1)

        @block.scalar
        def _(act):
            act.dma_start(WQKV, wqkv.rearrange("(k p) n -> p k n", p=128)).then_inc(wq_loaded, 16)
            act.dma_start(W1, w1.rearrange("(k p) n -> p k n", p=128)).then_inc(w_loaded, 16)
            for j, a in enumerate((att_src1, att_dst1)):
                act.dma_start(attb[:, j, :], a.rearrange("h c -> (h c)")[None, :].to_broadcast([128, HC]))\
                   .then_inc(att_loaded, 16)
            act.wait_ge(var_ready, 1)
            act.activation(std[:, :], ve[:, :], ACT.Sqrt).then_inc(std_ready, 1)
            act.wait_ge(ones_ready, 1)
            with act.Fori(0, T // 2) as u:
                for i in range(2):
                    t = 2 * u + i
                    act.wait_ge(xT_done, t + 1)
                    act.wait_ge(v_done, t)
                    act.wait_ge(xT_kept, t)
                    act.activation(xT[i][:, :, :].rearrange("p k r -> p (k r)"), p_xT[:, 0:KC * R], ACT.Copy)\
                       .then_inc(xT_copied, 1)
                    act.wait_ge(h1_done, t + 1)
                    act.activation(h1[:, ds(t, 1), :, 0:C1].rearrange("p a h c -> p (a h) c"),
                                   p_h1[:, :].rearrange("p (h c) -> p h c", h=H), ACT.Copy).then_inc(h1_out, 1)
                    act.wait_ge(v_done, t + 1)
                    act.activation(V[:, ds(t, 1), :].rearrange("p a n -> p (a n)"), p_v[:, :], ACT.Copy)\
                       .then_inc(v_out, 1)

        @block.tensor
        def _(pe):
            pe.wait_ge(wq_loaded, 16)
            pe.wait_ge(w_loaded, 16)
            with pe.Fori(0, T // 2) as u:
                for i in range(2):
                    t = 2 * u + i
                    pe.wait_ge(x_used, T + t + 1)
                    pe.wait_ge(xT_copied, t)
                    for k in range(KC):
                        last = pe.transpose(p_xT[:, k * R:(k + 1) * R], xn[i][:, k * 128:(k + 1) * 128], ident[0:R, 0:R])
                    last.then_inc(xT_done, 1)
                    pe.wait_ge(xT_copied, t + 1)
                    pe.wait_ge(qk_out, t)
                    for m in range(M):
                        for k in range(KC):
                            last = pe.matmul(p_qk[:, m // 4, m % 4 * R:(m % 4 + 1) * R], WQKV[:, k, m * 128:(m + 1) * 128],
                                             xT[i][:, k, :], start=k == 0, stop=k == KC - 1)
                    last.then_inc(qk_done, 1)
                    pe.wait_ge(h1_out, t)
                    for n in range(HC // BANK):
                        for k in range(KC):
                            last = pe.matmul(p_h1[:, n * BANK:(n + 1) * BANK], xT[i][:, k, :],
                                             W1[:, k, n * BANK:(n + 1) * BANK], start=k == 0, stop=k == KC - 1)
                    last.then_inc(h1_done, 1)
                    pe.wait_ge(v_out, t)
                    for k in range(KC):
                        last = pe.matmul(p_v[:, :], xT[i][:, k, :], WQKV[:, k, 2 * D:3 * D], start=k == 0, stop=k == KC - 1)
                    last.then_inc(v_done, 1)
            pe.wait_ge(watt_ready, 1)
            pe.wait_ge(xT_kept, T)
            pe.wait_ge(h1_out, T)
            pe.wait_ge(v_out, T)
            for b, (c0, w) in enumerate(CB):
                for k in range(KC):
                    last = pe.matmul(p_row[b][:, 0:w], watt[:, k, :], xT_all[:, k, c0:c0 + w], start=k == 0, stop=k == KC - 1)
                last.then_inc(row_done, 1)
            pe.wait_ge(xT_copied, T)
            pe.wait_ge(row_out, NB)
            for t in range(T):
                last = pe.transpose(p_col[:, t * 2 * H:(t + 1) * 2 * H], rows[:, t * R:(t + 1) * R], ident[0:2 * H, 0:2 * H])
            last.then_inc(col_done, 1)


def relu_attention(nc, s, x, gamma, beta, w_out, b_out, w2, att_src2, att_dst2, w2att, RB, ident, mix_dram):
    T, KC, H, D, N = s.T, s.KC, s.H, s.D, s.N
    M = 2 * D // 128
    C = D // H
    QK = RB[:, 0:M * N].rearrange("p (m n) -> p m n", m=M)
    V = RB[0:R, M * N:M * N + T * D].rearrange("p (t n) -> p t n", t=T)
    PAIRS = H // 2
    SCALE = float(C) ** -0.5
    GROUPS = ((0, 4), (4, 8), (8, T))
    with ExitStack() as ctx:
        def sb(name, shape, dt=F32):
            return ctx.enter_context(nc.sbuf_tensor(name, shape, dt))

        def ps(name, shape, dt=F32):
            return ctx.enter_context(nc.psum_tensor(name, shape, dt))

        def sem(name):
            return s.sems.new(name)

        WO = sb("w_out_sb", [128, KC, D])
        gcol, bcol = sb("mix_gamma", [128, KC]), sb("mix_beta", [128, KC])
        boutb = sb("b_out_rows", [R, D])
        q = [sb(f"q_tile{i}", [128, R]) for i in range(2)]
        at = [[sb(f"relu_scores{i}{e}", [R, T, R]) for e in range(2)] for i in range(2)]
        o = sb("mix_heads", [R, D])
        on = sb("mix_normed", [R, D])
        oT = sb("mix_normed_T", [128, KC, R])
        y, xt = sb("mix_out", [R, D]), sb("mix_x", [R, D])
        K2, C2 = s.HC // 128, s.C2
        W2 = sb("w2_for_att", [128, K2, H * C2])
        attb = sb("att2_rows", [128, 2, H * C2])
        prod = sb("w2_att_prod", [128, H * C2])
        stat, mv = sb("mix_stat", [R, 6]), sb("mix_mv", [R, 2])
        ve, std, rstd, scratch = (sb(f"mix_{n}", [R, 1]) for n in ("var_eps", "std", "rstd", "scratch"))
        p_s = [ps(f"p_scores{e}", [R, 3, BANK]) for e in range(2)]
        p_o = ps("p_heads", [R, BANK])
        p_y = ps("p_mix_out", [128, BANK])

        loaded, q_ready, s_done = sem("mix_loaded"), sem("q_ready"), sem("scores_done")
        relu_act, relu_dve, pv_done = sem("relu_even_ready"), sem("relu_odd_ready"), sem("pv_done")
        o_out, mvar, mstd, on_ready = sem("heads_out"), sem("mix_var_ready"), sem("mix_std_ready"), sem("on_ready")
        oT_done, oT_out, y_done, y_out, stored = (sem(n) for n in ("oT_done", "oT_out", "mixy_done", "mixy_out", "mix_stored"))
        vec_chain, pool_chain, turns = sem("mix_vec_chain"), sem("mix_pool_chain"), sem("mix_turns")
        x_loaded, w2_loaded, y_added = sem("mix_x_loaded"), sem("w2_att_loaded"), sem("mix_x_added")
        block = ctx.enter_context(nc.Block())

        @block.sync
        def _(sp):
            sp.dma_start(WO[:, :, :], w_out.rearrange("(k p) n -> p k n", p=128)).then_inc(loaded, 16)
            sp.dma_start(boutb[:, :], b_out[None, :].to_broadcast([R, D])).then_inc(loaded, 16)
            with nc.allow_non_contiguous_dma(reason="two vectors, once"):
                sp.dma_start(gcol[:, :], gamma.rearrange("(k p) -> p k", p=128)).then_inc(loaded, 16)
                sp.dma_start(bcol[:, :], beta.rearrange("(k p) -> p k", p=128)).then_inc(loaded, 16)
            sp.dma_start(W2[:, :, :], w2.rearrange("(k p) n -> p k n", p=128)).then_inc(w2_loaded, 16)
            for j, a in enumerate((att_src2, att_dst2)):
                sp.dma_start(attb[:, j, :], a.rearrange("h c -> (h c)")[None, :].to_broadcast([128, H * C2]))\
                  .then_inc(w2_loaded, 16)
            with sp.Fori(0, T) as t:
                sp.wait_ge(y_added, t)
                sp.dma_start(xt[:, :], x[ds(t * R, R), :]).then_inc(x_loaded, 16)
                sp.wait_ge(y_added, t + 1)
                sp.dma_start(mix_dram[ds(t * R, R), :], y[:, :]).then_inc(stored, 16)
            sp.wait_ge(stored, 16 * T)

        @block.gpsimd
        def _(pool):
            def tiles(t, first):
                for p in range(PAIRS):
                    if not (first and p == 0):
                        pool.wait_ge(s_done, (t * PAIRS + p - 1) * 2)
                    pool.tensor_copy(q[p % 2][:, :], QK[:, p, ds(t * R, R)]).then_inc(q_ready, 1)

            tiles(0, True)
            link = Chain(pool, pool_chain)
            prods = prod[:, :].rearrange("p (h c) -> p h c", h=H)
            pool.wait_ge(w2_loaded, 48)
            with pool.Fori(1, T) as t:
                tiles(t, False)
            for k in range(K2):
                for j in range(2):
                    link(pool.tensor_tensor(prod[:, :], W2[:, k, :], attb[:, j, :], ALU.mult))
                    c = C2 // 2
                    while c:
                        left, right = prods[:, :, 0:c], prods[:, :, c:2 * c]
                        to = left if c > 1 else w2att[:, k, j * H:(j + 1) * H].rearrange("p (h c) -> p h c", c=1)
                        link(pool.tensor_tensor(to, left, right, ALU.add))
                        c //= 2

        def relu_shape(p_tile, at_tile):
            return ((at_tile[:, 0:8, :].rearrange("p (b m) r -> p b (m r)", b=2), p_tile[:, 0:2, 0:4 * R]),
                    (at_tile[:, 8:T, :].rearrange("p m r -> p (m r)"), p_tile[:, 2, 0:(T - 8) * R]))

        def tail_act(act, t):
            act.wait_ge(mvar, t + 1)
            act.activation(std[:, :], ve[:, :], ACT.Sqrt).then_inc(mstd, 1)
            act.wait_ge(oT_done, t + 1)
            for k in range(KC):
                act.activation(oT[:, k, :], p_y[:, k * R:(k + 1) * R], ACT.Identity,
                               bias=bcol[:, k:k + 1], scale=gcol[:, k:k + 1]).then_inc(oT_out, 1)

        @block.scalar
        def _(act):
            act.wait_ge(loaded, 64)

            def pairs(t, first):
                for p in range(PAIRS):
                    n = t * PAIRS + p
                    act.wait_ge(s_done, 2 * n + 1)
                    if first and p < 2:
                        pass
                    else:
                        act.wait_ge(pv_done, 2 * (n - 2) + 1)
                    for j, (dst, src) in enumerate(relu_shape(p_s[0], at[p % 2][0])):
                        ins = act.activation(dst, src, ACT.Relu, scale=SCALE)
                    ins.then_inc(relu_act, 1)
                    if p == 0 and not first:
                        tail_act(act, t - 1)

            pairs(0, True)
            with act.Fori(1, T) as t:
                pairs(t, False)
            tail_act(act, T - 1)

        def tail_norm(dve, link, t):
            dve.wait_ge(pv_done, (t + 1) * 2 * PAIRS)
            link(dve.tensor_copy(o[:, :], p_o[:, :]))
            dve.sem_inc(o_out, 1)
            link(dve.bn_stats(stat[:, :], o[:, :]))
            dve.sem_inc(turns, 1)
            link(dve.bn_aggr(mv[:, :], stat[:, :]))
            link(dve.tensor_scalar(ve[:, :], mv[:, 1:2], LN_EPS, None, ALU.add))
            dve.sem_inc(mvar, 1)
            one_over_sqrt(dve, link, std[:, :], ve[:, :], rstd[:, :], mstd, t + 1, scratch[:, :])
            dve.tensor_scalar(on[:, :], o[:, :], mv[:, 0:1], rstd[:, 0:1], ALU.subtract, ALU.mult).then_inc(on_ready, 1)

        NORM_LINKS = 9

        def tail_out(dve, t):
            dve.wait_ge(y_done, t + 1)
            dve.wait_ge(stored, 16 * t)
            dve.tensor_tensor(y[:, :], p_y[0:R, :], boutb[:, :], ALU.add).then_inc(y_out, 1)
            dve.wait_ge(x_loaded, 16 * (t + 1))
            dve.wait_ge(y_out, t + 1)
            dve.tensor_tensor(y[:, :], y[:, :], xt[:, :], ALU.add).then_inc(y_added, 1)

        @block.vector
        def _(dve):
            link = Chain(dve, vec_chain)
            dve.wait_ge(loaded, 64)

            def pairs(t, first):
                for p in range(PAIRS):
                    n = t * PAIRS + p
                    dve.wait_ge(s_done, 2 * n + 2)
                    if not (first and p < 2):
                        dve.wait_ge(pv_done, 2 * (n - 2) + 2)
                    for j, (dst, src) in enumerate(relu_shape(p_s[1], at[p % 2][1])):
                        ins = dve.tensor_scalar(dst, src, SCALE, 0.0, ALU.mult, ALU.max)
                    ins.then_inc(relu_dve, 1)
                    if p == 0 and not first:
                        link.at((t - 1) * NORM_LINKS)
                        tail_norm(dve, link, t - 1)
                        assert link.n == NORM_LINKS
                    if p == 2 and not first:
                        tail_out(dve, t - 1)

            pairs(0, True)
            with dve.Fori(1, T) as t:
                pairs(t, False)
            link.at((T - 1) * NORM_LINKS)
            tail_norm(dve, link, T - 1)
            tail_out(dve, T - 1)
            dve.wait_ge(stored, 16 * T)

        def scores(pe, t, p):
            n = t * PAIRS + p
            pe.wait_ge(q_ready, n + 1)
            pe.wait_ge(relu_act, n)
            pe.wait_ge(relu_dve, n)
            for g0, g1 in GROUPS:
                for j in range(g0, g1):
                    for e in range(2):
                        last = pe.matmul(p_s[e][:, j // 4, j % 4 * R:(j % 4 + 1) * R],
                                         QK[e * C:(e + 1) * C, M // 2 + p, j * R:(j + 1) * R],
                                         q[p % 2][e * C:(e + 1) * C, :], start=True, stop=True)
                        if j == T - 1:
                            last.then_inc(s_done, 1)

        def values(pe, t, p):
            n = t * PAIRS + p
            for e in range(2):
                pe.wait_ge((relu_act, relu_dve)[e], n + 1)
                if p == 0 and e == 0:
                    pe.wait_ge(o_out, t)
                h = 2 * p + e
                for j in range(T):
                    last = pe.matmul(p_o[:, h * C:(h + 1) * C], at[p % 2][e][:, j, :], V[:, j, h * C:(h + 1) * C],
                                     start=j == 0, stop=j == T - 1)
                last.then_inc(pv_done, 1)

        def tail_pe_T(pe, t):
            pe.wait_ge(on_ready, t + 1)
            pe.wait_ge(y_out, t)
            for k in range(KC):
                last = pe.transpose(p_y[:, k * R:(k + 1) * R], on[:, k * 128:(k + 1) * 128], ident[0:R, 0:R])
            last.then_inc(oT_done, 1)

        def tail_pe_M(pe, t):
            pe.wait_ge(oT_out, KC * (t + 1))
            for k in range(KC):
                last = pe.matmul(p_y[0:R, :], oT[:, k, :], WO[:, k, :], start=k == 0, stop=k == KC - 1)
            last.then_inc(y_done, 1)

        @block.tensor
        def _(pe):
            pe.wait_ge(loaded, 64)
            scores(pe, 0, 0)
            for p in range(1, PAIRS):
                scores(pe, 0, p)
                values(pe, 0, p - 1)
            with pe.Fori(1, T) as t:
                scores(pe, t, 0)
                values(pe, t - 1, PAIRS - 1)
                scores(pe, t, 1)
                values(pe, t, 0)
                tail_pe_T(pe, t - 1)
                scores(pe, t, 2)
                tail_pe_M(pe, t - 1)
                values(pe, t, 1)
                scores(pe, t, 3)
                values(pe, t, 2)
            values(pe, T - 1, PAIRS - 1)
            tail_pe_T(pe, T - 1)
            tail_pe_M(pe, T - 1)


def constants(nc, s, ident, identb):
    zeros_ready, ident_ready = s.sems.new("zeros_ready"), s.sems.new("ident_ready")
    with nc.Block() as block:
        @block.gpsimd
        def _(pool):
            pool.memset(ident[:, :], 0.0).then_inc(zeros_ready, 1)
            pool.memset(identb[:, :], 0.0).then_inc(zeros_ready, 1)
            pool.wait_ge(zeros_ready, 2)
            for m in (ident, identb):
                pool.affine_select(out=m[:, :], in_=m[:, :], compare_op=ALU.not_equal, fill=1.0, base=0,
                                   pattern=[[-1, 128]], channel_multiplier=1).then_inc(ident_ready, 1)
            pool.wait_ge(ident_ready, 2)


def count_edges(nc, s, src, dst, CT, ident, identb, mask_dram):
    T, E, ET, N = s.T, s.E, s.ET, s.N
    G, DIG = 2, T // 2
    BASE = 16
    GOFF, TOFF = 4096, 2048
    NOWHERE = 20000.0
    NBUF = 4
    ROWS = 3
    RW = [min(128, ET - 128 * r) for r in range(ROWS)]
    PER = ET // T
    with ExitStack() as ctx:
        def sb(name, shape, dt=F32):
            return ctx.enter_context(nc.sbuf_tensor(name, shape, dt))

        def sem(name):
            return s.sems.new(name)

        raw = sb("edges_raw", [128, 2, ROWS, R], I32)
        rowf = sb("edges_f", [128, 2, ROWS, R])
        col = sb("edge_columns", [R, 2, ET])
        hi, lo, grp, dig = (sb(f"src_{n}", [R, ET]) for n in ("tile", "in_tile", "group", "digit"))
        keyp = sb("target_key", [R, ET + 2 * MARGIN])
        lop = sb("source_key", [R, ET + 2 * MARGIN])
        wt = sb("digit_weight", [R, ET + 2 * MARGIN])
        key3 = sb("general_key", [R, ET])
        keyw = [sb(f"key_window{n}", [R, WIN]) for n in range(3)]
        keyg = sb("general_window", [R, ET])
        iota32 = sb("iota32", [R, T * R], I32)
        iota_f = sb("iota_f", [R, T * R])
        iota_s, iota_d, iota_g = sb("iota_s", [R, R], I16), sb("iota_d", [R, G * R], I16), sb("iota_g", [R, T * R], I16)
        first = sb("block_first", [R, T])
        oh_s = [sb(f"onehot_s{i}", [R, R], BF16) for i in range(NBUF)]
        oh_d = [sb(f"onehot_d{i}", [R, G * R], BF16) for i in range(NBUF)]
        oh_g = [sb(f"onehot_g{i}", [R, T * R], BF16) for i in range(2)]
        zero = sb("zero_bf16", [R, BANK], BF16)
        packed = sb("packed", [R, G * R], I32)
        unpacked = sb("unpacked", [R, G, DIG, R], I32)
        found, top = sb("found", [R, T]), sb("top", [R, T])
        tally = sb("tally", [R, 2])
        onec = sb("ones_column", [R, 1])
        wrong = sb("wrong", [1, 4])
        wrong_i = sb("wrong_int", [1, 1], I32)
        cb = [sb(f"counts_bf16_{i}", [R, T, R], BF16) for i in range(2)]
        mk = [sb(f"mask_{i}", [R, N], BF16) for i in range(2)]

        loaded, iotas, colT, edges_float = sem("edges_loaded"), sem("iotas_ready"), sem("edges_transposed"), sem("edges_float")
        vec_chain, pool_chain = sem("count_vec_chain"), sem("count_pool_chain")
        onehot, used = sem("onehot_ready"), sem("onehot_used")
        packed_out, unpacked_ready, counts_out = (sem(n) for n in ("packed_out", "unpacked_ready", "counts_out"))
        tally_ready, tally_done, flag_ready = sem("tally_ready"), sem("tally_done"), sem("flag_ready")
        g_onehot, g_used, g_done, g_out = sem("g_onehot_ready"), sem("g_onehot_used"), sem("g_counted"), sem("g_out")
        loops_ready, cb_ready, ct_done, mask_ready = sem("loops_ready"), sem("cb_ready"), sem("ct_done"), sem("mask_ready")
        mask_stored = [sem(f"mask_stored{i}") for i in range(2)]

        with ExitStack() as one:
            p_col = [one.enter_context(nc.psum_tensor(f"p_edges{j}", [R, BANK], F32)) for j in range(2)]
            p_cnt = one.enter_context(nc.psum_tensor("p_counts", [R, BANK], F32))
            p_tal = one.enter_context(nc.psum_tensor("p_tally", [1, BANK], F32))
            block = one.enter_context(nc.Block())

            @block.sync
            def _(sp):
                for j, a in enumerate((src, dst)):
                    for r in range(ROWS):
                        sp.dma_start(raw[0:RW[r], j, r, :],
                                     a[128 * r * R:(128 * r + RW[r]) * R].rearrange("(k p) -> k p", p=R)).then_inc(loaded, 16)

            @block.gpsimd
            def _(pool):
                link = Chain(pool, pool_chain)
                link(pool.memset(zero[:, :], 0.0))
                link(pool.memset(onec[:, :], 1.0))
                for to, pattern in ((iota_s, [[1, R]]), (iota_d, [[GOFF, G], [1, R]]), (iota_g, [[TOFF, T], [1, R]])):
                    n = to.shape[1]
                    link(pool.iota(iota32[:, 0:n], pattern, base=0, channel_multiplier=0))
                    link(pool.tensor_copy(to[:, :], iota32[:, 0:n]))
                link(pool.iota(iota32[:, 0:T], [[R, T]], base=0, channel_multiplier=0))
                link(pool.tensor_copy(first[:, :], iota32[:, 0:T]))
                pool.sem_inc(iotas, 1)

            @block.tensor
            def _(pe):
                pe.wait_ge(edges_float, 1)
                for j in range(2):
                    for r in range(ROWS):
                        last = pe.transpose(p_col[j][:, 128 * r:128 * r + RW[r]], rowf[0:RW[r], j, r, :], ident[0:RW[r], 0:RW[r]])
                    last.then_inc(colT, 1)
                with pe.Fori(0, T) as b:
                    for k in range(WIN):
                        pe.wait_ge(onehot, b * WIN + k + 1)
                        if k == 0:
                            pe.wait_ge(packed_out, b)
                        pe.matmul(p_cnt[:, 0:G * R], oh_s[k % NBUF][:, :], oh_d[k % NBUF][:, :], start=k == 0, stop=k == WIN - 1)\
                          .then_inc(used, 1)
                pe.wait_ge(tally_ready, 1)
                pe.matmul(p_tal[:, 0:2], onec[:, :], tally[:, :], start=True, stop=True).then_inc(tally_done, 1)

            @block.vector
            def _(dve):
                link = Chain(dve, vec_chain)
                dve.wait_ge(loaded, 16 * 2 * ROWS)
                for r in range(ROWS):
                    link(dve.tensor_copy(rowf[0:RW[r], :, r, :], raw[0:RW[r], :, r, :]))
                dve.sem_inc(edges_float, 1)
                for j in range(2):
                    dve.wait_ge(colT, j + 1)
                    link(dve.tensor_copy(col[:, j, :], p_col[j][:, 0:ET]))
                dve.wait_ge(iotas, 1)
                S, D_ = col[:, 0, :], col[:, 1, :]
                link(dve.memset(hi[:, :], 0.0))
                for j in range(1, T):
                    link(dve.scalar_tensor_tensor(hi[:, :], S, float(j * R), hi[:, :], ALU.is_ge, ALU.add))
                link(dve.scalar_tensor_tensor(lo[:, :], hi[:, :], -float(R), S, ALU.mult, ALU.add))
                link(dve.tensor_scalar(grp[:, :], hi[:, :], float(DIG), None, ALU.is_ge))
                link(dve.scalar_tensor_tensor(dig[:, :], grp[:, :], -float(DIG), hi[:, :], ALU.mult, ALU.add))
                for pad, value in ((keyp, NOWHERE), (lop, 0.0), (wt, 1.0)):
                    link(dve.memset(pad[:, :], value))
                mid = slice(MARGIN, MARGIN + ET)
                link(dve.scalar_tensor_tensor(keyp[:, mid], grp[:, :], float(GOFF), D_, ALU.mult, ALU.add))
                link(dve.tensor_copy(lop[:, mid], lo[:, :]))
                for j in range(1, DIG):
                    link(dve.tensor_scalar(grp[:, :], dig[:, :], float(j), float(BASE ** j - BASE ** (j - 1)), ALU.is_ge, ALU.mult))
                    link(dve.tensor_tensor(wt[:, mid], wt[:, mid], grp[:, :], ALU.add))
                link(dve.scalar_tensor_tensor(key3[:, :], hi[:, :], float(TOFF), D_, ALU.mult, ALU.add))
                SETUP = link.n
                with dve.Fori(0, T) as b:
                    link.at(SETUP + 3 * b)
                    dve.wait_ge(used, b * WIN)
                    link(dve.tensor_scalar(keyw[0][:, :], keyp[:, ds(b * PER, WIN)], first[:, ds(b, 1)], None, ALU.subtract))
                    link(dve.tensor_copy(keyw[1][:, :], lop[:, ds(b * PER, WIN)]))
                    link(dve.tensor_copy(keyw[2][:, :], wt[:, ds(b * PER, WIN)]))
                    for k in range(WIN):
                        if k >= NBUF:
                            dve.wait_ge(used, b * WIN + k + 1 - NBUF)
                        dve.tensor_scalar(oh_s[k % NBUF][:, :], iota_s[:, :], keyw[1][:, k:k + 1], None, ALU.is_equal)
                        dve.tensor_scalar(oh_d[k % NBUF][:, :], iota_d[:, :], keyw[0][:, k:k + 1], keyw[2][:, k:k + 1],
                                          ALU.is_equal, ALU.mult).then_inc(onehot, 1)
                    dve.wait_ge(used, (b + 1) * WIN)
                    dve.wait_ge(counts_out, b)
                    dve.tensor_reduce(top[:, ds(b, 1)], p_cnt[:, 0:G * R], AX, ALU.max)
                    dve.tensor_copy(packed[:, :], p_cnt[:, 0:G * R]).then_inc(packed_out, 1)
                    dve.wait_ge(packed_out, b + 1)
                    pk = packed[:, :].rearrange("p (g c) -> p g c", g=G)
                    for j in range(DIG):
                        ins = dve.tensor_scalar(unpacked[:, :, j, :], pk, 4 * j, BASE - 1 if j < DIG - 1 else 0xffff,
                                                ALU.arith_shift_right, ALU.bitwise_and)
                    ins.then_inc(unpacked_ready, 1)
                dve.wait_ge(counts_out, T)
                link.at(SETUP + 3 * T)
                link(dve.tensor_scalar(top[:, :], top[:, :], float(BASE ** DIG), None, ALU.is_ge))
                link(dve.reduce_sum(tally[:, 0:1], found[:, :], AX))
                link(dve.reduce_sum(tally[:, 1:2], top[:, :], AX))
                dve.sem_inc(tally_ready, 1)
                dve.wait_ge(tally_done, 1)
                link(dve.tensor_scalar(wrong[:, 0:1], p_tal[:, 0:1], float(E), None, ALU.not_equal))
                link(dve.tensor_tensor(wrong[:, 1:2], wrong[:, 0:1], p_tal[:, 1:2], ALU.add))
                link(dve.tensor_scalar(wrong[:, 2:3], wrong[:, 1:2], 0.5, None, ALU.is_ge))
                link(dve.tensor_copy(wrong_i[:, :], wrong[:, 2:3]))
                dve.sem_inc(flag_ready, 1)

            @block.scalar
            def _(act):
                with act.Fori(0, T) as b:
                    act.wait_ge(unpacked_ready, b + 1)
                    act.activation(CT[:, :, ds(b * R, R)], unpacked[:, :, :, :].rearrange("p g j c -> p (g j) c"), ACT.Copy,
                                   accum_out=found[:, ds(b, 1)]).then_inc(counts_out, 1)

        general_count(nc, s, CT, zero, key3, keyg, lo, first, iota_s, iota_g, oh_s, oh_g, wrong_i,
                      g_onehot, g_used, g_done, g_out, vec_chain)

        with ExitStack() as two:
            PB = 1024
            RS = R + 1
            p_t = [two.enter_context(nc.psum_tensor(f"p_mask{i}", [R, 2, PB], BF16)) for i in range(2)]
            block = two.enter_context(nc.Block())

            @block.vector
            def _(dve):
                for t in range(T):
                    ins = dve.tensor_tensor(CT[:, t, t * R:(t + 1) * R], CT[:, t, t * R:(t + 1) * R], ident[0:R, 0:R], ALU.add)
                    ins.then_inc(loops_ready, 1)
                dve.wait_ge(loops_ready, T)
                with dve.Fori(0, T // 2) as u:
                    for i in range(2):
                        b = 2 * u + i
                        dve.wait_ge(ct_done, b)
                        dve.tensor_scalar(cb[i][:, :, :], CT[:, :, ds(b * R, R)], 1.0, None, ALU.min).then_inc(cb_ready, 1)
                        dve.wait_ge(ct_done, b + 1)
                        dve.wait_ge(mask_stored[i], 16 * u)
                        for h, (t0, t1) in enumerate(((0, 8), (8, T))):
                            ins = dve.tensor_scalar(mk[i][:, t0 * R:t1 * R].rearrange("p (t r) -> p t r", r=R),
                                                    p_t[i][:, h, 0:(t1 - t0) * RS].rearrange("p (t r) -> p t r", r=RS)[:, :, 0:R], 1.0, BIG,
                                                    ALU.subtract, ALU.mult)
                        ins.then_inc(mask_ready, 1)

            @block.tensor
            def _(pe):
                with pe.Fori(0, T // 2) as u:
                    for i in range(2):
                        b = 2 * u + i
                        pe.wait_ge(cb_ready, b + 1)
                        pe.wait_ge(mask_ready, b)
                        for t in range(T):
                            last = pe.transpose(p_t[i][:, t // 8, t % 8 * RS:t % 8 * RS + R], cb[i][:, t, :], identb[0:R, 0:R])
                        last.then_inc(ct_done, 1)

            @block.sync
            def _(sp):
                with sp.Fori(0, T // 2) as u:
                    for i in range(2):
                        b = 2 * u + i
                        sp.wait_ge(mask_ready, b + 1)
                        sp.dma_start(mask_dram[ds(b * R, R), :], mk[i][:, :]).then_inc(mask_stored[i], 16)
                for i in range(2):
                    sp.wait_ge(mask_stored[i], 16 * (T // 2))


def general_count(nc, s, CT, zero, key3, keyg, lo, first, iota_s, iota_g, oh_s, oh_g, wrong_i,
                  g_onehot, g_used, g_done, g_out, vec_chain):
    T, ET = s.T, s.ET
    COLS = [(k * 4 * R, min(4 * R, (T - 4 * k) * R)) for k in range(3)]
    with ExitStack() as ctx:
        p = [ctx.enter_context(nc.psum_tensor(f"p_general{k}", [R, BANK], F32)) for k in range(3)]
        g_key = s.sems.new("g_key_ready")
        g_block = s.sems.new("g_block_begun")
        block = ctx.enter_context(nc.Block())

        def bracket(pe, start):
            for k, (c, w) in enumerate(COLS):
                last = pe.matmul(p[k][:, 0:w], zero[:, 0:R], zero[:, 0:w], start=start, stop=not start)
            return last

        @block.tensor
        def _(pe):
            flag = pe.value_load(wrong_i[0:1, 0:1], min_val=0, max_val=1)
            with pe.If(flag > 0):
                with pe.Fori(0, T) as b:
                    pe.wait_ge(g_out, b)
                    bracket(pe, True)
                    with pe.Fori(0, ET // 2) as v:
                        for i in range(2):
                            n = b * ET + v * 2 + i
                            pe.wait_ge(g_onehot, n + 1)
                            for k, (c, w) in enumerate(COLS):
                                last = pe.matmul(p[k][:, 0:w], oh_s[i][:, :], oh_g[i][:, c:c + w], start=False, stop=False)
                            last.then_inc(g_used, 1)
                    bracket(pe, False).then_inc(g_done, 1)

        @block.vector
        def _(dve):
            flag = dve.value_load(wrong_i[0:1, 0:1], min_val=0, max_val=1)
            with dve.If(flag > 0):
                with dve.Fori(0, T) as b:
                    dve.wait_ge(g_used, b * ET)
                    dve.tensor_scalar(keyg[:, :], key3[:, :], first[:, ds(b, 1)], None, ALU.subtract).then_inc(g_key, 1)
                    dve.wait_ge(g_key, b + 1)
                    dve.sem_inc(g_block, 1)
                    with dve.Fori(0, ET // 2) as v:
                        for i in range(2):
                            n = b * ET + v * 2 + i
                            dve.wait_ge(g_used, b * ET + v * 2)
                            dve.tensor_scalar(oh_s[i][:, :], iota_s[:, :], lo[:, ds(v * 2 + i, 1)], None, ALU.is_equal)
                            dve.tensor_scalar(oh_g[i][:, :], iota_g[:, :], keyg[:, ds(v * 2 + i, 1)], None, ALU.is_equal)\
                               .then_inc(g_onehot, 1)
                    dve.wait_ge(g_done, b + 1)
                    for k, (c, w) in enumerate(COLS):
                        ins = dve.tensor_copy(CT[:, 4 * k:4 * k + w // R, ds(b * R, R)],
                                              p[k][:, 0:w].rearrange("p (t r) -> p t r", r=R))
                    ins.then_inc(g_out, 1)


def gat(nc, s, layer, C, haug, adcol, bias, rows_dram, mask_dram, CT, ident, spare, tail):
    T, N, H = s.T, s.N, s.H
    PAIRS = H // 2
    W = C + 1
    with ExitStack() as ctx:
        def sb(name, shape, dt=F32):
            return ctx.enter_context(nc.sbuf_tensor(f"{name}_{layer}", shape, dt))

        def sem(name):
            return s.sems.new(f"{name}_{layer}")

        a_src = sb("a_src", [R, H, N])
        mask = sb("mask_tile", [R, N], BF16)
        y = [sb(f"scores{i}", [R, N]) for i in range(4)]
        rl = [sb(f"relu{i}", [R, N]) for i in range(2)]
        pT = [sb(f"weights_T{i}", [R, T, R]) for i in range(2)]
        peak = [sb(f"peak{i}", [R, 2]) for i in range(2)]
        nz, nm = sb("neg_peak", [R, 2]), sb("neg_shift", [R, 2])
        shift = [sb(f"shift{i}", [R, 2, 2]) for i in range(2)]
        total, inv = sb("total", [R, 2]), sb("inv_total", [R, 2])
        bias_rows = spare[0:R, 0:H * C]
        res = spare[0:R, H * C:2 * H * C]
        p_t = [ctx.enter_context(nc.psum_tensor(f"p_weights_T{i}_{layer}", [128, 3, BANK], F32)) for i in range(2)]
        p_o = [ctx.enter_context(nc.psum_tensor(f"p_sums{i}_{layer}", [R, BANK], F32)) for i in range(2)]

        src_loaded = [sem(f"a_src_loaded{h}") for h in range(H)]
        bias_loaded, mask_loaded = sem("bias_loaded"), sem("mask_loaded")
        mask_used, shift_ready, relu_ready, logits_ready, weights_ready = (sem(n) for n in (
            "mask_used", "shift_ready", "relu_ready", "logits_ready", "weights_ready"))
        T_done, pT_ready, sum_done, res_ready = (sem(n) for n in ("T_done", "pT_ready", "sum_done", "res_ready"))
        vec_chain, turns = sem("gat_vec_chain"), sem("score_turns")
        tail = tail(nc, s, ctx, layer, sb, sem, res, p_t, spare, y)
        tail.res_ready = res_ready
        block = ctx.enter_context(nc.Block())

        @block.sync
        def _(sp):
            def load_mask(t):
                sp.dma_start(mask[:, :], mask_dram[ds(t * R, R), :]).then_inc(mask_loaded, 16)

            load_mask(0)
            for h in range(H):
                sp.dma_start(a_src[:, h, :], rows_dram[h:h + 1, :].to_broadcast([R, N])).then_inc(src_loaded[h], 16)
            sp.dma_start(bias_rows, bias[None, :].to_broadcast([R, H * C])).then_inc(bias_loaded, 16)
            tail.load(sp)
            with sp.Fori(1, T) as t:
                sp.wait_ge(mask_used, t)
                load_mask(t)
                tail.load_tile(sp, t)
            tail.store(sp)

        @block.vector
        def _(dve):
            link = Chain(dve, vec_chain)
            PER_PAIR = 6

            def pair_scores(t, p, first):
                if p == 0:
                    dve.wait_ge(mask_loaded, 16 * (t + 1))
                for e in range(2):
                    h = 2 * p + e
                    if first:
                        dve.wait_ge(src_loaded[h], 16)
                    if not (first and h < 4):
                        dve.wait_ge(T_done, t * H + h - 3)
                    dve.sem_inc(turns, 1)
                    ins = dve.tensor_tensor_reduce(out=y[h % 4][:, :], in0=a_src[:, h, :], in1=mask[:, :], scale=SLOPE,
                                                   scalar=-3.0e38, op0=ALU.add, op1=ALU.max,
                                                   accum_out=peak[p % 2][:, e:e + 1])
                link(ins)
                if p == PAIRS - 1:
                    dve.sem_inc(mask_used, 1)
                ad = adcol[:, ds(t, 1), H + 2 * p:H + 2 * p + 2].rearrange("p a h -> p (a h)")
                link(dve.scalar_tensor_tensor(nz[:, :], peak[p % 2][:, :], -1.0 / SLOPE, ad, ALU.mult, ALU.subtract))
                link(dve.scalar_tensor_tensor(nm[:, :], nz[:, :], SLOPE, nz[:, :], ALU.mult, ALU.min))
                dve.tensor_scalar(shift[p % 2][:, 0, :], ad, 1.0 - SLOPE, None, ALU.mult)
                link(dve.scalar_tensor_tensor(shift[p % 2][:, 1, :], ad, SLOPE, nm[:, :], ALU.mult, ALU.add))
                dve.sem_inc(shift_ready, 1)

            def pair_result(t, p):
                dve.wait_ge(sum_done, t * H + 2 * p + 2)
                if p == 0:
                    tail.wait_res_free(dve, t)
                sums = p_o[p % 2][:, 0:2 * W].rearrange("p (e w) -> p e w", e=2)
                link(dve.tensor_scalar(total[:, :], sums[:, :, C], 1e-16, None, ALU.add))
                link(dve.reciprocal(inv[:, :], total[:, :]))
                for e in range(2):
                    h = 2 * p + e
                    dve.scalar_tensor_tensor(res[:, h * C:(h + 1) * C], sums[:, e, 0:C], inv[:, e:e + 1],
                                             bias_rows[:, h * C:(h + 1) * C], ALU.mult, ALU.add).then_inc(res_ready, 1)
                if p == PAIRS - 1:
                    tail.vector(dve, t)

            def times_counts(t, h, first):
                Q = t * H + h
                dve.wait_ge(T_done, Q + 1)
                if not (first and h < 2):
                    dve.wait_ge(sum_done, Q - 1)
                for b0, b1 in ((0, 2), (2, 3)):
                    j0, j1 = 4 * b0, min(4 * b1, T)
                    ins = dve.tensor_tensor(
                        pT[h % 2][:, j0:j1, :].rearrange("p (b j) r -> p b j r", b=b1 - b0),
                        p_t[h % 2][0:R, b0:b1, 0:(j1 - j0) // (b1 - b0) * R].rearrange("p b (j r) -> p b j r", r=R),
                        CT[:, j0:j1, ds(t * R, R)].rearrange("p (b j) r -> p b j r", b=b1 - b0), ALU.mult)
                ins.then_inc(pT_ready, 1)

            def tile(t, first=False, last=False):
                for p in range(PAIRS):
                    if p < PAIRS - 1:
                        pair_scores(t, p + 1, first)
                    elif not last:
                        pair_scores(t + 1, 0, False)
                    if p > 0:
                        pair_result(t, p - 1)
                    elif not first:
                        pair_result(t - 1, PAIRS - 1)
                    times_counts(t, 2 * p, first)
                    times_counts(t, 2 * p + 1, first)

            dve.wait_ge(bias_loaded, 16)
            pair_scores(0, 0, True)
            tile(0, first=True)
            start = link.n
            with dve.Fori(1, T - 1) as t:
                link.at(start + (t - 1) * PER_PAIR * PAIRS)
                tile(t)
                assert link.n == PER_PAIR * PAIRS
            link.at(start + (T - 2) * PER_PAIR * PAIRS)
            tile(T - 1, last=True)
            pair_result(T - 1, PAIRS - 1)
            tail.vector_end(dve)

        @block.scalar
        def _(act):
            def relu(t, h, first):
                act.wait_ge(shift_ready, t * PAIRS + h // 2 + 1)
                if not (first and h < 2):
                    act.wait_ge(logits_ready, t * H + h - 1)
                act.activation(rl[h % 2][:, :], y[h % 4][:, :], ACT.Relu, bias=shift[h // 2 % 2][:, 0, h % 2:h % 2 + 1],
                               scale=(1.0 - SLOPE) / SLOPE).then_inc(relu_ready, 1)

            def exp(t, h):
                act.wait_ge(logits_ready, t * H + h + 1)
                act.activation(y[h % 4][:, :], y[h % 4][:, :], ACT.Exp, bias=shift[h // 2 % 2][:, 1, h % 2:h % 2 + 1])\
                   .then_inc(weights_ready, 1)

            def tile(t, first=False, last=False):
                for h in range(H):
                    if h < H - 1:
                        relu(t, h + 1, first)
                    elif not last:
                        relu(t + 1, 0, False)
                    exp(t, h)
                    if h == 2 and not first:
                        tail.scalar_first(act, t - 1)
                    if h == 3 and not first:
                        tail.scalar_second(act, t - 1)

            relu(0, 0, True)
            tile(0, first=True)
            with act.Fori(1, T - 1) as t:
                tile(t)
            tile(T - 1, last=True)
            tail.scalar_first(act, T - 1)
            tail.scalar_second(act, T - 1)
            tail.scalar_end(act)

        @block.gpsimd
        def _(pool):
            with pool.Fori(0, T) as t:
                for h in range(H):
                    pool.wait_ge(relu_ready, t * H + h + 1)
                    pool.tensor_tensor(y[h % 4][:, :], y[h % 4][:, :], rl[h % 2][:, :], ALU.add).then_inc(logits_ready, 1)

        @block.tensor
        def _(pe):
            def turn(t, h, first):
                Q = t * H + h
                pe.wait_ge(weights_ready, Q + 1)
                if not (first and h < 2):
                    pe.wait_ge(pT_ready, Q - 1)
                if h in (2, 3) and not first:
                    tail.wait_p_t_free(pe, t, h)
                for j in range(T):
                    last = pe.transpose(p_t[h % 2][0:R, j // 4, j % 4 * R:(j % 4 + 1) * R], y[h % 4][:, j * R:(j + 1) * R],
                                        ident[0:R, 0:R])
                last.then_inc(T_done, 1)

            def add_up(t, h):
                Q = t * H + h
                pe.wait_ge(pT_ready, Q + 1)
                if h % 2 == 0:
                    if not (isinstance(t, int) and Q < 4):
                        pe.wait_ge(res_ready, Q - 2)
                for j in range(T):
                    last = pe.matmul(p_o[h // 2 % 2][:, h % 2 * W:(h % 2 + 1) * W], pT[h % 2][:, j, :], haug[:, j, h, :],
                                     start=j == 0, stop=j == T - 1)
                last.then_inc(sum_done, 1)

            def tile(t, first=False):
                turn(t, 0, first)
                if not first:
                    add_up(t - 1, H - 1)
                turn(t, 1, first)
                add_up(t, 0)
                if not first:
                    tail.tensor_first(pe, t - 1)
                if not first:
                    add_up(t, 1)
                    tail.tensor_second(pe, t - 1)
                for h in range(2, H):
                    turn(t, h, first)
                    if h > 2 or first:
                        add_up(t, h - 1)

            tile(0, first=True)
            with pe.Fori(1, T) as t:
                tile(t)
            add_up(T - 1, H - 1)
            tail.tensor_first(pe, T - 1)
            tail.tensor_second(pe, T - 1)
            tail.tensor_end(pe)


class ToLayerTwo:

    def __init__(self, w2, w2att, haug2, adcol2, rows_dram, ident):
        self.w2_dram, self.w2att, self.haug2, self.adcol2, self.rows_dram, self.ident = (
            w2, w2att, haug2, adcol2, rows_dram, ident)

    def __call__(self, nc, s, ctx, layer, sb, sem, res, p_t, spare, y):
        self.s, self.res, self.p_t, self.y = s, res, p_t, y
        self.K = s.HC // 128
        self.D2 = s.H * s.C2
        self.w2 = sb("w2", [128, self.K, self.D2])
        n = self.K * R
        self.hT = spare[:, 2 * s.HC:2 * s.HC + n].rearrange("p (k r) -> p k r", k=self.K)
        (self.loaded, self.hT_done, self.hT_out, self.h2_done, self.h2_out, self.ones_ready, self.rows_done,
         self.rows_out, self.stored) = (sem(n) for n in (
            "w2_loaded", "hT_done", "hT_out", "h2_done", "h2_out", "h2_ones_ready", "rows_done", "rows_out", "rows_stored"))
        return self

    def load(self, sp):
        sp.dma_start(self.w2[:, :, :], self.w2_dram.rearrange("(k p) n -> p k n", p=128)).then_inc(self.loaded, 16)

    def load_tile(self, sp, t):
        pass

    def store(self, sp):
        sp.wait_ge(self.rows_out, 1)
        sp.dma_start(self.rows_dram, self.y[0][0:self.s.H, :]).then_inc(self.stored, 16)
        sp.wait_ge(self.stored, 16)

    def wait_res_free(self, dve, t):
        dve.wait_ge(self.hT_done, t)

    def vector(self, dve, t):
        pass

    def vector_end(self, dve):
        s = self.s
        dve.memset(self.haug2[:, :, :, s.C2:s.C2 + 1], 1.0)
        dve.wait_ge(self.rows_done, 1)
        for b in range(3):
            j0, j1 = 4 * b, min(4 * b + 4, s.T)
            ins = dve.tensor_copy(self.y[0][0:2 * s.H, j0 * R:j1 * R], self.p_t[0][0:2 * s.H, b, 0:(j1 - j0) * R])
        ins.then_inc(self.rows_out, 1)

    def scalar_first(self, act, t):
        act.wait_ge(self.hT_done, t + 1)
        act.wait_ge(self.h2_done, t)
        act.activation(self.hT.rearrange("p (b k) r -> p b (k r)", b=2), self.p_t[0][:, 0:2, 0:4 * R], ACT.Relu)\
           .then_inc(self.hT_out, 1)

    def scalar_second(self, act, t):
        s = self.s
        act.wait_ge(self.h2_done, t + 1)
        act.activation(self.haug2[:, ds(t, 1), :, 0:s.C2].rearrange("p a h c -> p (a h) c"),
                       self.p_t[1][0:R, 0, 0:self.D2].rearrange("p (h c) -> p h c", h=s.H), ACT.Copy)
        act.activation(self.adcol2[:, ds(t, 1), :].rearrange("p a h -> p (a h)"), self.p_t[1][0:R, 1, 0:2 * s.H], ACT.Copy)\
           .then_inc(self.h2_out, 1)

    def scalar_end(self, act):
        pass

    def wait_p_t_free(self, pe, t, h):
        pe.wait_ge(self.hT_out if h == 2 else self.h2_out, t)

    def tensor_first(self, pe, t):
        s = self.s
        pe.wait_ge(self.res_ready, s.H * (t + 1))
        for k in range(self.K):
            last = pe.transpose(self.p_t[0][:, k // 4, k % 4 * R:(k % 4 + 1) * R], self.res[:, k * 128:(k + 1) * 128],
                                self.ident[0:R, 0:R])
        last.then_inc(self.hT_done, 1)

    def tensor_second(self, pe, t):
        pe.wait_ge(self.loaded, 16)
        pe.wait_ge(self.hT_out, t + 1)
        for k in range(self.K):
            pe.matmul(self.p_t[1][0:R, 0, 0:self.D2], self.hT[:, k, :], self.w2[:, k, :], start=k == 0, stop=k == self.K - 1)
        for k in range(self.K):
            last = pe.matmul(self.p_t[1][0:R, 1, 0:2 * self.s.H], self.hT[:, k, :], self.w2att[:, k, :],
                             start=k == 0, stop=k == self.K - 1)
        last.then_inc(self.h2_done, 1)

    def tensor_end(self, pe):
        s = self.s
        pe.wait_ge(self.h2_out, s.T)
        for t in range(s.T):
            last = pe.transpose(self.p_t[0][0:2 * s.H, t // 4, t % 4 * R:(t % 4 + 1) * R], self.adcol2[:, t, :],
                                self.ident[0:R, 0:R])
        last.then_inc(self.rows_done, 1)


class ToResidual:

    def __init__(self, mix_dram, x1):
        self.mix_dram, self.x1 = mix_dram, x1

    def __call__(self, nc, s, ctx, layer, sb, sem, res, p_t, spare, y):
        self.s, self.res = s, res
        self.mix = sb("x_plus_mix", [R, s.D])
        self.junk = sb("log_softmax_exps", [R, s.D])
        self.neg_peak, self.sums, self.logs = (sb(f"log_softmax_{n}", [R, s.T]) for n in ("neg_peak", "sums", "logs"))
        self.mix_loaded, self.peaks_ready, self.exps_done, self.x1_ready, self.logs_ready, self.x1_done = (sem(n) for n in (
            "mix_loaded", "ls_peak_ready", "ls_exps_done", "x1_ready", "ls_logs_ready", "x1_done"))
        return self

    def load(self, sp):
        sp.dma_start(self.mix[:, :], self.mix_dram[0:R, :]).then_inc(self.mix_loaded, 16)

    def load_tile(self, sp, t):
        sp.wait_ge(self.x1_ready, t)
        sp.dma_start(self.mix[:, :], self.mix_dram[ds(t * R, R), :]).then_inc(self.mix_loaded, 16)

    def store(self, sp):
        pass

    def wait_res_free(self, dve, t):
        dve.wait_ge(self.exps_done, t)

    def vector(self, dve, t):
        dve.wait_ge(self.res_ready, self.s.H * (t + 1))
        dve.tensor_reduce(self.neg_peak[:, ds(t, 1)], self.res, AX, ALU.max, negate=True).then_inc(self.peaks_ready, 1)
        dve.wait_ge(self.mix_loaded, 16 * (t + 1))
        dve.wait_ge(self.peaks_ready, t + 1)
        dve.scalar_tensor_tensor(self.x1[:, ds(t, 1), :].rearrange("p a n -> p (a n)"), self.res,
                                 self.neg_peak[:, ds(t, 1)], self.mix[:, :], ALU.add, ALU.add).then_inc(self.x1_ready, 1)

    def vector_end(self, dve):
        s = self.s
        dve.wait_ge(self.x1_ready, s.T)
        dve.wait_ge(self.logs_ready, 1)
        for t in range(s.T):
            dve.tensor_scalar(self.x1[:, t, :], self.x1[:, t, :], self.logs[:, t:t + 1], None, ALU.subtract)\
               .then_inc(self.x1_done, 1)
        dve.wait_ge(self.x1_done, s.T)

    def scalar_first(self, act, t):
        act.wait_ge(self.peaks_ready, t + 1)
        act.activation(self.junk[:, :], self.res, ACT.Exp, bias=self.neg_peak[:, ds(t, 1)],
                       accum_out=self.sums[:, ds(t, 1)]).then_inc(self.exps_done, 1)

    def scalar_second(self, act, t):
        pass

    def scalar_end(self, act):
        act.wait_ge(self.exps_done, self.s.T)
        act.activation(self.logs[:, :], self.sums[:, :], ACT.Ln).then_inc(self.logs_ready, 1)

    def wait_p_t_free(self, pe, t, h):
        pass

    def tensor_first(self, pe, t):
        pass

    def tensor_second(self, pe, t):
        pass

    def tensor_end(self, pe):
        pass


def expert_ffn(nc, s, x1, router_w, w1, b1, w2, b2, ident, out):
    T, D, KC, N, NE, F = s.T, s.D, s.KC, s.N, s.NE, s.F
    KF = F // 128
    CB = [(k * BANK, min(N - k * BANK, BANK)) for k in range(3)]
    with ExitStack() as ctx:
        def sb(name, shape, dt=F32):
            return ctx.enter_context(nc.sbuf_tensor(f"ffn_{name}", shape, dt))

        def ps(name, shape, dt=F32):
            return ctx.enter_context(nc.psum_tensor(f"p_ffn_{name}", shape, dt))

        def sem(name):
            return s.sems.new(f"ffn_{name}")

        r_raw, w1_raw, w2_raw = sb("router", [NE, D]), sb("w1", [128, KF, D]), sb("w2", [128, KC, F])
        rT, w1T, w2T = sb("router_T", [128, KC, NE]), sb("w1_T", [128, KC, F]), sb("w2_T", [128, KF, D])
        b1c, b2b = sb("b1", [128, KF]), sb("b2", [R, D])
        xn = [sb(f"xn{i}", [R, D]) for i in range(2)]
        xT = [sb(f"xT{i}", [128, KC, R]) for i in range(2)]
        xT_all, hT = sb("xT_all", [128, KC, N]), sb("hT", [128, KF, N])
        stat, mv = sb("stat", [R, T, 6]), sb("mean_var", [R, T, 2])
        ve, std, rstd, scratch = (sb(n, [R, T]) for n in ("var_eps", "std", "rstd", "scratch"))
        logits, probs, sel, kept = (sb(n, [R, T, NE]) for n in ("logits", "probs", "chosen", "kept"))
        one = sb("one_chosen", [R, T, NE])
        selb = sb("chosen_bf16", [R, T, NE], BF16)
        peak, total, inv, gate = (sb(n, [R, T]) for n in ("peak", "total", "inv_total", "gate"))
        best = sb("best", [R, T, 8])
        best_i = sb("best_index", [R, T, 8], U32)
        best_f = sb("best_index_f", [R, T, 2])
        iota_i, iota_e = sb("iota_i", [R, NE], I32), sb("iota_e", [R, NE])
        upper, onesb = sb("earlier", [R, R], BF16), sb("ones_bf16", [R, R], BF16)
        yb = sb("y_plus_b2", [R, D])
        fin = [sb(f"result{i}", [R, D]) for i in range(2)]
        p_w = [ps(f"weights{i}", [128, BANK]) for i in range(2)]
        p_x, p_l = ps("xT", [128, BANK]), ps("logits", [R, BANK])
        p_h = [ps(f"h{i}", [128, BANK]) for i in range(2)]
        p_y = [ps(f"y{i}", [R, BANK]) for i in range(2)]

        (loaded, wT_done, wT_out, var_ready, std_ready, xn_ready, xT_done, xT_out, xT_kept, logits_done, logits_out,
         shifted, exps, consts, chosen, pos_done, h_done, h_out, y_done, y_out, fin_ready, chain, pool_chain) = (sem(n) for n in (
            "loaded", "wT_done", "wT_out", "var_ready", "std_ready", "xn_ready", "xT_done", "xT_out", "xT_kept",
            "logits_done", "logits_out", "logits_shifted", "exps_ready", "constants_ready", "chosen_ready", "positions_done",
            "h_done", "h_out", "y_done", "y_out", "result_ready", "vec_chain", "pool_chain"))
        stored = [sem(f"stored{i}") for i in range(2)]
        TURNS = ([[(rT[:, k, :], r_raw[:, k * 128:(k + 1) * 128], NE) for k in range(KC)]]
                 + [[(w1T[:, k, f * 128:(f + 1) * 128], w1_raw[:, f, k * 128:(k + 1) * 128], 128) for k in range(KC)]
                    for f in range(KF)]
                 + [[(w2T[:, f, k * 128:(k + 1) * 128], w2_raw[:, k, f * 128:(f + 1) * 128], 128) for k in range(KC)]
                    for f in range(KF)])
        block = ctx.enter_context(nc.Block())

        @block.sync
        def _(sp):
            sp.dma_start(r_raw[:, :], router_w).then_inc(loaded, 16)
            sp.dma_start(w1_raw[:, :, :], w1.rearrange("(f p) n -> p f n", p=128)).then_inc(loaded, 16)
            sp.dma_start(w2_raw[:, :, :], w2.rearrange("(k p) n -> p k n", p=128)).then_inc(loaded, 16)
            with nc.allow_non_contiguous_dma(reason="one short vector, once"):
                sp.dma_start(b1c[:, :], b1.rearrange("(f p) -> p f", p=128)).then_inc(loaded, 16)
            sp.dma_start(b2b[:, :], b2[None, :].to_broadcast([R, D])).then_inc(loaded, 16)
            for t in range(T):
                sp.wait_ge(fin_ready, t + 1)
                sp.dma_start(out[t * R:(t + 1) * R, :], fin[t % 2][:, :]).then_inc(stored[t % 2], 16)
            for i in range(2):
                sp.wait_ge(stored[i], 16 * (T // 2))

        @block.gpsimd
        def _(pool):
            link = Chain(pool, pool_chain)
            link(pool.iota(iota_i[:, :], [[1, NE]], base=0, channel_multiplier=0))
            link(pool.tensor_copy(iota_e[:, :], iota_i[:, :]))
            link(pool.memset(onesb[:, :], 1.0))
            link(pool.affine_select(out=upper[:, :], in_=onesb[:, :], compare_op=ALU.is_gt, fill=0.0, base=0,
                                    pattern=[[1, R]], channel_multiplier=-1))
            pool.sem_inc(consts, 1)

        @block.tensor
        def _(pe):
            pe.wait_ge(loaded, 16 * 5)
            for n, turn in enumerate(TURNS):
                if n >= 2:
                    pe.wait_ge(wT_out, n - 1)
                for k, (_, src, w) in enumerate(turn):
                    K = src.shape[0]
                    last = pe.transpose(p_w[n % 2][:, k * w:k * w + K], src, ident[0:K, 0:K])
                last.then_inc(wT_done, 1)
            pe.wait_ge(wT_out, len(TURNS))
            with pe.Fori(0, T // 2) as u:
                for i in range(2):
                    t = 2 * u + i
                    pe.wait_ge(xn_ready, t + 1)
                    pe.wait_ge(xT_out, t)
                    for k in range(KC):
                        last = pe.transpose(p_x[:, k * R:(k + 1) * R], xn[i][:, k * 128:(k + 1) * 128], ident[0:R, 0:R])
                    last.then_inc(xT_done, 1)
                    pe.wait_ge(xT_out, t + 1)
                    pe.wait_ge(logits_out, t)
                    for k in range(KC):
                        last = pe.matmul(p_l[:, 0:NE], xT[i][:, k, :], rT[:, k, :], start=k == 0, stop=k == KC - 1)
                    last.then_inc(logits_done, 1)
            pe.wait_ge(xT_kept, T)
            n = 0
            for c0, w in CB:
                for f in range(KF):
                    if n >= 2:
                        pe.wait_ge(h_out, n - 1)
                    for k in range(KC):
                        last = pe.matmul(p_h[n % 2][:, 0:w], w1T[:, k, f * 128:(f + 1) * 128], xT_all[:, k, c0:c0 + w],
                                         start=k == 0, stop=k == KC - 1)
                    last.then_inc(h_done, 1)
                    n += 1
            pe.wait_ge(consts, 1)
            pe.wait_ge(chosen, 1)
            for t in range(T):
                to = p_w[t // 8][0:R, t % 8 * NE:(t % 8 + 1) * NE]
                for e in range(t + 1):
                    last = pe.matmul(to, (onesb if e < t else upper)[:, :], selb[:, e, :], start=e == 0, stop=e == t)
            last.then_inc(pos_done, 1)
            pe.wait_ge(h_out, n)
            for t in range(T):
                if t >= 2:
                    pe.wait_ge(y_out, t - 1)
                for f in range(KF):
                    last = pe.matmul(p_y[t % 2][:, :], hT[:, f, t * R:(t + 1) * R], w2T[:, f, :], start=f == 0, stop=f == KF - 1)
                last.then_inc(y_done, 1)

        @block.scalar
        def _(act):
            act.wait_ge(var_ready, 1)
            act.activation(std[:, :], ve[:, :], ACT.Sqrt).then_inc(std_ready, 1)
            with act.Fori(0, T // 2) as u:
                for i in range(2):
                    t = 2 * u + i
                    act.wait_ge(xT_done, t + 1)
                    act.wait_ge(xT_kept, t)
                    act.wait_ge(logits_done, t)
                    act.activation(xT[i][:, :, :].rearrange("p k r -> p (k r)"), p_x[:, 0:KC * R], ACT.Copy).then_inc(xT_out, 1)
                    act.wait_ge(logits_done, t + 1)
                    act.activation(logits[:, ds(t, 1), :].rearrange("p a n -> p (a n)"), p_l[:, 0:NE], ACT.Copy)\
                       .then_inc(logits_out, 1)
            act.wait_ge(shifted, 1)
            act.activation(probs[:, :, :], logits[:, :, :], ACT.Exp).then_inc(exps, 1)
            n = 0
            for c0, w in CB:
                for f in range(KF):
                    act.wait_ge(h_done, n + 1)
                    act.activation(hT[:, f, c0:c0 + w], p_h[n % 2][:, 0:w], ACT.Gelu, bias=b1c[:, f:f + 1]).then_inc(h_out, 1)
                    n += 1

        @block.vector
        def _(dve):
            link = Chain(dve, chain)
            for t in range(T):
                ins = dve.bn_stats(stat[:, t, :], x1[:, t, :])
            link(ins)
            for t in range(T):
                ins = dve.bn_aggr(mv[:, t, :], stat[:, t, :])
            link(ins)
            dve.tensor_scalar(ve[:, :], mv[:, :, 1], LN_EPS, None, ALU.add).then_inc(var_ready, 1)
            dve.wait_ge(var_ready, 1)
            for n, turn in enumerate(TURNS):
                dve.wait_ge(wT_done, n + 1)
                for k, (to, src, w) in enumerate(turn):
                    ins = dve.tensor_copy(to, p_w[n % 2][:, k * w:k * w + src.shape[0]])
                ins.then_inc(wT_out, 1)
            one_over_sqrt(dve, link, std[:, :], ve[:, :], rstd[:, :], std_ready, 1, scratch[:, :])
            with dve.Fori(0, T // 2) as u:
                for i in range(2):
                    t = 2 * u + i
                    dve.wait_ge(xT_done, t)
                    dve.tensor_scalar(xn[i][:, :], x1[:, ds(t, 1), :].rearrange("p a n -> p (a n)"), mv[:, ds(t, 1), 0],
                                      rstd[:, ds(t, 1)], ALU.subtract, ALU.mult).then_inc(xn_ready, 1)
                    dve.wait_ge(xT_out, t + 1)
                    dve.tensor_copy(xT_all[:, :, ds(t * R, R)], xT[i][:, :, :]).then_inc(xT_kept, 1)
            dve.wait_ge(logits_out, T)
            link(dve.tensor_reduce(peak[:, :], logits[:, :, :], AX, ALU.max))
            link(dve.tensor_tensor(logits[:, :, :], logits[:, :, :], peak[:, :, None].to_broadcast([R, T, NE]), ALU.subtract))
            dve.sem_inc(shifted, 1)
            dve.wait_ge(exps, 1)
            link(dve.tensor_reduce(total[:, :], probs[:, :, :], AX, ALU.add))
            link(dve.reciprocal(inv[:, :], total[:, :]))
            link(dve.tensor_tensor(probs[:, :, :], probs[:, :, :], inv[:, :, None].to_broadcast([R, T, NE]), ALU.mult))
            for t in range(T):
                ins = dve.max(best[:, t, :], probs[:, t, :])
            link(ins)
            for t in range(T):
                ins = dve.max_index(best_i[:, t, :], best[:, t, :], probs[:, t, :])
            link(ins)
            link(dve.tensor_copy(best_f[:, :, :], best_i[:, :, 0:2]))
            dve.wait_ge(consts, 1)
            which = iota_e[:, None, :].to_broadcast([R, T, NE])
            dve.tensor_tensor(sel[:, :, :], which, best_f[:, :, 0:1].to_broadcast([R, T, NE]), ALU.is_equal)
            link(dve.tensor_tensor(one[:, :, :], which, best_f[:, :, 1:2].to_broadcast([R, T, NE]), ALU.is_equal))
            link(dve.tensor_tensor(sel[:, :, :], sel[:, :, :], one[:, :, :], ALU.add))
            link(dve.tensor_copy(selb[:, :, :], sel[:, :, :]))
            dve.sem_inc(chosen, 1)
            link(dve.tensor_tensor(probs[:, :, :], probs[:, :, :], sel[:, :, :], ALU.mult))
            dve.wait_ge(pos_done, 1)
            for b, (t0, t1) in enumerate(((0, 8), (8, T))):
                ins = dve.tensor_scalar(kept[:, t0:t1, :].rearrange("p t n -> p (t n)"), p_w[b][0:R, 0:(t1 - t0) * NE], float(CAP), None,
                                        ALU.is_lt)
            link(ins)
            link(dve.tensor_tensor(kept[:, :, :], kept[:, :, :], probs[:, :, :], ALU.mult))
            link(dve.tensor_reduce(gate[:, :], kept[:, :, :], AX, ALU.add))
            for t in range(T):
                dve.wait_ge(y_done, t + 1)
                if t >= 1:
                    dve.wait_ge(fin_ready, t)
                dve.tensor_tensor(yb[:, :], p_y[t % 2][:, :], b2b[:, :], ALU.add).then_inc(y_out, 1)
                dve.wait_ge(y_out, t + 1)
                if t >= 2:
                    dve.wait_ge(stored[t % 2], 16 * (t // 2))
                dve.scalar_tensor_tensor(fin[t % 2][:, :], yb[:, :], gate[:, t:t + 1], x1[:, t, :], ALU.mult, ALU.add)\
                   .then_inc(fin_ready, 1)


def gps_layer(nc, a, out):
    s = Shapes(nc, a["x"], a["src"], a["L0_gnn_W1"], a["L0_gnn_att_src1"], a["L0_gnn_att_src2"], a["L0_mix_w_out"],
               a["L0_ffn_router_w"], a["L0_ffn_w1"])
    N, D, T, H = s.N, s.D, s.T, s.H

    def scratch(name, shape, dt=F32):
        return nc.dram_tensor(name, shape, dt, kind="Internal").ap()

    rows1, rows2 = scratch("a_src1_rows", [H, N]), scratch("a_src2_rows", [H, N])
    mask, mix = scratch("mask", [N, N], BF16), scratch("x_plus_mix", [N, D])
    with ExitStack() as ctx:
        def sb(name, shape, dt=F32):
            return ctx.enter_context(nc.sbuf_tensor(name, shape, dt))

        ident, identb = sb("ident", [128, 128]), sb("ident_bf16", [128, 128], BF16)
        adcol1, adcol2 = sb("att1_columns", [R, T, 2 * H]), sb("att2_columns", [R, T, 2 * H])
        w2att = sb("w2_att", [128, s.HC // 128, 2 * H])
        h1 = sb("h1", [R, T, H, s.C1 + 1])
        RA = sb("weights_then_counts", [128, s.KC * (s.HC + 3 * D)])
        CT = RA[0:R, 0:T * N // 2].bitcast(U16).rearrange("p (t n) -> p t n", t=T)
        spare = RA[:, T * N // 2:s.KC * (s.HC + 3 * D)]
        constants(nc, s, ident, identb)
        with nc.sbuf_tensor("qkv", [128, 8 * N + T * D], F32) as RB:
            project(nc, s, a["x"], a["L0_gnn_W1"], a["L0_mix_w_qkv"], a["L0_gnn_att_src1"], a["L0_gnn_att_dst1"],
                    RA, RB, h1, ident, adcol1, rows1)
            count_edges(nc, s, a["src"], a["dst"], CT, ident, identb, mask)
            relu_attention(nc, s, a["x"], a["L0_mix_ln_gamma"], a["L0_mix_ln_beta"], a["L0_mix_w_out"], a["L0_mix_b_out"],
                           a["L0_gnn_W2"], a["L0_gnn_att_src2"], a["L0_gnn_att_dst2"], w2att, RB, ident, mix)
        s.sems.start_over()
        haug2 = sb("h2", [R, T, H, s.C2 + 1])
        gat(nc, s, 1, s.C1, h1, adcol1, a["L0_gnn_b1"], rows1, mask, CT, ident, spare,
            ToLayerTwo(a["L0_gnn_W2"], w2att, haug2, adcol2, rows2, ident))
        x1 = h1[:, :, :, :].rearrange("p t h c -> p (t h c)")[:, 0:T * D].rearrange("p (t n) -> p t n", t=T)
        gat(nc, s, 2, s.C2, haug2, adcol2, a["L0_gnn_b2"], rows2, mask, CT, ident, spare, ToResidual(mix, x1))
        expert_ffn(nc, s, x1, a["L0_ffn_router_w"], a["L0_ffn_w1"], a["L0_ffn_b1"], a["L0_ffn_w2"], a["L0_ffn_b2"], ident, out)


_INS = ["x", "src", "dst", "L0_gnn_W1", "L0_gnn_att_src1", "L0_gnn_att_dst1", "L0_gnn_b1", "L0_gnn_W2",
        "L0_gnn_att_src2", "L0_gnn_att_dst2", "L0_gnn_b2", "L0_mix_w_qkv", "L0_mix_ln_gamma", "L0_mix_ln_beta",
        "L0_mix_w_out", "L0_mix_b_out", "L0_ffn_router_w", "L0_ffn_w1", "L0_ffn_b1", "L0_ffn_w2", "L0_ffn_b2"]


def kernel(**inputs):
    import numpy as _np
    import concourse.bacc as _bacc
    from concourse.bass_utils import run_bass_kernel_spmd as _run

    nc = _bacc.Bacc("TRN2", target_bir_lowering=False, num_devices=1)
    arrays, args = {}, {}
    for name in _INS:
        a = _np.ascontiguousarray(inputs[name])
        arrays[f"in_{name}"] = a
        args[name] = nc.dram_tensor(f"in_{name}", a.shape, mybir.dt.from_np(a.dtype), kind="ExternalInput").ap()
    out = nc.dram_tensor("out_0", inputs["x"].shape, F32, kind="ExternalOutput").ap()
    gps_layer(nc, args, out)
    return _run(nc, [arrays], core_ids=[0]).results[0]["out_0"]
```

```python
from contextlib import ExitStack

import concourse.bass as bass
from concourse import mybir

F32 = mybir.dt.float32
BF16 = mybir.dt.bfloat16
I32 = mybir.dt.int32
I16 = mybir.dt.int16
U16 = mybir.dt.uint16
U32 = mybir.dt.uint32
ALU = mybir.AluOpType
ACT = mybir.ActivationFunctionType
AX = mybir.AxisListType.X

R = 125
BANK = 512
BIG = 1.0e30
LN_EPS = 1e-5
SLOPE = 0.2
WIN = 40
MARGIN = 4
CAP = 512


def ds(i, n):
    return bass.ds(i, n)


class Semaphores:

    def __init__(self, nc):
        self.nc, self.held = nc, []

    def new(self, name):
        self.held.append(self.nc.alloc_semaphore(name))
        return self.held[-1]

    def begin_at(self, value, *sems):
        for sem in sems:
            self.nc.gpsimd.sem_inc(sem, value)

    def start_over(self):
        self.nc.clear_and_free_semaphores(self.held)
        self.nc.all_engine_barrier()
        self.held = []


class Shapes:
    def __init__(self, nc, x, src, w1, att, att2, w_out, router, ffn_w1):
        self.sems = Semaphores(nc)
        self.N, self.D = x.shape
        self.T = self.N // R
        self.E = src.shape[0]
        self.ET = self.E // R
        self.H, self.C1 = att.shape
        self.C2 = att2.shape[1]
        self.HC = w1.shape[1]
        self.KC = self.D // 128
        self.NE = router.shape[0]
        self.F = ffn_w1.shape[0]
        assert self.N == self.T * R and self.E == self.ET * R and self.ET % self.T == 0
        assert self.ET // self.T + 2 * MARGIN == WIN


class Chain:

    def __init__(self, engine, sem, base=0):
        self.engine, self.sem, self.base, self.n = engine, sem, base, 0

    def at(self, base):
        self.base, self.n = base, 0

    def __call__(self, instruction):
        self.n += 1
        instruction.then_inc(self.sem, 1)
        self.engine.wait_ge(self.sem, self.base + self.n)


def one_over_sqrt(dve, link, std, ve, out, std_ready, value, scratch):
    dve.wait_ge(std_ready, value)
    link(dve.reciprocal(out, std))
    link(dve.tensor_tensor(scratch, out, out, ALU.mult))
    link(dve.tensor_tensor(scratch, scratch, ve, ALU.mult))
    link(dve.tensor_scalar(scratch, scratch, -0.5, 1.5, ALU.mult, ALU.add))
    link(dve.tensor_tensor(out, out, scratch, ALU.mult))


def project(nc, s, x, w1, wqkv, att_src1, att_dst1, w2, att_src2, att_dst2, RA, RB, ident, adcol, w2att, h1_dram, rows_dram):
    T, KC, H, D, C1, HC, N = s.T, s.KC, s.H, s.D, s.C1, s.HC, s.N
    W1 = RA[:, 0:KC * HC].rearrange("p (k n) -> p k n", k=KC)
    WQKV = RA[:, KC * HC:KC * (HC + 3 * D)].rearrange("p (k n) -> p k n", k=KC)
    M = 2 * D // 128
    QK = RB[:, 0:M * N].rearrange("p (m n) -> p m n", m=M)
    V = RB[0:R, M * N:M * N + T * D].rearrange("p (t n) -> p t n", t=T)
    with ExitStack() as ctx:
        def sb(name, shape, dt=F32):
            return ctx.enter_context(nc.sbuf_tensor(name, shape, dt))

        def ps(name, shape, dt=F32):
            return ctx.enter_context(nc.psum_tensor(name, shape, dt))

        def sem(name):
            return s.sems.new(name)

        xs = [sb(f"x_in{i}", [R, D]) for i in range(2)]
        xn = [sb(f"xn{i}", [R, D]) for i in range(2)]
        xT = [sb(f"xnT{i}", [128, KC, R]) for i in range(2)]
        xT_all = sb("xnT_all", [128, KC, N])
        attb = sb("att1_rows", [128, 2, HC])
        watt = sb("w1_att", [128, KC, 2 * H])
        prod = sb("w1_att_prod", [128, HC])
        h1 = [sb(f"h1_tile{i}", [R, HC]) for i in range(2)]
        K2, HC2 = HC // 128, H * s.C2
        W2, attb2 = sb("w2_for_att", [128, K2, HC2]), sb("att2_rows", [128, 2, HC2])
        stat = sb("ln_stat", [R, T, 6])
        mv = sb("ln_mean_var", [R, T, 2])
        ve, std, rstd, scratch = (sb(f"ln_{n}", [R, T]) for n in ("var_eps", "std", "rstd", "scratch"))
        rows = sb("att1_scores", [2 * H, N])
        p_xT = ps("p_xT", [128, BANK])
        p_h1 = ps("p_h1", [R, 2 * BANK])
        p_v = ps("p_v", [R, BANK])
        p_qk = ps("p_qk", [128, 2, BANK])
        NB = 3
        CB = [(k * BANK, min(N - k * BANK, BANK)) for k in range(NB)]

        x_loaded = [sem(f"x_loaded{i}") for i in range(2)]
        w_loaded, wq_loaded, att_loaded = sem("w1_loaded"), sem("wqkv_loaded"), sem("att1_loaded")
        x_used, std_ready, var_ready = sem("x_used"), sem("std_ready"), sem("var_ready")
        h1_stored = [sem(f"h1_stored{i}") for i in range(2)]
        w2_loaded = sem("w2_for_att_loaded")
        xT_done, xT_copied, xT_kept = sem("xT_done"), sem("xT_copied"), sem("xT_kept")
        qk_done, qk_out, h1_done, h1_out = sem("qk_done"), sem("qk_out"), sem("h1_done"), sem("h1_out")
        v_done, v_out = sem("v_done"), sem("v_out")
        watt_ready, row_done, row_out = sem("watt_ready"), sem("row_done"), sem("row_out")
        col_done, col_out, rows_stored = sem("col_done"), sem("col_out"), sem("rows_stored")
        vec_chain, pool_chain = sem("p1_vec_chain"), sem("p1_pool_chain")
        p_row = [p_h1[0:2 * H, 0:BANK], p_h1[0:2 * H, BANK:2 * BANK], p_v[0:2 * H, :]]
        p_col = p_xT[0:R, 0:T * 2 * H]
        s.sems.begin_at(1, xT_done, v_done, xT_kept, xT_copied, qk_out, h1_out, v_out)
        s.sems.begin_at(16, *h1_stored)
        block = ctx.enter_context(nc.Block())

        @block.sync
        def _(sp):
            for i in range(2):
                sp.dma_start(xs[i][:, :], x[i * R:(i + 1) * R, :]).then_inc(x_loaded[i], 16)
            with sp.Fori(1, T // 2) as u:
                for i in range(2):
                    sp.wait_ge(x_used, 2 * u - 1 + i)
                    sp.dma_start(xs[i][:, :], x[ds((2 * u + i) * R, R), :]).then_inc(x_loaded[i], 16)
            with sp.Fori(0, T // 2) as u:
                for i in range(2):
                    sp.wait_ge(x_used, T + 2 * u - 1 + i)
                    sp.dma_start(xs[i][:, :], x[ds((2 * u + i) * R, R), :]).then_inc(x_loaded[i], 16)
            sp.wait_ge(row_out, NB)
            sp.dma_start(rows_dram, rows[0:H, :]).then_inc(rows_stored, 16)
            sp.wait_ge(rows_stored, 16)

        @block.gpsimd
        def _(pool):
            link = Chain(pool, pool_chain)

            def through(w, rows, out, K, C):
                prods = prod[:, 0:H * C].rearrange("p (h c) -> p h c", h=H)
                for k in range(K):
                    for j in range(2):
                        link(pool.tensor_tensor(prod[:, 0:H * C], w[:, k, :], rows[:, j, :], ALU.mult))
                        c = C // 2
                        while c:
                            left, right = prods[:, :, 0:c], prods[:, :, c:2 * c]
                            to = left if c > 1 else out[:, k, j * H:(j + 1) * H].rearrange("p (h c) -> p h c", c=1)
                            link(pool.tensor_tensor(to, left, right, ALU.add))
                            c //= 2

            pool.wait_ge(w_loaded, 16)
            pool.wait_ge(att_loaded, 32)
            pool.dma_start(W2[:, :, :], w2.rearrange("(k p) n -> p k n", p=128)).then_inc(w2_loaded, 16)
            for j, a in enumerate((att_src2, att_dst2)):
                pool.dma_start(attb2[:, j, :], a.rearrange("h c -> (h c)")[None, :].to_broadcast([128, HC2]))\
                    .then_inc(w2_loaded, 16)
            through(W1, attb, watt, KC, C1)
            pool.sem_inc(watt_ready, 1)
            pool.wait_ge(w2_loaded, 48)
            through(W2, attb2, w2att, K2, s.C2)

        @block.vector
        def _(dve):
            link = Chain(dve, vec_chain)
            with dve.Fori(0, T // 2) as u:
                for i in range(2):
                    t = 2 * u + i
                    dve.wait_ge(x_loaded[i], 16 * (u + 1))
                    dve.bn_stats(stat[:, ds(t, 1), :].rearrange("p a b -> p (a b)"), xs[i][:, :]).then_inc(x_used, 1)
            dve.wait_ge(x_used, T)
            for t in range(T):
                ins = dve.bn_aggr(mv[:, t, :], stat[:, t, :])
            link(ins)
            dve.tensor_scalar(ve[:, :], mv[:, :, 1], LN_EPS, None, ALU.add).then_inc(var_ready, 1)
            dve.wait_ge(var_ready, 1)
            one_over_sqrt(dve, link, std[:, :], ve[:, :], rstd[:, :], std_ready, 1, scratch[:, :])
            with dve.Fori(0, T // 2) as u:
                for i in range(2):
                    t = 2 * u + i
                    dve.wait_ge(x_loaded[i], 16 * (u + 1 + T // 2))
                    dve.wait_ge(xT_done, t + 1)
                    dve.tensor_scalar(xn[i][:, :], xs[i][:, :], mv[:, ds(t, 1), 0], rstd[:, ds(t, 1)],
                                      ALU.subtract, ALU.mult).then_inc(x_used, 1)
                    dve.wait_ge(xT_copied, t + 1 + 1)
                    dve.tensor_copy(xT_all[:, :, ds(t * R, R)], xT[i][:, :, :])\
                       .then_inc(xT_kept, 1)
                    dve.wait_ge(qk_done, t + 1)
                    dve.tensor_copy(QK[:, :, ds(t * R, R)].rearrange("p (b m) r -> p b m r", b=2),
                                    p_qk[:, :, 0:4 * R].rearrange("p b (m r) -> p b m r", m=4)).then_inc(qk_out, 1)
            for k, (c0, w) in enumerate(CB):
                dve.wait_ge(row_done, k + 1)
                dve.tensor_copy(rows[:, c0:c0 + w], p_row[k][:, 0:w]).then_inc(row_out, 1)
            dve.wait_ge(col_done, 1)
            dve.tensor_copy(adcol[:, :, :], p_col.rearrange("p (t h) -> p t h", t=T)).then_inc(col_out, 1)
            dve.wait_ge(col_out, 1)

        @block.scalar
        def _(act):
            act.dma_start(WQKV, wqkv.rearrange("(k p) n -> p k n", p=128)).then_inc(wq_loaded, 16)
            act.dma_start(W1, w1.rearrange("(k p) n -> p k n", p=128)).then_inc(w_loaded, 16)
            for j, a in enumerate((att_src1, att_dst1)):
                act.dma_start(attb[:, j, :], a.rearrange("h c -> (h c)")[None, :].to_broadcast([128, HC]))\
                   .then_inc(att_loaded, 16)
            act.wait_ge(var_ready, 1)
            act.activation(std[:, :], ve[:, :], ACT.Sqrt).then_inc(std_ready, 1)
            with act.Fori(0, T // 2) as u:
                for i in range(2):
                    t = 2 * u + i
                    act.wait_ge(xT_done, t + 1 + 1)
                    act.wait_ge(v_done, t + 1)
                    act.wait_ge(xT_kept, t + 1)
                    act.activation(xT[i][:, :, :].rearrange("p k r -> p (k r)"), p_xT[:, 0:KC * R], ACT.Copy)\
                       .then_inc(xT_copied, 1)
                    act.wait_ge(h1_done, t + 1)
                    act.wait_ge(h1_stored[i], 16 * (u + 1))
                    act.activation(h1[i][:, :], p_h1[:, :], ACT.Copy).then_inc(h1_out, 1)
                    act.wait_ge(v_done, t + 1 + 1)
                    act.activation(V[:, ds(t, 1), :].rearrange("p a n -> p (a n)"), p_v[:, :], ACT.Copy)\
                       .then_inc(v_out, 1)
                    act.wait_ge(h1_out, t + 1 + 1)
                    act.dma_start(h1_dram[ds(t * R, R), :], h1[i][:, :]).then_inc(h1_stored[i], 16)
            for i in range(2):
                act.wait_ge(h1_stored[i], 16 * (T // 2 + 1))

        @block.tensor
        def _(pe):
            pe.wait_ge(wq_loaded, 16)
            pe.wait_ge(w_loaded, 16)
            with pe.Fori(0, T // 2) as u:
                for i in range(2):
                    t = 2 * u + i
                    pe.wait_ge(x_used, T + t + 1)
                    pe.wait_ge(xT_copied, t + 1)
                    for k in range(KC):
                        last = pe.transpose(p_xT[:, k * R:(k + 1) * R], xn[i][:, k * 128:(k + 1) * 128], ident[0:R, 0:R])
                    last.then_inc(xT_done, 1)
                    pe.wait_ge(xT_copied, t + 1 + 1)
                    pe.wait_ge(qk_out, t + 1)
                    for m in range(M):
                        for k in range(KC):
                            last = pe.matmul(p_qk[:, m // 4, m % 4 * R:(m % 4 + 1) * R], WQKV[:, k, m * 128:(m + 1) * 128],
                                             xT[i][:, k, :], start=k == 0, stop=k == KC - 1)
                    last.then_inc(qk_done, 1)
                    pe.wait_ge(h1_out, t + 1)
                    for n in range(HC // BANK):
                        for k in range(KC):
                            last = pe.matmul(p_h1[:, n * BANK:(n + 1) * BANK], xT[i][:, k, :],
                                             W1[:, k, n * BANK:(n + 1) * BANK], start=k == 0, stop=k == KC - 1)
                    last.then_inc(h1_done, 1)
                    pe.wait_ge(v_out, t + 1)
                    for k in range(KC):
                        last = pe.matmul(p_v[:, :], xT[i][:, k, :], WQKV[:, k, 2 * D:3 * D], start=k == 0, stop=k == KC - 1)
                    last.then_inc(v_done, 1)
            pe.wait_ge(watt_ready, 1)
            pe.wait_ge(xT_kept, T + 1)
            pe.wait_ge(h1_out, T + 1)
            pe.wait_ge(v_out, T + 1)
            for b, (c0, w) in enumerate(CB):
                for k in range(KC):
                    last = pe.matmul(p_row[b][:, 0:w], watt[:, k, :], xT_all[:, k, c0:c0 + w], start=k == 0, stop=k == KC - 1)
                last.then_inc(row_done, 1)
            pe.wait_ge(xT_copied, T + 1)
            pe.wait_ge(row_out, NB)
            for t in range(T):
                last = pe.transpose(p_col[:, t * 2 * H:(t + 1) * 2 * H], rows[:, t * R:(t + 1) * R], ident[0:2 * H, 0:2 * H])
            last.then_inc(col_done, 1)




def constants(nc, s, ident, identb):
    zeros_ready, ident_ready = s.sems.new("zeros_ready"), s.sems.new("ident_ready")
    with nc.Block() as block:
        @block.gpsimd
        def _(pool):
            pool.memset(ident[:, :], 0.0).then_inc(zeros_ready, 1)
            pool.memset(identb[:, :], 0.0).then_inc(zeros_ready, 1)
            pool.wait_ge(zeros_ready, 2)
            for m in (ident, identb):
                pool.affine_select(out=m[:, :], in_=m[:, :], compare_op=ALU.not_equal, fill=1.0, base=0,
                                   pattern=[[-1, 128]], channel_multiplier=1).then_inc(ident_ready, 1)
            pool.wait_ge(ident_ready, 2)


def guarded(engine, flag, program):
    if flag is None:
        program()
    else:
        value = engine.value_load(flag, min_val=0, max_val=1)
        with engine.If(value > 0):
            program()


class Counting:

    G, BASE = 2, 16
    GOFF, TOFF = 4096, 2048
    NOWHERE = 20000.0

    def __init__(self, s, ctx, nc):
        T, ET = s.T, s.ET
        self.DIG = T // 2

        def sb(name, shape, dt=F32):
            return ctx.enter_context(nc.sbuf_tensor(name, shape, dt))

        self.keyp, self.lop, self.wt = (sb(n, [R, ET + 2 * MARGIN]) for n in ("target_key", "source_key", "digit_weight"))
        self.key3 = sb("general_key", [R, ET])
        self.iota_s, self.iota_d = sb("iota_s", [R, R], I16), sb("iota_d", [R, self.G * R], I16)
        self.first = sb("block_first", [R, T])
        self.found, self.top = sb("found", [R, T]), sb("top", [R, T])
        self.wrong_i = sb("wrong_int", [1, 1], I32)


def prepare_edges(nc, s, cnt, src, dst, ident):
    T, ET = s.T, s.ET
    G, DIG, BASE = cnt.G, cnt.DIG, cnt.BASE
    ROWS = 3
    RW = [min(128, ET - 128 * r) for r in range(ROWS)]
    with ExitStack() as ctx:
        def sb(name, shape, dt=F32):
            return ctx.enter_context(nc.sbuf_tensor(name, shape, dt))

        sem = s.sems.new
        raw = sb("edges_raw", [128, 2, ROWS, R], I32)
        rowf = sb("edges_f", [128, 2, ROWS, R])
        col = sb("edge_columns", [R, 2, ET])
        hi, grp, dig = (sb(f"src_{n}", [R, ET]) for n in ("tile", "group", "digit"))
        iota32 = sb("iota32", [R, G * R], I32)
        loaded, iotas, colT, edges_float = sem("edges_loaded"), sem("iotas_ready"), sem("edges_transposed"), sem("edges_float")
        vec_chain, pool_chain = sem("edge_vec_chain"), sem("edge_pool_chain")
        p_col = [ctx.enter_context(nc.psum_tensor(f"p_edges{j}", [R, BANK], F32)) for j in range(2)]
        block = ctx.enter_context(nc.Block())

        @block.sync
        def _(sp):
            for j, a in enumerate((src, dst)):
                for r in range(ROWS):
                    sp.dma_start(raw[0:RW[r], j, r, :],
                                 a[128 * r * R:(128 * r + RW[r]) * R].rearrange("(k p) -> k p", p=R)).then_inc(loaded, 16)

        @block.gpsimd
        def _(pool):
            link = Chain(pool, pool_chain)
            for to, pattern in ((cnt.iota_s, [[1, R]]), (cnt.iota_d, [[cnt.GOFF, G], [1, R]]), (cnt.first, [[R, T]])):
                n = to.shape[1]
                link(pool.iota(iota32[:, 0:n], pattern, base=0, channel_multiplier=0))
                link(pool.tensor_copy(to[:, :], iota32[:, 0:n]))

        @block.tensor
        def _(pe):
            pe.wait_ge(edges_float, 1)
            for j in range(2):
                for r in range(ROWS):
                    last = pe.transpose(p_col[j][:, 128 * r:128 * r + RW[r]], rowf[0:RW[r], j, r, :], ident[0:RW[r], 0:RW[r]])
                last.then_inc(colT, 1)

        @block.vector
        def _(dve):
            link = Chain(dve, vec_chain)
            dve.wait_ge(loaded, 16 * 2 * ROWS)
            for r in range(ROWS):
                link(dve.tensor_copy(rowf[0:RW[r], :, r, :], raw[0:RW[r], :, r, :]))
            dve.sem_inc(edges_float, 1)
            for j in range(2):
                dve.wait_ge(colT, j + 1)
                link(dve.tensor_copy(col[:, j, :], p_col[j][:, 0:ET]))
            S, D_ = col[:, 0, :], col[:, 1, :]
            link(dve.memset(hi[:, :], 0.0))
            for j in range(1, T):
                link(dve.scalar_tensor_tensor(hi[:, :], S, float(j * R), hi[:, :], ALU.is_ge, ALU.add))
            for pad, value in ((cnt.keyp, cnt.NOWHERE), (cnt.lop, 0.0), (cnt.wt, 1.0)):
                link(dve.memset(pad[:, :], value))
            mid = slice(MARGIN, MARGIN + ET)
            link(dve.scalar_tensor_tensor(cnt.lop[:, mid], hi[:, :], -float(R), S, ALU.mult, ALU.add))
            link(dve.tensor_scalar(grp[:, :], hi[:, :], float(DIG), None, ALU.is_ge))
            link(dve.scalar_tensor_tensor(dig[:, :], grp[:, :], -float(DIG), hi[:, :], ALU.mult, ALU.add))
            link(dve.scalar_tensor_tensor(cnt.keyp[:, mid], grp[:, :], float(cnt.GOFF), D_, ALU.mult, ALU.add))
            for j in range(1, DIG):
                link(dve.tensor_scalar(grp[:, :], dig[:, :], float(j), float(BASE ** j - BASE ** (j - 1)), ALU.is_ge, ALU.mult))
                link(dve.tensor_tensor(cnt.wt[:, mid], cnt.wt[:, mid], grp[:, :], ALU.add))
            link(dve.scalar_tensor_tensor(cnt.key3[:, :], hi[:, :], float(cnt.TOFF), D_, ALU.mult, ALU.add))


def attend_and_count(nc, s, cnt, x, gamma, beta, w_out, b_out, RB, CT, spare, ident, identb, rows_dram, mask_dram,
                     mix_dram, peaks):
    T, KC, H, D, N, E = s.T, s.KC, s.H, s.D, s.N, s.E
    M = 2 * D // 128
    C = D // H
    QK = RB[:, 0:M * N].rearrange("p (m n) -> p m n", m=M)
    V = RB[0:R, M * N:M * N + T * D].rearrange("p (t n) -> p t n", t=T)
    PAIRS = H // 2
    SCALE = float(C) ** -0.5
    GROUPS = ((0, 4), (4, 8), (8, T))
    UNITS = 2 * len(GROUPS)
    SLOTS = 4
    G, DIG, BASE = cnt.G, cnt.DIG, cnt.BASE
    PER = s.ET // T
    STEP = WIN // PAIRS
    HALF = T // 2
    RS = R + 1
    OH = RS + G * R
    with ExitStack() as ctx:
        def sb(name, shape, dt=F32):
            return ctx.enter_context(nc.sbuf_tensor(name, shape, dt))

        def ps(name, shape, dt=F32):
            return ctx.enter_context(nc.psum_tensor(name, shape, dt))

        sem = s.sems.new
        a_src = sb("a_src_rows_1", [R, H, N])
        WO = sb("w_out_sb", [128, KC, D])
        gcol, bcol = sb("mix_gamma", [128, KC]), sb("mix_beta", [128, KC])
        q = [sb(f"q_tile{i}", [128, R]) for i in range(2)]
        at = [[sb(f"relu_scores{i}{e}", [R, T, R]) for e in range(2)] for i in range(2)]
        o, on, oT = sb("mix_heads", [R, D]), sb("mix_normed", [R, D]), sb("mix_normed_T", [128, KC, R])
        y, xt = sb("mix_out", [R, D]), sb("mix_x", [R, D])
        junk = spare[0:R, 0:N // 2].bitcast(BF16)
        boutb = spare[0:R, N // 2:N // 2 + D]
        at_spare = N // 2 + D
        packed = spare[0:R, at_spare:at_spare + G * R].bitcast(I32)
        unpacked = spare[0:R, at_spare + G * R:at_spare + G * R + G * DIG * R].bitcast(I32)\
            .rearrange("p (g j c) -> p g j c", g=G, j=DIG)
        stat, mv = sb("mix_stat", [R, 6]), sb("mix_mv", [R, 2])
        ve, std, rstd, scratch = (sb(f"mix_{n}", [R, 1]) for n in ("var_eps", "std", "rstd", "scratch"))
        keyw = [sb(f"key_window{n}", [R, WIN]) for n in range(3)]
        at_spare += G * R + G * DIG * R
        onehot = [spare[0:R, c:c + OH // 2].bitcast(BF16) for c in range(at_spare, spare.shape[1] - OH // 2 + 1, OH // 2)]
        onehot += [sb(f"onehots{i}", [R, OH], BF16)[:, :] for i in range(2 * STEP - len(onehot))]
        oh_s, oh_d = [to[:, 0:R] for to in onehot], [to[:, RS:OH] for to in onehot]
        cb, mk = sb("counts_bf16", [R, T, R], BF16), sb("mask_rows", [R, N], BF16)
        peak = sb("peak_of_tile", [R, H])
        p_s = [ps(f"p_scores{i}", [R, BANK]) for i in range(SLOTS)]
        p_o, p_y, p_cnt = ps("p_heads", [R, BANK]), ps("p_mix_out", [128, BANK]), ps("p_counts", [R, BANK])
        p_m = ps("p_mask", [R, 2 * BANK], BF16)

        (loaded, q_ready, s_done, relu_done, pv_done, o_out, mvar, mstd, on_ready, oT_done, oT_out, y_done, y_out,
         stored, vec_chain, x_loaded, y_added, turns) = (sem(f"mix_{n}") for n in (
            "loaded", "q_ready", "scores_done", "relu_done", "pv_done", "heads_out", "var_ready", "std_ready", "normed",
            "normed_T_done", "normed_T_out", "y_done", "y_out", "stored", "vec_chain", "x_loaded", "x_added", "turns"))
        src_loaded, windows, oh_ready, used = (sem(n) for n in (
            "a_src1_loaded", "windows_ready", "onehots_ready", "onehots_used"))
        unpacked_ready, counts_out, cb_ready, maskT, mask_half, mask_ready, mask_stored, scored, count_chain = (sem(n) for n in (
            "unpacked_ready", "counts_out", "counts_bf16_ready", "mask_T_done", "mask_half_out", "mask_ready", "mask_stored",
            "mask_scored", "count_chain"))
        s.sems.begin_at(1, y_added, y_out, used, mask_ready)
        s.sems.begin_at(16, stored, mask_stored)
        block = ctx.enter_context(nc.Block())

        @block.sync
        def _(sp):
            sp.dma_start(WO[:, :, :], w_out.rearrange("(k p) n -> p k n", p=128)).then_inc(loaded, 16)
            sp.dma_start(boutb, b_out[None, :].to_broadcast([R, D])).then_inc(loaded, 16)
            with nc.allow_non_contiguous_dma(reason="two vectors, once"):
                sp.dma_start(gcol[:, :], gamma.rearrange("(k p) -> p k", p=128)).then_inc(loaded, 16)
                sp.dma_start(bcol[:, :], beta.rearrange("(k p) -> p k", p=128)).then_inc(loaded, 16)
            for h in range(H):
                sp.dma_start(a_src[:, h, :], rows_dram[h:h + 1, :].to_broadcast([R, N])).then_inc(src_loaded, 16)
            with sp.Fori(0, T) as t:
                sp.wait_ge(y_added, t + 1)
                sp.dma_start(xt[:, :], x[ds(t * R, R), :]).then_inc(x_loaded, 16)
                sp.wait_ge(mask_ready, t + 2)
                sp.dma_start(mask_dram[ds(t * R, R), :], mk[:, :]).then_inc(mask_stored, 16)
                sp.wait_ge(y_added, t + 2)
                sp.dma_start(mix_dram[ds(t * R, R), :], y[:, :]).then_inc(stored, 16)
            sp.wait_ge(stored, 16 * (T + 1))
            sp.wait_ge(mask_stored, 16 * (T + 1))

        @block.gpsimd
        def _(pool):
            def steps(t, first):
                for p in range(PAIRS):
                    if not (first and p == 0):
                        pool.wait_ge(s_done, (t * PAIRS + p - 1) * UNITS)
                    pool.tensor_copy(q[p % 2][:, :], QK[:, p, ds(t * R, R)]).then_inc(q_ready, 1)

            steps(0, True)
            with pool.Fori(1, T) as t:
                steps(t, False)

        @block.scalar
        def _(act):
            act.wait_ge(loaded, 64)

            def root(t):
                act.wait_ge(mvar, t + 1)
                act.activation(std[:, :], ve[:, :], ACT.Sqrt).then_inc(mstd, 1)

            def scale_normed(t):
                act.wait_ge(oT_done, t + 1)
                for k in range(KC):
                    act.activation(oT[:, k, :], p_y[:, k * R:(k + 1) * R], ACT.Identity,
                                   bias=bcol[:, k:k + 1], scale=gcol[:, k:k + 1]).then_inc(oT_out, 1)

            def keep_counts(t):
                act.wait_ge(unpacked_ready, t + 1)
                act.activation(CT[:, :, ds(t * R, R)], unpacked.rearrange("p g j c -> p (g j) c"), ACT.Copy,
                               accum_out=cnt.found[:, ds(t, 1)]).then_inc(counts_out, 1)

            def steps(t, first):
                for p in range(PAIRS):
                    n = t * PAIRS + p
                    for b, (j0, j1) in enumerate(GROUPS):
                        for e in range(2):
                            u = 2 * b + e
                            act.wait_ge(s_done, n * UNITS + u + 1)
                            if b == 0 and not (first and p < 2):
                                act.wait_ge(pv_done, 2 * (n - 2) + e + 1)
                            act.activation(at[p % 2][e][:, j0:j1, :].rearrange("p j r -> p (j r)"),
                                           p_s[(p * UNITS + u) % SLOTS][:, 0:(j1 - j0) * R], ACT.Relu, scale=SCALE)\
                               .then_inc(relu_done, 1)
                    if p == 0 and not first:
                        keep_counts(t - 1)
                        root(t - 1)
                    if p == 1 and not first:
                        scale_normed(t - 1)

            steps(0, True)
            with act.Fori(1, T) as t:
                steps(t, False)
            keep_counts(T - 1)
            root(T - 1)
            scale_normed(T - 1)

        @block.vector
        def _(dve):
            mix, count = Chain(dve, vec_chain), Chain(dve, count_chain)
            NORM_LINKS, COUNT_LINKS = 9, 3 + H

            def norm_tail(t):
                mix.at(t * NORM_LINKS)
                dve.wait_ge(pv_done, (t + 1) * H)
                mix(dve.tensor_copy(o[:, :], p_o[:, :]))
                dve.sem_inc(o_out, 1)
                mix(dve.bn_stats(stat[:, :], o[:, :]))
                dve.sem_inc(turns, 1)
                mix(dve.bn_aggr(mv[:, :], stat[:, :]))
                mix(dve.tensor_scalar(ve[:, :], mv[:, 1:2], LN_EPS, None, ALU.add))
                dve.sem_inc(mvar, 1)
                one_over_sqrt(dve, mix, std[:, :], ve[:, :], rstd[:, :], mstd, t + 1, scratch[:, :])
                dve.tensor_scalar(on[:, :], o[:, :], mv[:, 0:1], rstd[:, 0:1], ALU.subtract, ALU.mult).then_inc(on_ready, 1)
                assert mix.n == NORM_LINKS

            def out_tail(t):
                dve.wait_ge(y_done, t + 1)
                dve.wait_ge(stored, 16 * (t + 1))
                dve.tensor_tensor(y[:, :], p_y[0:R, :], boutb, ALU.add).then_inc(y_out, 1)
                dve.wait_ge(x_loaded, 16 * (t + 1))
                dve.wait_ge(y_out, t + 2)
                dve.tensor_tensor(y[:, :], y[:, :], xt[:, :], ALU.add).then_inc(y_added, 1)

            def window(t, first=False):
                if not first:
                    dve.wait_ge(oh_ready, t * WIN)
                dve.tensor_scalar(keyw[0][:, :], cnt.keyp[:, ds(t * PER, WIN)], cnt.first[:, ds(t, 1)], None, ALU.subtract)
                dve.tensor_copy(keyw[1][:, :], cnt.lop[:, ds(t * PER, WIN)])
                dve.tensor_copy(keyw[2][:, :], cnt.wt[:, ds(t * PER, WIN)]).then_inc(windows, 1)
                dve.wait_ge(windows, t + 1)

            def onehots(t, p, first):
                for k in range(STEP):
                    i = p * STEP + k
                    b = i % (2 * STEP)
                    if not (first and p < 2):
                        dve.wait_ge(used, t * WIN + i + 1 - 2 * STEP + 1)
                    dve.tensor_scalar(oh_s[b], cnt.iota_s[:, :], keyw[1][:, i:i + 1], None, ALU.is_equal)
                    dve.tensor_scalar(oh_d[b], cnt.iota_d[:, :], keyw[0][:, i:i + 1], keyw[2][:, i:i + 1],
                                      ALU.is_equal, ALU.mult).then_inc(oh_ready, 1)

            def unpack(t):
                count.at(t * COUNT_LINKS)
                dve.wait_ge(used, (t + 1) * WIN + 1)
                dve.tensor_reduce(cnt.top[:, ds(t, 1)], p_cnt[:, 0:G * R], AX, ALU.max)
                count(dve.tensor_copy(packed, p_cnt[:, 0:G * R]))
                pk = packed.rearrange("p (g c) -> p g c", g=G)
                for j in range(DIG):
                    ins = dve.tensor_scalar(unpacked[:, :, j, :], pk, 4 * j, BASE - 1 if j < DIG - 1 else 0xffff,
                                            ALU.arith_shift_right, ALU.bitwise_and)
                ins.then_inc(unpacked_ready, 1)

            def self_loops(t):
                dve.wait_ge(counts_out, t + 1)
                own = CT[:, ds(t, 1), ds(t * R, R)].rearrange("p a r -> p (a r)")
                count(dve.tensor_tensor(own, own, ident[0:R, 0:R], ALU.add))
                dve.tensor_scalar(cb[:, :, :], CT[:, :, ds(t * R, R)], 1.0, None, ALU.min).then_inc(cb_ready, 1)

            def mask_part(t, half):
                dve.wait_ge(maskT, 2 * t + half + 1)
                if half == 0:
                    dve.wait_ge(mask_stored, 16 * (t + 1))
                ins = dve.tensor_scalar(mk[:, half * HALF * R:(half + 1) * HALF * R].rearrange("p (t r) -> p t r", r=R),
                                        p_m[:, 0:HALF * RS].rearrange("p (t r) -> p t r", r=RS)[:, :, 0:R], 1.0, BIG,
                                        ALU.subtract, ALU.mult)
                if half == 0:
                    ins.then_inc(mask_half, 1)
                else:
                    count(ins)
                    dve.sem_inc(mask_ready, 1)

            def see(t, h0, h1):
                for h in range(h0, h1):
                    dve.sem_inc(turns, 1)
                    count(dve.tensor_tensor_reduce(out=junk, in0=a_src[:, h, :], in1=mk[:, :], scale=1.0, scalar=-3.0e38,
                                                   op0=ALU.add, op1=ALU.max, accum_out=peak[:, h:h + 1]))
                if h1 == H:
                    dve.tensor_copy(peaks[:, ds(t, 1), :].rearrange("p a h -> p (a h)"), peak[:, :]).then_inc(scored, 1)

            def steps(t, first=False, last=False):
                if not first:
                    unpack(t - 1)
                onehots(t, 1, first)
                if not first:
                    norm_tail(t - 1)
                    self_loops(t - 1)
                onehots(t, 2, first)
                if not first:
                    mask_part(t - 1, 0)
                    mask_part(t - 1, 1)
                onehots(t, 3, first)
                if not first:
                    out_tail(t - 1)
                    see(t - 1, 0, H // 2)
                if not last:
                    window(t + 1)
                    onehots(t + 1, 0, False)
                if not first:
                    see(t - 1, H // 2, H)
                    assert count.n == COUNT_LINKS

            dve.wait_ge(loaded, 64)
            window(0, True)
            onehots(0, 0, True)
            steps(0, first=True)
            dve.wait_ge(src_loaded, 16 * H)
            with dve.Fori(1, T - 1) as t:
                steps(t)
            steps(T - 1, last=True)
            unpack(T - 1)
            norm_tail(T - 1)
            self_loops(T - 1)
            mask_part(T - 1, 0)
            mask_part(T - 1, 1)
            see(T - 1, 0, H)
            out_tail(T - 1)
            dve.wait_ge(scored, T)

        @block.tensor
        def _(pe):
            def scores(t, p, first):
                n = t * PAIRS + p
                pe.wait_ge(q_ready, n + 1)
                for b, (j0, j1) in enumerate(GROUPS):
                    if not (first and p * UNITS + 2 * b + 2 <= SLOTS):
                        pe.wait_ge(relu_done, n * UNITS + 2 * b + 2 - SLOTS)
                    for j in range(j0, j1):
                        for e in range(2):
                            last = pe.matmul(p_s[(p * UNITS + 2 * b + e) % SLOTS][:, (j - j0) * R:(j - j0 + 1) * R],
                                             QK[e * C:(e + 1) * C, M // 2 + p, j * R:(j + 1) * R],
                                             q[p % 2][e * C:(e + 1) * C, :], start=True, stop=True)
                            if j == j1 - 1:
                                last.then_inc(s_done, 1)

            def values(t, p):
                n = t * PAIRS + p
                pe.wait_ge(relu_done, (n + 1) * UNITS)
                if p == 0 and not (isinstance(t, int) and t == 0):
                    pe.wait_ge(o_out, t)
                for e in range(2):
                    h = 2 * p + e
                    for j in range(T):
                        last = pe.matmul(p_o[:, h * C:(h + 1) * C], at[p % 2][e][:, j, :], V[:, j, h * C:(h + 1) * C],
                                         start=j == 0, stop=j == T - 1)
                    last.then_inc(pv_done, 1)

            def counts(t, p):
                for k in range(STEP):
                    i = p * STEP + k
                    b = i % (2 * STEP)
                    pe.wait_ge(oh_ready, t * WIN + i + 1)
                    if p == 0 and k == 0 and not (isinstance(t, int) and t == 0):
                        pe.wait_ge(unpacked_ready, t)
                    pe.matmul(p_cnt[:, 0:G * R], oh_s[b], oh_d[b], start=p == 0 and k == 0,
                              stop=p == PAIRS - 1 and k == STEP - 1).then_inc(used, 1)

            def mask_T(t, half):
                pe.wait_ge(cb_ready, t + 1)
                if half == 0:
                    pe.wait_ge(mask_ready, t + 1)
                else:
                    pe.wait_ge(mask_half, t + 1)
                for j in range(HALF):
                    last = pe.transpose(p_m[:, j * RS:j * RS + R], cb[:, half * HALF + j, :], identb[0:R, 0:R])
                last.then_inc(maskT, 1)

            def normed_T(t):
                pe.wait_ge(on_ready, t + 1)
                pe.wait_ge(y_out, t + 1)
                for k in range(KC):
                    last = pe.transpose(p_y[:, k * R:(k + 1) * R], on[:, k * 128:(k + 1) * 128], ident[0:R, 0:R])
                last.then_inc(oT_done, 1)

            def out_product(t):
                pe.wait_ge(oT_out, KC * (t + 1))
                for k in range(KC):
                    last = pe.matmul(p_y[0:R, :], oT[:, k, :], WO[:, k, :], start=k == 0, stop=k == KC - 1)
                last.then_inc(y_done, 1)

            def steps(t, first):
                scores(t, 0, first)
                if not first:
                    values(t - 1, PAIRS - 1)
                counts(t, 0)
                scores(t, 1, first)
                counts(t, 1)
                values(t, 0)
                if not first:
                    mask_T(t - 1, 0)
                    normed_T(t - 1)
                scores(t, 2, first)
                if not first:
                    mask_T(t - 1, 1)
                    out_product(t - 1)
                counts(t, 2)
                values(t, 1)
                scores(t, 3, first)
                counts(t, 3)
                values(t, 2)

            pe.wait_ge(loaded, 64)
            steps(0, True)
            with pe.Fori(1, T) as t:
                steps(t, False)
            values(T - 1, PAIRS - 1)
            mask_T(T - 1, 0)
            normed_T(T - 1)
            mask_T(T - 1, 1)
            out_product(T - 1)


def verify_counts(nc, s, cnt):
    T, E = s.T, s.E
    with ExitStack() as ctx:
        def sb(name, shape, dt=F32):
            return ctx.enter_context(nc.sbuf_tensor(name, shape, dt))

        sem = s.sems.new
        tally, onec, wrong = sb("tally", [R, 2]), sb("ones_column", [R, 1]), sb("wrong", [1, 4])
        p_tal = ctx.enter_context(nc.psum_tensor("p_tally", [1, BANK], F32))
        tally_ready, tally_done, vec_chain = sem("tally_ready"), sem("tally_done"), sem("tally_chain")
        block = ctx.enter_context(nc.Block())

        @block.tensor
        def _(pe):
            pe.wait_ge(tally_ready, 1)
            pe.matmul(p_tal[:, 0:2], onec[:, :], tally[:, :], start=True, stop=True).then_inc(tally_done, 1)

        @block.vector
        def _(dve):
            link = Chain(dve, vec_chain)
            link(dve.memset(onec[:, :], 1.0))
            link(dve.tensor_scalar(cnt.top[:, :], cnt.top[:, :], float(cnt.BASE ** cnt.DIG), None, ALU.is_ge))
            link(dve.reduce_sum(tally[:, 0:1], cnt.found[:, :], AX))
            link(dve.reduce_sum(tally[:, 1:2], cnt.top[:, :], AX))
            dve.sem_inc(tally_ready, 1)
            dve.wait_ge(tally_done, 1)
            link(dve.tensor_scalar(wrong[:, 0:1], p_tal[:, 0:1], float(E), None, ALU.not_equal))
            link(dve.tensor_tensor(wrong[:, 1:2], wrong[:, 0:1], p_tal[:, 1:2], ALU.add))
            link(dve.tensor_scalar(wrong[:, 2:3], wrong[:, 1:2], 0.5, None, ALU.is_ge))
            link(dve.tensor_copy(cnt.wrong_i[:, :], wrong[:, 2:3]))


def general_path(nc, s, cnt, CT, ident, identb, rows_dram, mask_dram, peaks):
    T, ET, N = s.T, s.ET, s.N
    COLS = [(k * 4 * R, min(4 * R, (T - 4 * k) * R)) for k in range(3)]
    flag = cnt.wrong_i[0:1, 0:1]
    with ExitStack() as ctx:
        def sb(name, shape, dt=F32):
            return ctx.enter_context(nc.sbuf_tensor(name, shape, dt))

        sem = s.sems.new
        keyg = sb("general_window", [R, ET])
        oh_s = [sb(f"general_onehot_s{i}", [R, R], BF16) for i in range(2)]
        oh_g = [sb(f"general_onehot_d{i}", [R, T * R], BF16) for i in range(2)]
        iota32, iota_g = sb("iota32_general", [R, T * R], I32), sb("iota_general", [R, T * R], I16)
        zero = sb("zero_bf16", [R, BANK], BF16)
        onehot, used, done, out, key_ready, begun, iotas, pool_chain = (sem(f"general_{n}") for n in (
            "onehot_ready", "onehot_used", "counted", "out", "key_ready", "block_begun", "iota_ready", "pool_chain"))
        p = [ctx.enter_context(nc.psum_tensor(f"p_general{k}", [R, BANK], F32)) for k in range(3)]
        s.sems.begin_at(1, used, out)
        block = ctx.enter_context(nc.Block())

        def bracket(pe, start):
            for k, (c, w) in enumerate(COLS):
                last = pe.matmul(p[k][:, 0:w], zero[:, 0:R], zero[:, 0:w], start=start, stop=not start)
            return last

        @block.gpsimd
        def _(pool):
            def program():
                link = Chain(pool, pool_chain)
                link(pool.memset(zero[:, :], 0.0))
                link(pool.iota(iota32[:, :], [[cnt.TOFF, T], [1, R]], base=0, channel_multiplier=0))
                link(pool.tensor_copy(iota_g[:, :], iota32[:, :]))
                pool.sem_inc(iotas, 1)

            guarded(pool, flag, program)

        @block.tensor
        def _(pe):
            def program():
                pe.wait_ge(iotas, 1)
                with pe.Fori(0, T) as b:
                    pe.wait_ge(out, b + 1)
                    bracket(pe, True)
                    with pe.Fori(0, ET // 2) as v:
                        for i in range(2):
                            pe.wait_ge(onehot, b * ET + v * 2 + i + 1)
                            for k, (c, w) in enumerate(COLS):
                                last = pe.matmul(p[k][:, 0:w], oh_s[i][:, :], oh_g[i][:, c:c + w], start=False, stop=False)
                            last.then_inc(used, 1)
                    bracket(pe, False).then_inc(done, 1)

            guarded(pe, flag, program)

        @block.vector
        def _(dve):
            def program():
                dve.wait_ge(iotas, 1)
                with dve.Fori(0, T) as b:
                    dve.wait_ge(used, b * ET + 1)
                    dve.tensor_scalar(keyg[:, :], cnt.key3[:, :], cnt.first[:, ds(b, 1)], None, ALU.subtract).then_inc(key_ready, 1)
                    dve.wait_ge(key_ready, b + 1)
                    dve.sem_inc(begun, 1)
                    with dve.Fori(0, ET // 2) as v:
                        for i in range(2):
                            dve.wait_ge(used, b * ET + v * 2 + 1)
                            dve.tensor_scalar(oh_s[i][:, :], cnt.iota_s[:, :], cnt.lop[:, ds(v * 2 + i + MARGIN, 1)], None,
                                              ALU.is_equal)
                            dve.tensor_scalar(oh_g[i][:, :], iota_g[:, :], keyg[:, ds(v * 2 + i, 1)], None, ALU.is_equal)\
                               .then_inc(onehot, 1)
                    dve.wait_ge(done, b + 1)
                    for k, (c, w) in enumerate(COLS):
                        ins = dve.tensor_copy(CT[:, 4 * k:4 * k + w // R, ds(b * R, R)],
                                              p[k][:, 0:w].rearrange("p (t r) -> p t r", r=R))
                    ins.then_inc(out, 1)

            guarded(dve, flag, program)

    with ExitStack() as ctx:
        sem = s.sems.new
        PB = 1024
        RS = R + 1
        cb = [ctx.enter_context(nc.sbuf_tensor(f"general_counts_bf16_{i}", [R, T, R], BF16)) for i in range(2)]
        mk = [ctx.enter_context(nc.sbuf_tensor(f"general_mask_{i}", [R, N], BF16)) for i in range(2)]
        loops_ready, cb_ready, ct_done, mask_ready = (sem(f"general_{n}") for n in (
            "loops_ready", "cb_ready", "ct_done", "mask_ready"))
        mask_stored = [sem(f"general_mask_stored{i}") for i in range(2)]
        p_t = [ctx.enter_context(nc.psum_tensor(f"p_general_mask{i}", [R, 2, PB], BF16)) for i in range(2)]
        s.sems.begin_at(1, ct_done, mask_ready)
        s.sems.begin_at(16, *mask_stored)
        block = ctx.enter_context(nc.Block())

        @block.vector
        def _(dve):
            def program():
                for t in range(T):
                    dve.tensor_tensor(CT[:, t, t * R:(t + 1) * R], CT[:, t, t * R:(t + 1) * R], ident[0:R, 0:R], ALU.add)\
                       .then_inc(loops_ready, 1)
                dve.wait_ge(loops_ready, T)
                dve.sem_inc(loops_ready, 1)
                with dve.Fori(0, T // 2) as u:
                    for i in range(2):
                        b = 2 * u + i
                        dve.wait_ge(ct_done, b + 1)
                        dve.tensor_scalar(cb[i][:, :, :], CT[:, :, ds(b * R, R)], 1.0, None, ALU.min).then_inc(cb_ready, 1)
                        dve.wait_ge(ct_done, b + 2)
                        dve.wait_ge(mask_stored[i], 16 * u + 16)
                        for h, (t0, t1) in enumerate(((0, 8), (8, T))):
                            ins = dve.tensor_scalar(mk[i][:, t0 * R:t1 * R].rearrange("p (t r) -> p t r", r=R),
                                                    p_t[i][:, h, 0:(t1 - t0) * RS].rearrange("p (t r) -> p t r", r=RS)[:, :, 0:R],
                                                    1.0, BIG, ALU.subtract, ALU.mult)
                        ins.then_inc(mask_ready, 1)

            guarded(dve, flag, program)

        @block.tensor
        def _(pe):
            def program():
                with pe.Fori(0, T // 2) as u:
                    for i in range(2):
                        b = 2 * u + i
                        pe.wait_ge(cb_ready, b + 1)
                        pe.wait_ge(mask_ready, b + 1)
                        for t in range(T):
                            last = pe.transpose(p_t[i][:, t // 8, t % 8 * RS:t % 8 * RS + R], cb[i][:, t, :], identb[0:R, 0:R])
                        last.then_inc(ct_done, 1)

            guarded(pe, flag, program)

        @block.sync
        def _(sp):
            def program():
                with sp.Fori(0, T // 2) as u:
                    for i in range(2):
                        sp.wait_ge(mask_ready, 2 * u + i + 2)
                        sp.dma_start(mask_dram[ds((2 * u + i) * R, R), :], mk[i][:, :]).then_inc(mask_stored[i], 16)
                for i in range(2):
                    sp.wait_ge(mask_stored[i], 16 * (T // 2) + 16)

            guarded(sp, flag, program)

    see_sources(nc, s, "general", rows_dram, mask_dram, peaks, flag)


def see_sources(nc, s, name, rows_dram, mask_dram, peaks, flag=None):
    T, H, N = s.T, s.H, s.N
    with ExitStack() as ctx:
        sem = s.sems.new
        a_src = ctx.enter_context(nc.sbuf_tensor(f"a_src_rows_{name}", [R, H, N], F32))
        mask = [ctx.enter_context(nc.sbuf_tensor(f"mask_{name}{i}", [R, N], BF16)) for i in range(2)]
        peak = [ctx.enter_context(nc.sbuf_tensor(f"peak_{name}{i}", [R, H], F32)) for i in range(2)]
        junk = ctx.enter_context(nc.sbuf_tensor(f"masked_{name}", [R, N], BF16))
        src_loaded = [sem(f"a_src_loaded_{name}{h}") for h in range(H)]
        mask_loaded = [sem(f"mask_loaded_{name}{i}") for i in range(2)]
        seen, kept, turns, see_chain = (sem(f"{n}_{name}") for n in ("seen", "kept", "turns", "see_chain"))
        s.sems.begin_at(2, seen)
        block = ctx.enter_context(nc.Block())

        @block.sync
        def _(sp):
            def program():
                def load(t, i):
                    sp.wait_ge(seen, t + 1)
                    sp.dma_start(mask[i][:, :], mask_dram[ds(t * R, R), :]).then_inc(mask_loaded[i], 16)

                sp.dma_start(a_src[:, 0, :], rows_dram[0:1, :].to_broadcast([R, N])).then_inc(src_loaded[0], 16)
                for i in range(2):
                    load(i, i)
                for h in range(1, H):
                    sp.dma_start(a_src[:, h, :], rows_dram[h:h + 1, :].to_broadcast([R, N])).then_inc(src_loaded[h], 16)
                with sp.Fori(1, T // 2) as u:
                    for i in range(2):
                        load(2 * u + i, i)

            guarded(sp, flag, program)

        @block.vector
        def _(dve):
            link = Chain(dve, see_chain)

            def tile(t, u, i, first):
                link.at(t * H)
                dve.wait_ge(mask_loaded[i], 16 * (u + 1))
                for h in range(H):
                    if first:
                        dve.wait_ge(src_loaded[h], 16)
                    dve.sem_inc(turns, 1)
                    link(dve.tensor_tensor_reduce(out=junk[:, :], in0=a_src[:, h, :], in1=mask[i][:, :], scale=1.0,
                                                  scalar=-3.0e38, op0=ALU.add, op1=ALU.max, accum_out=peak[i][:, h:h + 1]))
                dve.sem_inc(seen, 1)
                dve.tensor_copy(peaks[:, ds(t, 1), :].rearrange("p a h -> p (a h)"), peak[i][:, :]).then_inc(kept, 1)

            def program():
                for i in range(2):
                    tile(i, 0, i, i == 0)
                with dve.Fori(1, T // 2) as u:
                    for i in range(2):
                        tile(2 * u + i, u, i, False)
                dve.wait_ge(kept, T)

            guarded(dve, flag, program)


def gat(nc, s, layer, C, haug, adcol, bias, rows_dram, mask_dram, CT, ident, spare, tail):
    T, N, H = s.T, s.N, s.H
    PAIRS = H // 2
    W = C + 1
    AHEAD = 5
    with ExitStack() as ctx:
        def sb(name, shape, dt=F32):
            return ctx.enter_context(nc.sbuf_tensor(f"{name}_{layer}", shape, dt))

        def sem(name):
            return s.sems.new(f"{name}_{layer}")

        a_src = sb("a_src", [R, H, N])
        mask = sb("mask_tile", [R, N], BF16)
        y = [sb(f"scores{h}", [R, N]) for h in range(H)]
        rl = [sb(f"relu{i}", [R, N]) for i in range(2)]
        pT = [sb(f"weights_T{i}", [R, T, R]) for i in range(2)]
        peak = [sb(f"peak{p}", [R, 2]) for p in range(PAIRS)]
        nz, nm = sb("neg_peak", [R, 2]), sb("neg_shift", [R, 2])
        shift = [sb(f"shift{p}", [R, 2, 2]) for p in range(PAIRS)]
        total, inv = sb("total", [R, 2]), sb("inv_total", [R, 2])
        bias_rows = spare[0:R, 0:H * C]
        res = spare[0:R, H * C:2 * H * C]
        p_t = [ctx.enter_context(nc.psum_tensor(f"p_weights_T{i}_{layer}", [128, 3, BANK], F32)) for i in range(2)]
        p_o = [ctx.enter_context(nc.psum_tensor(f"p_sums{i}_{layer}", [R, BANK], F32)) for i in range(2)]

        src_loaded = [sem(f"a_src_loaded{h}") for h in range(H)]
        bias_loaded, mask_loaded = sem("bias_loaded"), sem("mask_loaded")
        mask_used, shift_ready, relu_ready, logits_ready, weights_ready = (sem(n) for n in (
            "mask_used", "shift_ready", "relu_ready", "logits_ready", "weights_ready"))
        T_done, pT_ready, sum_done, res_ready = (sem(n) for n in ("T_done", "pT_ready", "sum_done", "res_ready"))
        vec_chain, turns = sem("gat_vec_chain"), sem("score_turns")
        tail = tail(nc, s, ctx, layer, sb, sem, res, p_t, spare, y)
        tail.res_ready = res_ready
        block = ctx.enter_context(nc.Block())

        @block.sync
        def _(sp):
            def load_mask(t):
                sp.dma_start(mask[:, :], mask_dram[ds(t * R, R), :]).then_inc(mask_loaded, 16)

            load_mask(0)
            for h in range(H):
                sp.dma_start(a_src[:, h, :], rows_dram[h:h + 1, :].to_broadcast([R, N])).then_inc(src_loaded[h], 16)
            sp.dma_start(bias_rows, bias[None, :].to_broadcast([R, H * C])).then_inc(bias_loaded, 16)
            tail.load(sp)
            with sp.Fori(1, T) as t:
                sp.wait_ge(mask_used, t)
                load_mask(t)
                tail.load_tile(sp, t)
            tail.store(sp)

        @block.vector
        def _(dve):
            link = Chain(dve, vec_chain)
            PER_PAIR = 6

            def scores(t, h, first):
                e, p = h % 2, h // 2
                if h == 0:
                    dve.wait_ge(mask_loaded, 16 * (t + 1))
                if first:
                    dve.wait_ge(src_loaded[h], 16)
                else:
                    dve.wait_ge(T_done, (t - 1) * H + h + 1)
                dve.sem_inc(turns, 1)
                ins = dve.tensor_tensor_reduce(out=y[h][:, :], in0=a_src[:, h, :], in1=mask[:, :], scale=SLOPE,
                                               scalar=-3.0e38, op0=ALU.add, op1=ALU.max, accum_out=peak[p][:, e:e + 1])
                if e == 0:
                    return
                link(ins)
                if h == H - 1:
                    dve.sem_inc(mask_used, 1)
                ad = adcol[:, ds(t, 1), H + 2 * p:H + 2 * p + 2].rearrange("p a h -> p (a h)")
                link(dve.scalar_tensor_tensor(nz[:, :], peak[p][:, :], -1.0 / SLOPE, ad, ALU.mult, ALU.subtract))
                link(dve.scalar_tensor_tensor(nm[:, :], nz[:, :], SLOPE, nz[:, :], ALU.mult, ALU.min))
                dve.tensor_scalar(shift[p][:, 0, :], ad, 1.0 - SLOPE, None, ALU.mult)
                link(dve.scalar_tensor_tensor(shift[p][:, 1, :], ad, SLOPE, nm[:, :], ALU.mult, ALU.add))
                dve.sem_inc(shift_ready, 1)

            def pair_result(t, p):
                dve.wait_ge(sum_done, t * H + 2 * p + 2)
                if p == 0:
                    tail.wait_res_free(dve, t)
                sums = p_o[p % 2][:, 0:2 * W].rearrange("p (e w) -> p e w", e=2)
                link(dve.tensor_scalar(total[:, :], sums[:, :, C], 1e-16, None, ALU.add))
                link(dve.reciprocal(inv[:, :], total[:, :]))
                for e in range(2):
                    h = 2 * p + e
                    dve.scalar_tensor_tensor(res[:, h * C:(h + 1) * C], sums[:, e, 0:C], inv[:, e:e + 1],
                                             bias_rows[:, h * C:(h + 1) * C], ALU.mult, ALU.add).then_inc(res_ready, 1)
                if p == PAIRS - 1:
                    tail.vector(dve, t)

            def times_counts(t, h, first):
                Q = t * H + h
                dve.wait_ge(T_done, Q + 1)
                if not (first and h < 2):
                    dve.wait_ge(sum_done, Q - 1)
                for b0, b1 in ((0, 2), (2, 3)):
                    j0, j1 = 4 * b0, min(4 * b1, T)
                    ins = dve.tensor_tensor(
                        pT[h % 2][:, j0:j1, :].rearrange("p (b j) r -> p b j r", b=b1 - b0),
                        p_t[h % 2][0:R, b0:b1, 0:(j1 - j0) // (b1 - b0) * R].rearrange("p b (j r) -> p b j r", r=R),
                        CT[:, j0:j1, ds(t * R, R)].rearrange("p (b j) r -> p b j r", b=b1 - b0), ALU.mult)
                ins.then_inc(pT_ready, 1)

            def tile(t, first=False, last=False):
                for h in range(H):
                    if h + AHEAD < H:
                        scores(t, h + AHEAD, first)
                    elif not last:
                        scores(t + 1, h + AHEAD - H, False)
                    if h % 2 == 1 and h > 1:
                        pair_result(t, h // 2 - 1)
                    elif h == 1 and not first:
                        pair_result(t - 1, PAIRS - 1)
                    times_counts(t, h, first)

            tail.vector_begin(dve)
            dve.wait_ge(bias_loaded, 16)
            for h in range(AHEAD):
                scores(0, h, True)
            tile(0, first=True)
            start = link.n
            with dve.Fori(1, T - 1) as t:
                link.at(start + (t - 1) * PER_PAIR * PAIRS)
                tile(t)
                assert link.n == PER_PAIR * PAIRS
            link.at(start + (T - 2) * PER_PAIR * PAIRS)
            tile(T - 1, last=True)
            pair_result(T - 1, PAIRS - 1)
            tail.vector_end(dve)

        @block.scalar
        def _(act):
            def relu(t, h, first):
                act.wait_ge(shift_ready, t * PAIRS + h // 2 + 1)
                if not (first and h < 2):
                    act.wait_ge(logits_ready, t * H + h - 1)
                act.activation(rl[h % 2][:, :], y[h][:, :], ACT.Relu, bias=shift[h // 2][:, 0, h % 2:h % 2 + 1],
                               scale=(1.0 - SLOPE) / SLOPE).then_inc(relu_ready, 1)

            def exp(t, h):
                act.wait_ge(logits_ready, t * H + h + 1)
                act.activation(y[h][:, :], y[h][:, :], ACT.Exp, bias=shift[h // 2][:, 1, h % 2:h % 2 + 1])\
                   .then_inc(weights_ready, 1)

            def tile(t, first=False, last=False):
                for h in range(H):
                    if h < H - 1:
                        relu(t, h + 1, first)
                    elif not last:
                        relu(t + 1, 0, False)
                    exp(t, h)
                    if h == 4 and not first:
                        tail.scalar_first(act, t - 1)
                    if h == 4 and not first:
                        tail.scalar_second(act, t - 1)

            relu(0, 0, True)
            tile(0, first=True)
            with act.Fori(1, T - 1) as t:
                tile(t)
            tile(T - 1, last=True)
            tail.scalar_first(act, T - 1)
            tail.scalar_second(act, T - 1)
            tail.scalar_end(act)

        @block.gpsimd
        def _(pool):
            with pool.Fori(0, T) as t:
                for h in range(H):
                    pool.wait_ge(relu_ready, t * H + h + 1)
                    pool.tensor_tensor(y[h][:, :], y[h][:, :], rl[h % 2][:, :], ALU.add).then_inc(logits_ready, 1)

        @block.tensor
        def _(pe):
            def turn(t, h, first):
                Q = t * H + h
                pe.wait_ge(weights_ready, Q + 1)
                if not (first and h < 2):
                    pe.wait_ge(pT_ready, Q - 1)
                if h in (2, 3) and not first:
                    tail.wait_p_t_free(pe, t, h)
                for j in range(T):
                    last = pe.transpose(p_t[h % 2][0:R, j // 4, j % 4 * R:(j % 4 + 1) * R], y[h][:, j * R:(j + 1) * R],
                                        ident[0:R, 0:R])
                last.then_inc(T_done, 1)

            def add_up(t, h):
                Q = t * H + h
                pe.wait_ge(pT_ready, Q + 1)
                if h % 2 == 0:
                    if not (isinstance(t, int) and Q < 4):
                        pe.wait_ge(res_ready, Q - 2)
                for j in range(T):
                    last = pe.matmul(p_o[h // 2 % 2][:, h % 2 * W:(h % 2 + 1) * W], pT[h % 2][:, j, :], haug[:, j, h, :],
                                     start=j == 0, stop=j == T - 1)
                last.then_inc(sum_done, 1)

            def tile(t, first=False):
                turn(t, 0, first)
                if not first:
                    add_up(t - 1, H - 1)
                turn(t, 1, first)
                add_up(t, 0)
                if not first:
                    tail.tensor_first(pe, t - 1)
                if not first:
                    add_up(t, 1)
                    tail.tensor_second(pe, t - 1)
                for h in range(2, H):
                    turn(t, h, first)
                    if h > 2 or first:
                        add_up(t, h - 1)

            tail.wait_values(pe)
            tile(0, first=True)
            with pe.Fori(1, T) as t:
                tile(t)
            add_up(T - 1, H - 1)
            tail.tensor_first(pe, T - 1)
            tail.tensor_second(pe, T - 1)
            tail.tensor_end(pe)


class ToLayerTwo:

    def __init__(self, h1_dram, haug, w2, w2att, h2_dram, adcol2, rows_dram, ident):
        self.h1_dram, self.haug = h1_dram, haug
        self.w2_dram, self.w2att, self.h2_dram, self.adcol2, self.rows_dram, self.ident = (
            w2, w2att, h2_dram, adcol2, rows_dram, ident)

    def __call__(self, nc, s, ctx, layer, sb, sem, res, p_t, spare, y):
        self.s, self.res, self.p_t, self.y = s, res, p_t, y
        self.K = s.HC // 128
        self.D2 = s.H * s.C2
        self.w2 = sb("w2", [128, self.K, self.D2])
        self.h2 = sb("h2_tile", [R, self.D2])
        n = self.K * R
        self.hT = spare[:, 2 * s.HC:2 * s.HC + n].rearrange("p (k r) -> p k r", k=self.K)
        (self.loaded, self.hT_done, self.hT_out, self.h2_done, self.h2_out, self.rows_done,
         self.rows_out, self.stored) = (sem(n) for n in (
            "w2_loaded", "hT_done", "hT_out", "h2_done", "h2_out", "rows_done", "rows_out", "rows_stored"))
        self.h2_stored = sem("h2_stored")
        self.h1_loaded, self.ones_ready = sem("h1_loaded"), sem("h1_ones_ready")
        s.sems.begin_at(1, self.h2_done)
        s.sems.begin_at(16, self.h2_stored)
        return self

    def load(self, sp):
        s = self.s
        for t in range(s.T):
            sp.dma_start(self.haug[:, t, :, 0:s.C1], self.h1_dram[t * R:(t + 1) * R, :].rearrange("r (h c) -> r h c", h=s.H))\
              .then_inc(self.h1_loaded, 16)
        sp.dma_start(self.w2[:, :, :], self.w2_dram.rearrange("(k p) n -> p k n", p=128)).then_inc(self.loaded, 16)

    def load_tile(self, sp, t):
        pass

    def store(self, sp):
        sp.wait_ge(self.rows_out, 1)
        sp.dma_start(self.rows_dram, self.y[0][0:self.s.H, :]).then_inc(self.stored, 16)
        sp.wait_ge(self.stored, 16)

    def wait_res_free(self, dve, t):
        dve.wait_ge(self.hT_done, t)

    def vector_begin(self, dve):
        dve.memset(self.haug[:, :, :, self.s.C1:self.s.C1 + 1], 1.0).then_inc(self.ones_ready, 1)

    def vector(self, dve, t):
        pass

    def vector_end(self, dve):
        s = self.s
        dve.wait_ge(self.rows_done, 1)
        for b in range(3):
            j0, j1 = 4 * b, min(4 * b + 4, s.T)
            ins = dve.tensor_copy(self.y[0][0:2 * s.H, j0 * R:j1 * R], self.p_t[0][0:2 * s.H, b, 0:(j1 - j0) * R])
        ins.then_inc(self.rows_out, 1)

    def scalar_first(self, act, t):
        act.wait_ge(self.hT_done, t + 1)
        act.wait_ge(self.h2_done, t + 1)
        act.activation(self.hT.rearrange("p (b k) r -> p b (k r)", b=2), self.p_t[0][:, 0:2, 0:4 * R], ACT.Relu)\
           .then_inc(self.hT_out, 1)

    def scalar_second(self, act, t):
        s = self.s
        act.wait_ge(self.h2_done, t + 1 + 1)
        act.wait_ge(self.h2_stored, 16 * (t + 1))
        act.activation(self.h2[:, :], self.p_t[1][0:R, 0, 0:self.D2], ACT.Copy)
        act.activation(self.adcol2[:, ds(t, 1), :].rearrange("p a h -> p (a h)"), self.p_t[1][0:R, 1, 0:2 * s.H], ACT.Copy)\
           .then_inc(self.h2_out, 1)
        act.wait_ge(self.h2_out, t + 1)
        act.dma_start(self.h2_dram[ds(t * R, R), :], self.h2[:, :]).then_inc(self.h2_stored, 16)

    def scalar_end(self, act):
        act.wait_ge(self.h2_stored, 16 * (self.s.T + 1))

    def wait_values(self, pe):
        pe.wait_ge(self.h1_loaded, 16 * self.s.T)
        pe.wait_ge(self.ones_ready, 1)

    def wait_p_t_free(self, pe, t, h):
        pe.wait_ge(self.hT_out if h == 2 else self.h2_out, t)

    def tensor_first(self, pe, t):
        s = self.s
        pe.wait_ge(self.res_ready, s.H * (t + 1))
        for k in range(self.K):
            last = pe.transpose(self.p_t[0][:, k // 4, k % 4 * R:(k % 4 + 1) * R], self.res[:, k * 128:(k + 1) * 128],
                                self.ident[0:R, 0:R])
        last.then_inc(self.hT_done, 1)

    def tensor_second(self, pe, t):
        pe.wait_ge(self.loaded, 16)
        pe.wait_ge(self.hT_out, t + 1)
        for k in range(self.K):
            pe.matmul(self.p_t[1][0:R, 0, 0:self.D2], self.hT[:, k, :], self.w2[:, k, :], start=k == 0, stop=k == self.K - 1)
        for k in range(self.K):
            last = pe.matmul(self.p_t[1][0:R, 1, 0:2 * self.s.H], self.hT[:, k, :], self.w2att[:, k, :],
                             start=k == 0, stop=k == self.K - 1)
        last.then_inc(self.h2_done, 1)

    def tensor_end(self, pe):
        s = self.s
        pe.wait_ge(self.h2_out, s.T)
        for t in range(s.T):
            last = pe.transpose(self.p_t[0][0:2 * s.H, t // 4, t % 4 * R:(t % 4 + 1) * R], self.adcol2[:, t, :],
                                self.ident[0:R, 0:R])
        last.then_inc(self.rows_done, 1)


class ToResidual:

    def __init__(self, h2_dram, haug2, mix_dram, x1):
        self.h2_dram, self.haug2, self.mix_dram, self.x1 = h2_dram, haug2, mix_dram, x1

    def __call__(self, nc, s, ctx, layer, sb, sem, res, p_t, spare, y):
        self.s, self.res = s, res
        self.mix, self.junk = (spare[0:R, i * s.D:(i + 1) * s.D] for i in (2, 3))
        self.neg_peak, self.sums, self.logs = (sb(f"log_softmax_{n}", [R, s.T]) for n in ("neg_peak", "sums", "logs"))
        self.mix_loaded, self.peaks_ready, self.exps_done, self.x1_ready, self.logs_ready, self.x1_done = (sem(n) for n in (
            "mix_loaded", "ls_peak_ready", "ls_exps_done", "x1_ready", "ls_logs_ready", "x1_done"))
        self.h2_loaded, self.ones_ready = sem("h2_loaded"), sem("h2_ones_ready")
        return self

    def load(self, sp):
        for t in range(self.s.T):
            sp.dma_start(self.haug2[:, t, :, 0:self.s.C2], self.h2_dram[t * R:(t + 1) * R, :].rearrange("r (h c) -> r h c", h=self.s.H))\
              .then_inc(self.h2_loaded, 16)
        sp.dma_start(self.mix[:, :], self.mix_dram[0:R, :]).then_inc(self.mix_loaded, 16)

    def load_tile(self, sp, t):
        sp.wait_ge(self.x1_ready, t)
        sp.dma_start(self.mix[:, :], self.mix_dram[ds(t * R, R), :]).then_inc(self.mix_loaded, 16)

    def store(self, sp):
        pass

    def wait_res_free(self, dve, t):
        dve.wait_ge(self.exps_done, t)

    def vector(self, dve, t):
        dve.wait_ge(self.res_ready, self.s.H * (t + 1))
        dve.tensor_reduce(self.neg_peak[:, ds(t, 1)], self.res, AX, ALU.max, negate=True).then_inc(self.peaks_ready, 1)
        dve.wait_ge(self.mix_loaded, 16 * (t + 1))
        dve.wait_ge(self.peaks_ready, t + 1)
        dve.scalar_tensor_tensor(self.x1[:, ds(t, 1), :].rearrange("p a n -> p (a n)"), self.res,
                                 self.neg_peak[:, ds(t, 1)], self.mix[:, :], ALU.add, ALU.add).then_inc(self.x1_ready, 1)

    def vector_end(self, dve):
        s = self.s
        dve.wait_ge(self.x1_ready, s.T)
        dve.wait_ge(self.logs_ready, 1)
        for t in range(s.T):
            dve.tensor_scalar(self.x1[:, t, :], self.x1[:, t, :], self.logs[:, t:t + 1], None, ALU.subtract)\
               .then_inc(self.x1_done, 1)
        dve.wait_ge(self.x1_done, s.T)

    def scalar_first(self, act, t):
        act.wait_ge(self.peaks_ready, t + 1)
        act.activation(self.junk[:, :], self.res, ACT.Exp, bias=self.neg_peak[:, ds(t, 1)],
                       accum_out=self.sums[:, ds(t, 1)]).then_inc(self.exps_done, 1)

    def scalar_second(self, act, t):
        pass

    def vector_begin(self, dve):
        dve.memset(self.haug2[:, :, :, self.s.C2:self.s.C2 + 1], 1.0).then_inc(self.ones_ready, 1)

    def wait_values(self, pe):
        pe.wait_ge(self.h2_loaded, 16 * self.s.T)
        pe.wait_ge(self.ones_ready, 1)

    def scalar_end(self, act):
        act.wait_ge(self.exps_done, self.s.T)
        act.activation(self.logs[:, :], self.sums[:, :], ACT.Ln).then_inc(self.logs_ready, 1)

    def wait_p_t_free(self, pe, t, h):
        pass

    def tensor_first(self, pe, t):
        pass

    def tensor_second(self, pe, t):
        pass

    def tensor_end(self, pe):
        pass


def expert_ffn(nc, s, x1, router_w, w1, b1, w2, b2, ident, out):
    T, D, KC, N, NE, F = s.T, s.D, s.KC, s.N, s.NE, s.F
    KF = F // 128
    CB = [(k * BANK, min(N - k * BANK, BANK)) for k in range(3)]
    with ExitStack() as ctx:
        def sb(name, shape, dt=F32):
            return ctx.enter_context(nc.sbuf_tensor(f"ffn_{name}", shape, dt))

        def ps(name, shape, dt=F32):
            return ctx.enter_context(nc.psum_tensor(f"p_ffn_{name}", shape, dt))

        def sem(name):
            return s.sems.new(f"ffn_{name}")

        r_raw, w1_raw, w2_raw = sb("router", [NE, D]), sb("w1", [128, KF, D]), sb("w2", [128, KC, F])
        rT, w1T, w2T = sb("router_T", [128, KC, NE]), sb("w1_T", [128, KC, F]), sb("w2_T", [128, KF, D])
        b1c, b2b = sb("b1", [128, KF]), sb("b2", [R, D])
        xn = [sb(f"xn{i}", [R, D]) for i in range(2)]
        xT = [sb(f"xT{i}", [128, KC, R]) for i in range(2)]
        xT_all, hT = sb("xT_all", [128, KC, N]), sb("hT", [128, KF, N])
        stat, mv = sb("stat", [R, T, 6]), sb("mean_var", [R, T, 2])
        ve, std, rstd, scratch = (sb(n, [R, T]) for n in ("var_eps", "std", "rstd", "scratch"))
        logits, probs, sel, kept = (sb(n, [R, T, NE]) for n in ("logits", "probs", "chosen", "kept"))
        one = sb("one_chosen", [R, T, NE])
        selb = sb("chosen_bf16", [R, T, NE], BF16)
        peak, total, inv, gate = (sb(n, [R, T]) for n in ("peak", "total", "inv_total", "gate"))
        best = sb("best", [R, T, 8])
        best_i = sb("best_index", [R, T, 8], U32)
        best_f = sb("best_index_f", [R, T, 2])
        iota_i, iota_e = sb("iota_i", [R, NE], I32), sb("iota_e", [R, NE])
        upper, onesb = sb("earlier", [R, R], BF16), sb("ones_bf16", [R, R], BF16)
        yb = sb("y_plus_b2", [R, D])
        fin = [sb(f"result{i}", [R, D]) for i in range(2)]
        p_w = [ps(f"weights{i}", [128, BANK]) for i in range(2)]
        p_x, p_l = ps("xT", [128, BANK]), ps("logits", [R, BANK])
        p_h = [ps(f"h{i}", [128, BANK]) for i in range(2)]
        p_y = [ps(f"y{i}", [R, BANK]) for i in range(2)]

        (loaded, wT_done, wT_out, var_ready, std_ready, xn_ready, xT_done, xT_out, xT_kept, logits_done, logits_out,
         shifted, exps, consts, chosen, pos_done, h_done, h_out, y_done, y_out, fin_ready, chain, pool_chain) = (sem(n) for n in (
            "loaded", "wT_done", "wT_out", "var_ready", "std_ready", "xn_ready", "xT_done", "xT_out", "xT_kept",
            "logits_done", "logits_out", "logits_shifted", "exps_ready", "constants_ready", "chosen_ready", "positions_done",
            "h_done", "h_out", "y_done", "y_out", "result_ready", "vec_chain", "pool_chain"))
        stored = [sem(f"stored{i}") for i in range(2)]
        TURNS = ([[(rT[:, k, :], r_raw[:, k * 128:(k + 1) * 128], NE) for k in range(KC)]]
                 + [[(w1T[:, k, f * 128:(f + 1) * 128], w1_raw[:, f, k * 128:(k + 1) * 128], 128) for k in range(KC)]
                    for f in range(KF)]
                 + [[(w2T[:, f, k * 128:(k + 1) * 128], w2_raw[:, k, f * 128:(f + 1) * 128], 128) for k in range(KC)]
                    for f in range(KF)])
        s.sems.begin_at(1, xT_done, xT_out, logits_out, xT_kept, logits_done)
        block = ctx.enter_context(nc.Block())

        @block.sync
        def _(sp):
            sp.dma_start(r_raw[:, :], router_w).then_inc(loaded, 16)
            sp.dma_start(w1_raw[:, :, :], w1.rearrange("(f p) n -> p f n", p=128)).then_inc(loaded, 16)
            sp.dma_start(w2_raw[:, :, :], w2.rearrange("(k p) n -> p k n", p=128)).then_inc(loaded, 16)
            with nc.allow_non_contiguous_dma(reason="one short vector, once"):
                sp.dma_start(b1c[:, :], b1.rearrange("(f p) -> p f", p=128)).then_inc(loaded, 16)
            sp.dma_start(b2b[:, :], b2[None, :].to_broadcast([R, D])).then_inc(loaded, 16)
            for t in range(T):
                sp.wait_ge(fin_ready, t + 1)
                sp.dma_start(out[t * R:(t + 1) * R, :], fin[t % 2][:, :]).then_inc(stored[t % 2], 16)
            for i in range(2):
                sp.wait_ge(stored[i], 16 * (T // 2))

        @block.gpsimd
        def _(pool):
            link = Chain(pool, pool_chain)
            link(pool.iota(iota_i[:, :], [[1, NE]], base=0, channel_multiplier=0))
            link(pool.tensor_copy(iota_e[:, :], iota_i[:, :]))
            link(pool.memset(onesb[:, :], 1.0))
            link(pool.affine_select(out=upper[:, :], in_=onesb[:, :], compare_op=ALU.is_gt, fill=0.0, base=0,
                                    pattern=[[1, R]], channel_multiplier=-1))
            pool.sem_inc(consts, 1)

        @block.tensor
        def _(pe):
            pe.wait_ge(loaded, 16 * 5)
            for n, turn in enumerate(TURNS):
                if n >= 2:
                    pe.wait_ge(wT_out, n - 1)
                for k, (_, src, w) in enumerate(turn):
                    K = src.shape[0]
                    last = pe.transpose(p_w[n % 2][:, k * w:k * w + K], src, ident[0:K, 0:K])
                last.then_inc(wT_done, 1)
            pe.wait_ge(wT_out, len(TURNS))
            with pe.Fori(0, T // 2) as u:
                for i in range(2):
                    t = 2 * u + i
                    pe.wait_ge(xn_ready, t + 1)
                    pe.wait_ge(xT_out, t + 1)
                    for k in range(KC):
                        last = pe.transpose(p_x[:, k * R:(k + 1) * R], xn[i][:, k * 128:(k + 1) * 128], ident[0:R, 0:R])
                    last.then_inc(xT_done, 1)
                    pe.wait_ge(xT_out, t + 1 + 1)
                    pe.wait_ge(logits_out, t + 1)
                    for k in range(KC):
                        last = pe.matmul(p_l[:, 0:NE], xT[i][:, k, :], rT[:, k, :], start=k == 0, stop=k == KC - 1)
                    last.then_inc(logits_done, 1)
            pe.wait_ge(xT_kept, T + 1)
            n = 0
            for c0, w in CB:
                for f in range(KF):
                    if n >= 2:
                        pe.wait_ge(h_out, n - 1)
                    for k in range(KC):
                        last = pe.matmul(p_h[n % 2][:, 0:w], w1T[:, k, f * 128:(f + 1) * 128], xT_all[:, k, c0:c0 + w],
                                         start=k == 0, stop=k == KC - 1)
                    last.then_inc(h_done, 1)
                    n += 1
            pe.wait_ge(consts, 1)
            pe.wait_ge(chosen, 1)
            for t in range(T):
                to = p_w[t // 8][0:R, t % 8 * NE:(t % 8 + 1) * NE]
                for e in range(t + 1):
                    last = pe.matmul(to, (onesb if e < t else upper)[:, :], selb[:, e, :], start=e == 0, stop=e == t)
            last.then_inc(pos_done, 1)
            pe.wait_ge(h_out, n)
            for t in range(T):
                if t >= 2:
                    pe.wait_ge(y_out, t - 1)
                for f in range(KF):
                    last = pe.matmul(p_y[t % 2][:, :], hT[:, f, t * R:(t + 1) * R], w2T[:, f, :], start=f == 0, stop=f == KF - 1)
                last.then_inc(y_done, 1)

        @block.scalar
        def _(act):
            act.wait_ge(var_ready, 1)
            act.activation(std[:, :], ve[:, :], ACT.Sqrt).then_inc(std_ready, 1)
            with act.Fori(0, T // 2) as u:
                for i in range(2):
                    t = 2 * u + i
                    act.wait_ge(xT_done, t + 1 + 1)
                    act.wait_ge(xT_kept, t + 1)
                    act.wait_ge(logits_done, t + 1)
                    act.activation(xT[i][:, :, :].rearrange("p k r -> p (k r)"), p_x[:, 0:KC * R], ACT.Copy).then_inc(xT_out, 1)
                    act.wait_ge(logits_done, t + 1 + 1)
                    act.activation(logits[:, ds(t, 1), :].rearrange("p a n -> p (a n)"), p_l[:, 0:NE], ACT.Copy)\
                       .then_inc(logits_out, 1)
            act.wait_ge(shifted, 1)
            act.activation(probs[:, :, :], logits[:, :, :], ACT.Exp).then_inc(exps, 1)
            n = 0
            for c0, w in CB:
                for f in range(KF):
                    act.wait_ge(h_done, n + 1)
                    act.activation(hT[:, f, c0:c0 + w], p_h[n % 2][:, 0:w], ACT.Gelu, bias=b1c[:, f:f + 1]).then_inc(h_out, 1)
                    n += 1

        @block.vector
        def _(dve):
            link = Chain(dve, chain)
            for t in range(T):
                ins = dve.bn_stats(stat[:, t, :], x1[:, t, :])
            link(ins)
            for t in range(T):
                ins = dve.bn_aggr(mv[:, t, :], stat[:, t, :])
            link(ins)
            dve.tensor_scalar(ve[:, :], mv[:, :, 1], LN_EPS, None, ALU.add).then_inc(var_ready, 1)
            dve.wait_ge(var_ready, 1)
            for n, turn in enumerate(TURNS):
                dve.wait_ge(wT_done, n + 1)
                for k, (to, src, w) in enumerate(turn):
                    ins = dve.tensor_copy(to, p_w[n % 2][:, k * w:k * w + src.shape[0]])
                ins.then_inc(wT_out, 1)
            one_over_sqrt(dve, link, std[:, :], ve[:, :], rstd[:, :], std_ready, 1, scratch[:, :])
            with dve.Fori(0, T // 2) as u:
                for i in range(2):
                    t = 2 * u + i
                    dve.wait_ge(xT_done, t + 1)
                    dve.tensor_scalar(xn[i][:, :], x1[:, ds(t, 1), :].rearrange("p a n -> p (a n)"), mv[:, ds(t, 1), 0],
                                      rstd[:, ds(t, 1)], ALU.subtract, ALU.mult).then_inc(xn_ready, 1)
                    dve.wait_ge(xT_out, t + 1 + 1)
                    dve.tensor_copy(xT_all[:, :, ds(t * R, R)], xT[i][:, :, :]).then_inc(xT_kept, 1)
            dve.wait_ge(logits_out, T + 1)
            link(dve.tensor_reduce(peak[:, :], logits[:, :, :], AX, ALU.max))
            link(dve.tensor_tensor(logits[:, :, :], logits[:, :, :], peak[:, :, None].to_broadcast([R, T, NE]), ALU.subtract))
            dve.sem_inc(shifted, 1)
            dve.wait_ge(exps, 1)
            link(dve.tensor_reduce(total[:, :], probs[:, :, :], AX, ALU.add))
            link(dve.reciprocal(inv[:, :], total[:, :]))
            link(dve.tensor_tensor(probs[:, :, :], probs[:, :, :], inv[:, :, None].to_broadcast([R, T, NE]), ALU.mult))
            for t in range(T):
                ins = dve.max(best[:, t, :], probs[:, t, :])
            link(ins)
            for t in range(T):
                ins = dve.max_index(best_i[:, t, :], best[:, t, :], probs[:, t, :])
            link(ins)
            link(dve.tensor_copy(best_f[:, :, :], best_i[:, :, 0:2]))
            dve.wait_ge(consts, 1)
            which = iota_e[:, None, :].to_broadcast([R, T, NE])
            dve.tensor_tensor(sel[:, :, :], which, best_f[:, :, 0:1].to_broadcast([R, T, NE]), ALU.is_equal)
            link(dve.tensor_tensor(one[:, :, :], which, best_f[:, :, 1:2].to_broadcast([R, T, NE]), ALU.is_equal))
            link(dve.tensor_tensor(sel[:, :, :], sel[:, :, :], one[:, :, :], ALU.add))
            link(dve.tensor_copy(selb[:, :, :], sel[:, :, :]))
            dve.sem_inc(chosen, 1)
            link(dve.tensor_tensor(probs[:, :, :], probs[:, :, :], sel[:, :, :], ALU.mult))
            dve.wait_ge(pos_done, 1)
            for b, (t0, t1) in enumerate(((0, 8), (8, T))):
                ins = dve.tensor_scalar(kept[:, t0:t1, :].rearrange("p t n -> p (t n)"), p_w[b][0:R, 0:(t1 - t0) * NE], float(CAP), None,
                                        ALU.is_lt)
            link(ins)
            link(dve.tensor_tensor(kept[:, :, :], kept[:, :, :], probs[:, :, :], ALU.mult))
            link(dve.tensor_reduce(gate[:, :], kept[:, :, :], AX, ALU.add))
            for t in range(T):
                dve.wait_ge(y_done, t + 1)
                if t >= 1:
                    dve.wait_ge(fin_ready, t)
                dve.tensor_tensor(yb[:, :], p_y[t % 2][:, :], b2b[:, :], ALU.add).then_inc(y_out, 1)
                dve.wait_ge(y_out, t + 1)
                if t >= 2:
                    dve.wait_ge(stored[t % 2], 16 * (t // 2))
                dve.scalar_tensor_tensor(fin[t % 2][:, :], yb[:, :], gate[:, t:t + 1], x1[:, t, :], ALU.mult, ALU.add)\
                   .then_inc(fin_ready, 1)


def gps_layer(nc, a, out):
    s = Shapes(nc, a["x"], a["src"], a["L0_gnn_W1"], a["L0_gnn_att_src1"], a["L0_gnn_att_src2"], a["L0_mix_w_out"],
               a["L0_ffn_router_w"], a["L0_ffn_w1"])
    N, D, T, H = s.N, s.D, s.T, s.H

    def scratch(name, shape, dt=F32):
        return nc.dram_tensor(name, shape, dt, kind="Internal").ap()

    rows1, rows2 = scratch("a_src1_rows", [H, N]), scratch("a_src2_rows", [H, N])
    mask, mix = scratch("mask", [N, N], BF16), scratch("x_plus_mix", [N, D])
    h1_dram = scratch("h1_rows", [N, s.HC])
    h2 = scratch("h2_rows", [N, H * s.C2])
    with ExitStack() as ctx:
        def sb(name, shape, dt=F32):
            return ctx.enter_context(nc.sbuf_tensor(name, shape, dt))

        ident, identb = sb("ident", [128, 128]), sb("ident_bf16", [128, 128], BF16)
        adcol1, adcol2 = sb("att1_columns", [R, T, 2 * H]), sb("att2_columns", [R, T, 2 * H])
        w2att = sb("w2_att", [128, s.HC // 128, 2 * H])
        RA = sb("weights_then_counts", [128, s.KC * (s.HC + 3 * D)])
        CT = RA[0:R, 0:T * N // 2].bitcast(U16).rearrange("p (t n) -> p t n", t=T)
        spare = RA[:, T * N // 2:s.KC * (s.HC + 3 * D)]
        peaks = sb("largest_a_src", [R, T, H])
        constants(nc, s, ident, identb)
        with ExitStack() as counting, ExitStack() as attention:
            cnt = Counting(s, counting, nc)
            RB = attention.enter_context(nc.sbuf_tensor("qkv", [128, 8 * N + T * D], F32))
            project(nc, s, a["x"], a["L0_gnn_W1"], a["L0_mix_w_qkv"], a["L0_gnn_att_src1"], a["L0_gnn_att_dst1"],
                    a["L0_gnn_W2"], a["L0_gnn_att_src2"], a["L0_gnn_att_dst2"], RA, RB, ident, adcol1, w2att, h1_dram, rows1)
            prepare_edges(nc, s, cnt, a["src"], a["dst"], ident)
            s.sems.start_over()
            attend_and_count(nc, s, cnt, a["x"], a["L0_mix_ln_gamma"], a["L0_mix_ln_beta"], a["L0_mix_w_out"],
                             a["L0_mix_b_out"], RB, CT, spare, ident, identb, rows1, mask, mix, peaks)
            attention.close()
            verify_counts(nc, s, cnt)
            s.sems.start_over()
            general_path(nc, s, cnt, CT, ident, identb, rows1, mask, peaks)
        s.sems.start_over()
        h1 = sb("h1", [R, T, H, s.C1 + 1])
        gat(nc, s, 1, s.C1, h1, adcol1, a["L0_gnn_b1"], rows1, mask, CT, ident, spare,
            ToLayerTwo(h1_dram, h1, a["L0_gnn_W2"], w2att, h2, adcol2, rows2, ident))
        haug2 = sb("h2_columns", [R, T, H, s.C2 + 1])
        x1 = h1[:, :, :, :].rearrange("p t h c -> p (t h c)")[:, 0:T * D].rearrange("p (t n) -> p t n", t=T)
        gat(nc, s, 2, s.C2, haug2, adcol2, a["L0_gnn_b2"], rows2, mask, CT, ident, spare, ToResidual(h2, haug2, mix, x1))
        expert_ffn(nc, s, x1, a["L0_ffn_router_w"], a["L0_ffn_w1"], a["L0_ffn_b1"], a["L0_ffn_w2"], a["L0_ffn_b2"], ident, out)


_INS = ["x", "src", "dst", "L0_gnn_W1", "L0_gnn_att_src1", "L0_gnn_att_dst1", "L0_gnn_b1", "L0_gnn_W2",
        "L0_gnn_att_src2", "L0_gnn_att_dst2", "L0_gnn_b2", "L0_mix_w_qkv", "L0_mix_ln_gamma", "L0_mix_ln_beta",
        "L0_mix_w_out", "L0_mix_b_out", "L0_ffn_router_w", "L0_ffn_w1", "L0_ffn_b1", "L0_ffn_w2", "L0_ffn_b2"]


def kernel(**inputs):
    import numpy as _np
    import concourse.bacc as _bacc
    from concourse.bass_utils import run_bass_kernel_spmd as _run

    nc = _bacc.Bacc("TRN2", target_bir_lowering=False, num_devices=1)
    arrays, args = {}, {}
    for name in _INS:
        a = _np.ascontiguousarray(inputs[name])
        arrays[f"in_{name}"] = a
        args[name] = nc.dram_tensor(f"in_{name}", a.shape, mybir.dt.from_np(a.dtype), kind="ExternalInput").ap()
    out = nc.dram_tensor("out_0", inputs["x"].shape, F32, kind="ExternalOutput").ap()
    gps_layer(nc, args, out)
    return _run(nc, [arrays], core_ids=[0]).results[0]["out_0"]
```

```python
from contextlib import ExitStack

import concourse.bass as bass
from concourse import mybir

F32 = mybir.dt.float32
BF16 = mybir.dt.bfloat16
I32 = mybir.dt.int32
I16 = mybir.dt.int16
U16 = mybir.dt.uint16
U32 = mybir.dt.uint32
ALU = mybir.AluOpType
ACT = mybir.ActivationFunctionType
AX = mybir.AxisListType.X

R = 125
BANK = 512
BIG = 1.0e30
LN_EPS = 1e-5
SLOPE = 0.2
WIN = 40
MARGIN = 4
CAP = 512


def ds(i, n):
    return bass.ds(i, n)


class Semaphores:

    def __init__(self, nc):
        self.nc, self.held = nc, []

    def new(self, name):
        self.held.append(self.nc.alloc_semaphore(name))
        return self.held[-1]

    def begin_at(self, value, *sems):
        for sem in sems:
            self.nc.gpsimd.sem_inc(sem, value)

    def start_over(self):
        self.nc.clear_and_free_semaphores(self.held)
        self.nc.all_engine_barrier()
        self.held = []


class Shapes:
    def __init__(self, nc, x, src, w1, att, att2, w_out, router, ffn_w1):
        self.sems = Semaphores(nc)
        self.N, self.D = x.shape
        self.T = self.N // R
        self.E = src.shape[0]
        self.ET = self.E // R
        self.H, self.C1 = att.shape
        self.C2 = att2.shape[1]
        self.HC = w1.shape[1]
        self.KC = self.D // 128
        self.NE = router.shape[0]
        self.F = ffn_w1.shape[0]
        assert self.N == self.T * R and self.E == self.ET * R and self.ET % self.T == 0
        assert self.ET // self.T + 2 * MARGIN == WIN


class Chain:

    def __init__(self, engine, sem, base=0):
        self.engine, self.sem, self.base, self.n = engine, sem, base, 0

    def at(self, base):
        self.base, self.n = base, 0

    def __call__(self, instruction):
        self.n += 1
        instruction.then_inc(self.sem, 1)
        self.engine.wait_ge(self.sem, self.base + self.n)


def one_over_sqrt(dve, link, std, ve, out, std_ready, value, scratch):
    dve.wait_ge(std_ready, value)
    link(dve.reciprocal(out, std))
    link(dve.tensor_tensor(scratch, out, out, ALU.mult))
    link(dve.tensor_tensor(scratch, scratch, ve, ALU.mult))
    link(dve.tensor_scalar(scratch, scratch, -0.5, 1.5, ALU.mult, ALU.add))
    link(dve.tensor_tensor(out, out, scratch, ALU.mult))


def guarded(engine, flag, program):
    if flag is None:
        program()
    else:
        value = engine.value_load(flag, min_val=0, max_val=1)
        with engine.If(value > 0):
            program()


class Counting:

    G, BASE = 2, 16
    GOFF, TOFF = 4096, 2048
    NOWHERE = 20000.0

    def __init__(self, s, ctx, nc):
        T, ET = s.T, s.ET
        self.DIG = T // 2

        def sb(name, shape, dt=F32):
            return ctx.enter_context(nc.sbuf_tensor(name, shape, dt))

        self.keyp, self.lop, self.wt = (sb(n, [R, ET + 2 * MARGIN]) for n in ("target_key", "source_key", "digit_weight"))
        self.key3 = sb("general_key", [R, ET])
        self.iota_s, self.iota_d = sb("iota_s", [R, R], I16), sb("iota_d", [R, self.G * R], I16)
        self.first = sb("block_first", [R, T])
        self.found, self.top = sb("found", [R, T]), sb("top", [R, T])
        self.wrong_i = sb("wrong_int", [1, 1], I32)


def edge_keys(nc, s, ctx, cnt, src, dst, ident):
    T, ET = s.T, s.ET
    G, DIG, BASE = cnt.G, cnt.DIG, cnt.BASE
    ROWS = 3
    RW = [min(128, ET - 128 * r) for r in range(ROWS)]
    def sb(name, shape, dt=F32):
        return ctx.enter_context(nc.sbuf_tensor(name, shape, dt))

    sem = s.sems.new
    raw = sb("edges_raw", [128, 2, ROWS, R], I32)
    rowf = sb("edges_f", [128, 2, ROWS, R])
    col = sb("edge_columns", [R, 2, ET])
    hi, grp, dig = (sb(f"src_{n}", [R, ET]) for n in ("tile", "group", "digit"))
    iota32 = sb("iota32", [R, G * R], I32)
    loaded, colT, edges_float = sem("edges_loaded"), sem("edges_transposed"), sem("edges_float")
    vec_chain, pool_chain = sem("edge_vec_chain"), sem("edge_pool_chain")
    p_col = [ctx.enter_context(nc.psum_tensor(f"p_edges{j}", [R, BANK], F32)) for j in range(2)]
    def on_gpsimd(pool):
        for j, a in enumerate((src, dst)):
            for r in range(ROWS):
                pool.dma_start(raw[0:RW[r], j, r, :],
                             a[128 * r * R:(128 * r + RW[r]) * R].rearrange("(k p) -> k p", p=R)).then_inc(loaded, 16)
        link = Chain(pool, pool_chain)
        for to, pattern in ((cnt.iota_s, [[1, R]]), (cnt.iota_d, [[cnt.GOFF, G], [1, R]]), (cnt.first, [[R, T]])):
            n = to.shape[1]
            link(pool.iota(iota32[:, 0:n], pattern, base=0, channel_multiplier=0))
            link(pool.tensor_copy(to[:, :], iota32[:, 0:n]))

    def on_tensor(pe):
        pe.wait_ge(edges_float, 1)
        for j in range(2):
            for r in range(ROWS):
                last = pe.transpose(p_col[j][:, 128 * r:128 * r + RW[r]], rowf[0:RW[r], j, r, :], ident[0:RW[r], 0:RW[r]])
            last.then_inc(colT, 1)

    def on_vector(dve):
        link = Chain(dve, vec_chain)
        dve.wait_ge(loaded, 16 * 2 * ROWS)
        for r in range(ROWS):
            link(dve.tensor_copy(rowf[0:RW[r], :, r, :], raw[0:RW[r], :, r, :]))
        dve.sem_inc(edges_float, 1)
        for j in range(2):
            dve.wait_ge(colT, j + 1)
            link(dve.tensor_copy(col[:, j, :], p_col[j][:, 0:ET]))

    def make_keys(dve):
        link = Chain(dve, vec_chain, ROWS + 2)
        S, D_ = col[:, 0, :], col[:, 1, :]
        link(dve.memset(hi[:, :], 0.0))
        for j in range(1, T):
            link(dve.scalar_tensor_tensor(hi[:, :], S, float(j * R), hi[:, :], ALU.is_ge, ALU.add))
        for pad, value in ((cnt.keyp, cnt.NOWHERE), (cnt.lop, 0.0), (cnt.wt, 1.0)):
            link(dve.memset(pad[:, :], value))
        mid = slice(MARGIN, MARGIN + ET)
        link(dve.scalar_tensor_tensor(cnt.lop[:, mid], hi[:, :], -float(R), S, ALU.mult, ALU.add))
        link(dve.tensor_scalar(grp[:, :], hi[:, :], float(DIG), None, ALU.is_ge))
        link(dve.scalar_tensor_tensor(dig[:, :], grp[:, :], -float(DIG), hi[:, :], ALU.mult, ALU.add))
        link(dve.scalar_tensor_tensor(cnt.keyp[:, mid], grp[:, :], float(cnt.GOFF), D_, ALU.mult, ALU.add))
        for j in range(1, DIG):
            link(dve.tensor_scalar(grp[:, :], dig[:, :], float(j), float(BASE ** j - BASE ** (j - 1)), ALU.is_ge, ALU.mult))
            link(dve.tensor_tensor(cnt.wt[:, mid], cnt.wt[:, mid], grp[:, :], ALU.add))
        link(dve.scalar_tensor_tensor(cnt.key3[:, :], hi[:, :], float(cnt.TOFF), D_, ALU.mult, ALU.add))

    return on_gpsimd, on_tensor, on_vector, make_keys


def project(nc, s, cnt, src, dst, x, w1, wqkv, att_src1, att_dst1, w2, att_src2, att_dst2, W1, WQKV, RB, ident, adcol,
            w2att, h1_dram, rows_dram):
    T, KC, H, D, C1, HC, N = s.T, s.KC, s.H, s.D, s.C1, s.HC, s.N
    W1 = W1[:, :].rearrange("p (k n) -> p k n", k=KC)
    WQKV = WQKV[:, 0:KC * 3 * D].rearrange("p (k n) -> p k n", k=KC)
    M = 2 * D // 128
    QK = RB[:, 0:M * N].rearrange("p (m n) -> p m n", m=M)
    V = RB[0:R, M * N:M * N + T * D].rearrange("p (t n) -> p t n", t=T)
    with ExitStack() as ctx:
        def sb(name, shape, dt=F32):
            return ctx.enter_context(nc.sbuf_tensor(name, shape, dt))

        def ps(name, shape, dt=F32):
            return ctx.enter_context(nc.psum_tensor(name, shape, dt))

        def sem(name):
            return s.sems.new(name)

        xs = [sb(f"x_in{i}", [R, D]) for i in range(2)]
        xn = [sb(f"xn{i}", [R, D]) for i in range(2)]
        xT = [sb(f"xnT{i}", [128, KC, R]) for i in range(2)]
        xT_all = sb("xnT_all", [128, KC, N])
        attb = sb("att1_rows", [128, 2, HC])
        watt = sb("w1_att", [128, KC, 2 * H])
        prod = sb("w1_att_prod", [128, HC])
        h1 = [sb(f"h1_tile{i}", [R, HC]) for i in range(2)]
        K2, HC2 = HC // 128, H * s.C2
        W2, attb2 = sb("w2_for_att", [128, K2, HC2]), sb("att2_rows", [128, 2, HC2])
        stat, mv = sb("ln_stat", [R, 6]), sb("ln_mean_var", [R, 2])
        ve, std, rstd, scratch = (sb(f"ln_{n}", [R, 1]) for n in ("var_eps", "std", "rstd", "scratch"))
        rows = sb("att1_scores", [2 * H, N])
        p_xT = ps("p_xT", [128, BANK])
        p_h1 = ps("p_h1", [R, 2 * BANK])
        p_v = ps("p_v", [R, BANK])
        p_qk = ps("p_qk", [128, 2, BANK])
        NB = 3
        CB = [(k * BANK, min(N - k * BANK, BANK)) for k in range(NB)]

        x_loaded = [sem(f"x_loaded{i}") for i in range(2)]
        w_loaded, wq_loaded, att_loaded = sem("w1_loaded"), sem("wqkv_loaded"), sem("att1_loaded")
        x_used, std_ready, var_ready, turns = sem("x_used"), sem("std_ready"), sem("var_ready"), sem("ln_turns")
        h1_stored = [sem(f"h1_stored{i}") for i in range(2)]
        w2_loaded, wv_loaded = sem("w2_for_att_loaded"), sem("wv_loaded")
        xT_done, xT_copied, xT_kept = sem("xT_done"), sem("xT_copied"), sem("xT_kept")
        qk_done, qk_out, h1_done, h1_out = sem("qk_done"), sem("qk_out"), sem("h1_done"), sem("h1_out")
        v_done, v_out = sem("v_done"), sem("v_out")
        watt_ready, row_done, row_out = sem("watt_ready"), sem("row_done"), sem("row_out")
        col_done, col_out, rows_stored = sem("col_done"), sem("col_out"), sem("rows_stored")
        vec_chain, pool_chain = sem("p1_vec_chain"), sem("p1_pool_chain")
        p_row = [p_h1[0:2 * H, 0:BANK], p_h1[0:2 * H, BANK:2 * BANK], p_v[0:2 * H, :]]
        p_col = p_xT[0:R, 0:T * 2 * H]
        s.sems.begin_at(1, xT_done, v_done, xT_kept, xT_copied, qk_out, h1_out, v_out)
        s.sems.begin_at(16, *h1_stored)
        edges_on_gpsimd, edges_on_tensor, edges_on_vector, make_edge_keys = edge_keys(nc, s, ctx, cnt, src, dst, ident)
        block = ctx.enter_context(nc.Block())

        @block.sync
        def _(sp):
            for i in range(2):
                sp.dma_start(xs[i][:, :], x[i * R:(i + 1) * R, :]).then_inc(x_loaded[i], 16)
            with sp.Fori(1, T // 2) as u:
                for i in range(2):
                    sp.wait_ge(x_used, 2 * u - 1 + i)
                    sp.dma_start(xs[i][:, :], x[ds((2 * u + i) * R, R), :]).then_inc(x_loaded[i], 16)
            sp.wait_ge(row_out, NB)
            sp.dma_start(rows_dram, rows[0:H, :]).then_inc(rows_stored, 16)
            sp.wait_ge(rows_stored, 16)

        @block.gpsimd
        def _(pool):
            edges_on_gpsimd(pool)
            link = Chain(pool, pool_chain)

            def through(w, rows, out, K, C):
                prods = prod[:, 0:H * C].rearrange("p (h c) -> p h c", h=H)
                for k in range(K):
                    for j in range(2):
                        link(pool.tensor_tensor(prod[:, 0:H * C], w[:, k, :], rows[:, j, :], ALU.mult))
                        c = C // 2
                        while c:
                            left, right = prods[:, :, 0:c], prods[:, :, c:2 * c]
                            to = left if c > 1 else out[:, k, j * H:(j + 1) * H].rearrange("p (h c) -> p h c", c=1)
                            link(pool.tensor_tensor(to, left, right, ALU.add))
                            c //= 2

            pool.wait_ge(w_loaded, 16)
            pool.wait_ge(att_loaded, 32)
            pool.dma_start(W2[:, :, :], w2.rearrange("(k p) n -> p k n", p=128)).then_inc(w2_loaded, 16)
            for j, a in enumerate((att_src2, att_dst2)):
                pool.dma_start(attb2[:, j, :], a.rearrange("h c -> (h c)")[None, :].to_broadcast([128, HC2]))\
                    .then_inc(w2_loaded, 16)
            through(W1, attb, watt, KC, C1)
            pool.sem_inc(watt_ready, 1)
            pool.wait_ge(w2_loaded, 48)
            through(W2, attb2, w2att, K2, s.C2)

        @block.vector
        def _(dve):
            link = Chain(dve, vec_chain)
            LINKS = 8

            def normalise(t, u, i):
                link.at(t * LINKS)
                dve.wait_ge(x_loaded[i], 16 * (u + 1))
                link(dve.bn_stats(stat[:, :], xs[i][:, :]))
                dve.sem_inc(turns, 1)
                link(dve.bn_aggr(mv[:, :], stat[:, :]))
                link(dve.tensor_scalar(ve[:, :], mv[:, 1:2], LN_EPS, None, ALU.add))
                dve.sem_inc(var_ready, 1)
                one_over_sqrt(dve, link, std[:, :], ve[:, :], rstd[:, :], std_ready, t + 1, scratch[:, :])
                if not (isinstance(t, int) and t == 0):
                    dve.wait_ge(xT_done, t)
                dve.tensor_scalar(xn[i][:, :], xs[i][:, :], mv[:, 0:1], rstd[:, 0:1], ALU.subtract, ALU.mult).then_inc(x_used, 1)
                assert link.n == LINKS

            def keep(t, i):
                dve.wait_ge(xT_copied, t + 1 + 1)
                dve.tensor_copy(xT_all[:, :, ds(t * R, R)], xT[i][:, :, :]).then_inc(xT_kept, 1)
                dve.wait_ge(qk_done, t + 1)
                dve.tensor_copy(QK[:, :, ds(t * R, R)].rearrange("p (b m) r -> p b m r", b=2),
                                p_qk[:, :, 0:4 * R].rearrange("p b (m r) -> p b m r", m=4)).then_inc(qk_out, 1)

            normalise(0, 0, 0)
            with dve.Fori(0, T // 2 - 1) as u:
                for i in range(2):
                    normalise(2 * u + i + 1, u + i, 1 - i)
                    keep(2 * u + i, i)
            edges_on_vector(dve)
            normalise(T - 1, T // 2 - 1, 1)
            keep(T - 2, 0)
            make_edge_keys(dve)
            keep(T - 1, 1)
            for k, (c0, w) in enumerate(CB):
                dve.wait_ge(row_done, k + 1)
                dve.tensor_copy(rows[:, c0:c0 + w], p_row[k][:, 0:w]).then_inc(row_out, 1)
            dve.wait_ge(col_done, 1)
            dve.tensor_copy(adcol[:, :, :], p_col.rearrange("p (t h) -> p t h", t=T)).then_inc(col_out, 1)
            dve.wait_ge(col_out, 1)

        @block.scalar
        def _(act):
            wqkv_rows = wqkv.rearrange("(k p) n -> p k n", p=128)
            act.dma_start(WQKV[:, :, 0:2 * D], wqkv_rows[:, :, 0:2 * D]).then_inc(wq_loaded, 16)
            act.dma_start(W1, w1.rearrange("(k p) n -> p k n", p=128)).then_inc(w_loaded, 16)
            act.dma_start(WQKV[:, :, 2 * D:3 * D], wqkv_rows[:, :, 2 * D:3 * D]).then_inc(wv_loaded, 16)
            for j, a in enumerate((att_src1, att_dst1)):
                act.dma_start(attb[:, j, :], a.rearrange("h c -> (h c)")[None, :].to_broadcast([128, HC]))\
                   .then_inc(att_loaded, 16)

            def root(t):
                act.wait_ge(var_ready, t + 1)
                act.activation(std[:, :], ve[:, :], ACT.Sqrt).then_inc(std_ready, 1)

            def copy_xT(t, i):
                act.wait_ge(xT_done, t + 1 + 1)
                act.wait_ge(xT_kept, t)
                act.wait_ge(v_done, t)
                act.activation(xT[i][:, :, :].rearrange("p k r -> p (k r)"), p_xT[:, 0:KC * R], ACT.Copy)\
                   .then_inc(xT_copied, 1)

            def products_out(t, u, i):
                act.wait_ge(h1_done, t + 1)
                act.wait_ge(h1_stored[i], 16 * (u + 1))
                act.activation(h1[i][:, :], p_h1[:, :], ACT.Copy).then_inc(h1_out, 1)
                act.wait_ge(v_done, t + 1 + 1)
                act.activation(V[:, ds(t, 1), :].rearrange("p a n -> p (a n)"), p_v[:, :], ACT.Copy)\
                   .then_inc(v_out, 1)
                act.wait_ge(h1_out, t + 1 + 1)
                act.dma_start(h1_dram[ds(t * R, R), :], h1[i][:, :]).then_inc(h1_stored[i], 16)

            def pair(u, last=False):
                for i in range(2):
                    if not (last and i == 1):
                        root(2 * u + i + 1)
                        copy_xT(2 * u + i + 1, 1 - i)
                    products_out(2 * u + i, u, i)

            root(0)
            act.wait_ge(xT_done, 1 + 1)
            act.activation(xT[0][:, :, :].rearrange("p k r -> p (k r)"), p_xT[:, 0:KC * R], ACT.Copy).then_inc(xT_copied, 1)
            with act.Fori(0, T // 2 - 1) as u:
                pair(u)
            pair(T // 2 - 1, last=True)
            for i in range(2):
                act.wait_ge(h1_stored[i], 16 * (T // 2 + 1))

        @block.tensor
        def _(pe):
            pe.wait_ge(wq_loaded, 16)

            def turn(t, i):
                pe.wait_ge(x_used, t + 1)
                pe.wait_ge(xT_copied, t + 1)
                for k in range(KC):
                    last = pe.transpose(p_xT[:, k * R:(k + 1) * R], xn[i][:, k * 128:(k + 1) * 128], ident[0:R, 0:R])
                last.then_inc(xT_done, 1)

            def pair(u, last=False):
                for i in range(2):
                    t = 2 * u + i
                    pe.wait_ge(xT_copied, t + 1 + 1)
                    pe.wait_ge(qk_out, t + 1)
                    for m in range(M):
                        for k in range(KC):
                            ins = pe.matmul(p_qk[:, m // 4, m % 4 * R:(m % 4 + 1) * R], WQKV[:, k, m * 128:(m + 1) * 128],
                                            xT[i][:, k, :], start=k == 0, stop=k == KC - 1)
                    ins.then_inc(qk_done, 1)
                    if not (last and i == 1):
                        turn(t + 1, 1 - i)
                    pe.wait_ge(w_loaded, 16)
                    pe.wait_ge(h1_out, t + 1)
                    for n in range(HC // BANK):
                        for k in range(KC):
                            ins = pe.matmul(p_h1[:, n * BANK:(n + 1) * BANK], xT[i][:, k, :],
                                            W1[:, k, n * BANK:(n + 1) * BANK], start=k == 0, stop=k == KC - 1)
                    ins.then_inc(h1_done, 1)
                    pe.wait_ge(wv_loaded, 16)
                    pe.wait_ge(v_out, t + 1)
                    for k in range(KC):
                        ins = pe.matmul(p_v[:, :], xT[i][:, k, :], WQKV[:, k, 2 * D:3 * D], start=k == 0, stop=k == KC - 1)
                    ins.then_inc(v_done, 1)

            turn(0, 0)
            with pe.Fori(0, T // 2 - 1) as u:
                pair(u)
            edges_on_tensor(pe)
            pair(T // 2 - 1, last=True)
            pe.wait_ge(watt_ready, 1)
            pe.wait_ge(xT_kept, T + 1)
            pe.wait_ge(h1_out, T + 1)
            pe.wait_ge(v_out, T + 1)
            for b, (c0, w) in enumerate(CB):
                for k in range(KC):
                    last = pe.matmul(p_row[b][:, 0:w], watt[:, k, :], xT_all[:, k, c0:c0 + w], start=k == 0, stop=k == KC - 1)
                last.then_inc(row_done, 1)
            pe.wait_ge(xT_copied, T + 1)
            pe.wait_ge(row_out, NB)
            for t in range(T):
                last = pe.transpose(p_col[:, t * 2 * H:(t + 1) * 2 * H], rows[:, t * R:(t + 1) * R], ident[0:2 * H, 0:2 * H])
            last.then_inc(col_done, 1)




def constants(nc, s, ident, identb):
    zeros_ready, ident_ready = s.sems.new("zeros_ready"), s.sems.new("ident_ready")
    with nc.Block() as block:
        @block.gpsimd
        def _(pool):
            pool.memset(ident[:, :], 0.0).then_inc(zeros_ready, 1)
            pool.memset(identb[:, :], 0.0).then_inc(zeros_ready, 1)
            pool.wait_ge(zeros_ready, 2)
            for m in (ident, identb):
                pool.affine_select(out=m[:, :], in_=m[:, :], compare_op=ALU.not_equal, fill=1.0, base=0,
                                   pattern=[[-1, 128]], channel_multiplier=1).then_inc(ident_ready, 1)
            pool.wait_ge(ident_ready, 2)


def attend_and_count(nc, s, cnt, x, gamma, beta, w_out, b_out, RB, CT, spare, ident, identb, rows_dram, mask_dram,
                     mix_dram, peaks):
    T, KC, H, D, N = s.T, s.KC, s.H, s.D, s.N
    M = 2 * D // 128
    C = D // H
    QK = RB[:, 0:M * N].rearrange("p (m n) -> p m n", m=M)
    V = RB[0:R, M * N:M * N + T * D].rearrange("p (t n) -> p t n", t=T)
    PAIRS = H // 2
    SCALE = float(C) ** -0.5
    GROUPS = ((0, 4), (4, 8), (8, T))
    UNITS = 2 * len(GROUPS)
    SLOTS = 4
    G, DIG, BASE = cnt.G, cnt.DIG, cnt.BASE
    PER = s.ET // T
    STEP = WIN // PAIRS
    HALF = T // 2
    RS = R + 1
    OH = RS + G * R
    with ExitStack() as ctx:
        def sb(name, shape, dt=F32):
            return ctx.enter_context(nc.sbuf_tensor(name, shape, dt))

        def ps(name, shape, dt=F32):
            return ctx.enter_context(nc.psum_tensor(name, shape, dt))

        sem = s.sems.new
        a_src = sb("a_src_rows_1", [R, H, N])
        WO = sb("w_out_sb", [128, KC, D])
        gcol, bcol = sb("mix_gamma", [128, KC]), sb("mix_beta", [128, KC])
        q = [sb(f"q_tile{i}", [128, R]) for i in range(2)]
        at = [[sb(f"relu_scores{i}{e}", [R, T, R]) for e in range(2)] for i in range(2)]
        o, on, oT = sb("mix_heads", [R, D]), sb("mix_normed", [R, D]), sb("mix_normed_T", [128, KC, R])
        y, xt = sb("mix_out", [R, D]), sb("mix_x", [R, D])
        junk = spare[0:R, 0:N // 2].bitcast(BF16)
        boutb = spare[0:R, N // 2:N // 2 + D]
        at_spare = N // 2 + D
        packed = spare[0:R, at_spare:at_spare + G * R].bitcast(I32)
        unpacked = spare[0:R, at_spare + G * R:at_spare + G * R + G * DIG * R].bitcast(I32)\
            .rearrange("p (g j c) -> p g j c", g=G, j=DIG)
        stat, mv = sb("mix_stat", [R, 6]), sb("mix_mv", [R, 2])
        ve, std, rstd, scratch = (sb(f"mix_{n}", [R, 1]) for n in ("var_eps", "std", "rstd", "scratch"))
        keyw = [sb(f"key_window{n}", [R, WIN]) for n in range(3)]
        at_spare += G * R + G * DIG * R
        onehot = [spare[0:R, c:c + OH // 2].bitcast(BF16) for c in range(at_spare, spare.shape[1] - OH // 2 + 1, OH // 2)]
        onehot += [sb(f"onehots{i}", [R, OH], BF16)[:, :] for i in range(2 * STEP - len(onehot))]
        oh_s, oh_d = [to[:, 0:R] for to in onehot], [to[:, RS:OH] for to in onehot]
        cb, mk = sb("counts_bf16", [R, T, R], BF16), sb("mask_rows", [R, N], BF16)
        peak = sb("peak_of_tile", [R, H])
        p_s = [ps(f"p_scores{i}", [R, BANK]) for i in range(SLOTS)]
        p_o, p_y, p_cnt = ps("p_heads", [R, BANK]), ps("p_mix_out", [128, BANK]), ps("p_counts", [R, BANK])
        p_m = ps("p_mask", [R, 2 * BANK], BF16)

        (loaded, q_ready, s_done, relu_done, pv_done, o_out, mvar, mstd, on_ready, oT_done, oT_out, y_done, y_out,
         stored, vec_chain, x_loaded, y_added, turns) = (sem(f"mix_{n}") for n in (
            "loaded", "q_ready", "scores_done", "relu_done", "pv_done", "heads_out", "var_ready", "std_ready", "normed",
            "normed_T_done", "normed_T_out", "y_done", "y_out", "stored", "vec_chain", "x_loaded", "x_added", "turns"))
        src_loaded, windows, oh_ready, used = (sem(n) for n in (
            "a_src1_loaded", "windows_ready", "onehots_ready", "onehots_used"))
        unpacked_ready, counts_out, cb_ready, maskT, mask_half, mask_ready, mask_stored, scored, count_chain = (sem(n) for n in (
            "unpacked_ready", "counts_out", "counts_bf16_ready", "mask_T_done", "mask_half_out", "mask_ready", "mask_stored",
            "mask_scored", "count_chain"))
        s.sems.begin_at(1, y_added, y_out, used, mask_ready)
        s.sems.begin_at(16, stored, mask_stored)
        block = ctx.enter_context(nc.Block())

        @block.sync
        def _(sp):
            sp.dma_start(WO[:, :, :], w_out.rearrange("(k p) n -> p k n", p=128)).then_inc(loaded, 16)
            sp.dma_start(boutb, b_out[None, :].to_broadcast([R, D])).then_inc(loaded, 16)
            with nc.allow_non_contiguous_dma(reason="two vectors, once"):
                sp.dma_start(gcol[:, :], gamma.rearrange("(k p) -> p k", p=128)).then_inc(loaded, 16)
                sp.dma_start(bcol[:, :], beta.rearrange("(k p) -> p k", p=128)).then_inc(loaded, 16)
            for h in range(H):
                sp.dma_start(a_src[:, h, :], rows_dram[h:h + 1, :].to_broadcast([R, N])).then_inc(src_loaded, 16)
            with sp.Fori(0, T) as t:
                sp.wait_ge(y_added, t + 1)
                sp.dma_start(xt[:, :], x[ds(t * R, R), :]).then_inc(x_loaded, 16)
                sp.wait_ge(mask_ready, t + 2)
                sp.dma_start(mask_dram[ds(t * R, R), :], mk[:, :]).then_inc(mask_stored, 16)
                sp.wait_ge(y_added, t + 2)
                sp.dma_start(mix_dram[ds(t * R, R), :], y[:, :]).then_inc(stored, 16)
            sp.wait_ge(stored, 16 * (T + 1))
            sp.wait_ge(mask_stored, 16 * (T + 1))

        @block.gpsimd
        def _(pool):
            def steps(t, first):
                for p in range(PAIRS):
                    if not (first and p == 0):
                        pool.wait_ge(s_done, (t * PAIRS + p - 1) * UNITS)
                    pool.tensor_copy(q[p % 2][:, :], QK[:, p, ds(t * R, R)]).then_inc(q_ready, 1)

            steps(0, True)
            with pool.Fori(1, T) as t:
                steps(t, False)

        @block.scalar
        def _(act):
            def root(t):
                act.wait_ge(mvar, t + 1)
                act.activation(std[:, :], ve[:, :], ACT.Sqrt).then_inc(mstd, 1)

            def scale_normed(t):
                act.wait_ge(loaded, 64)
                act.wait_ge(oT_done, t + 1)
                for k in range(KC):
                    act.activation(oT[:, k, :], p_y[:, k * R:(k + 1) * R], ACT.Identity,
                                   bias=bcol[:, k:k + 1], scale=gcol[:, k:k + 1]).then_inc(oT_out, 1)

            def keep_counts(t):
                act.wait_ge(unpacked_ready, t + 1)
                act.activation(CT[:, :, ds(t * R, R)], unpacked.rearrange("p g j c -> p (g j) c"), ACT.Copy,
                               accum_out=cnt.found[:, ds(t, 1)]).then_inc(counts_out, 1)

            def steps(t, first):
                for p in range(PAIRS):
                    n = t * PAIRS + p
                    for b, (j0, j1) in enumerate(GROUPS):
                        for e in range(2):
                            u = 2 * b + e
                            act.wait_ge(s_done, n * UNITS + u + 1)
                            if b == 0 and not (first and p < 2):
                                act.wait_ge(pv_done, 2 * (n - 2) + e + 1)
                            act.activation(at[p % 2][e][:, j0:j1, :].rearrange("p j r -> p (j r)"),
                                           p_s[(p * UNITS + u) % SLOTS][:, 0:(j1 - j0) * R], ACT.Relu, scale=SCALE)\
                               .then_inc(relu_done, 1)
                        if p == 1 and b == 0 and not first:
                            root(t - 1)
                    if p == 0 and not first:
                        keep_counts(t - 1)
                    if p == 1 and not first:
                        scale_normed(t - 1)

            steps(0, True)
            with act.Fori(1, T) as t:
                steps(t, False)
            keep_counts(T - 1)
            root(T - 1)
            scale_normed(T - 1)

        @block.vector
        def _(dve):
            mix, count = Chain(dve, vec_chain), Chain(dve, count_chain)
            NORM_LINKS, COUNT_LINKS = 8, 3 + H

            def heads_out(t, half):
                dve.wait_ge(pv_done, t * H + (half + 1) * H // 2)
                products = p_o[:, :].rearrange("p (q e w c) -> p q e w c", q=PAIRS // 2, e=2, w=2)
                to = o[:, half * D // 2:(half + 1) * D // 2].rearrange("p (q e c) -> p q e c", q=PAIRS // 2, e=2)
                for e in range(2):
                    ins = dve.tensor_copy(to[:, :, e, :], products[:, :, e, e, :])
                ins.then_inc(o_out, 1)

            def norm_tail(t):
                mix.at(t * NORM_LINKS)
                heads_out(t, 1)
                dve.wait_ge(o_out, 2 * t + 2)
                mix(dve.bn_stats(stat[:, :], o[:, :]))
                dve.sem_inc(turns, 1)
                mix(dve.bn_aggr(mv[:, :], stat[:, :]))
                mix(dve.tensor_scalar(ve[:, :], mv[:, 1:2], LN_EPS, None, ALU.add))
                dve.sem_inc(mvar, 1)
                one_over_sqrt(dve, mix, std[:, :], ve[:, :], rstd[:, :], mstd, t + 1, scratch[:, :])
                dve.tensor_scalar(on[:, :], o[:, :], mv[:, 0:1], rstd[:, 0:1], ALU.subtract, ALU.mult).then_inc(on_ready, 1)
                assert mix.n == NORM_LINKS

            def out_tail(t):
                dve.wait_ge(loaded, 64)
                dve.wait_ge(y_done, t + 1)
                dve.wait_ge(stored, 16 * (t + 1))
                dve.tensor_tensor(y[:, :], p_y[0:R, :], boutb, ALU.add).then_inc(y_out, 1)
                dve.wait_ge(x_loaded, 16 * (t + 1))
                dve.wait_ge(y_out, t + 2)
                dve.tensor_tensor(y[:, :], y[:, :], xt[:, :], ALU.add).then_inc(y_added, 1)

            def window(t, first=False):
                if not first:
                    dve.wait_ge(oh_ready, t * WIN)
                dve.tensor_scalar(keyw[0][:, :], cnt.keyp[:, ds(t * PER, WIN)], cnt.first[:, ds(t, 1)], None, ALU.subtract)
                dve.tensor_copy(keyw[1][:, :], cnt.lop[:, ds(t * PER, WIN)])
                dve.tensor_copy(keyw[2][:, :], cnt.wt[:, ds(t * PER, WIN)]).then_inc(windows, 1)
                dve.wait_ge(windows, t + 1)

            def onehots(t, p, first):
                for k in range(STEP):
                    i = p * STEP + k
                    b = i % (2 * STEP)
                    if not (first and p < 2):
                        dve.wait_ge(used, t * WIN + i + 1 - 2 * STEP + 1)
                    dve.tensor_scalar(oh_s[b], cnt.iota_s[:, :], keyw[1][:, i:i + 1], None, ALU.is_equal)
                    dve.tensor_scalar(oh_d[b], cnt.iota_d[:, :], keyw[0][:, i:i + 1], keyw[2][:, i:i + 1],
                                      ALU.is_equal, ALU.mult).then_inc(oh_ready, 1)

            def unpack(t):
                count.at(t * COUNT_LINKS)
                dve.wait_ge(used, (t + 1) * WIN + 1)
                dve.tensor_reduce(cnt.top[:, ds(t, 1)], p_cnt[:, 0:G * R], AX, ALU.max)
                count(dve.tensor_copy(packed, p_cnt[:, 0:G * R]))
                pk = packed.rearrange("p (g c) -> p g c", g=G)
                for j in range(DIG):
                    ins = dve.tensor_scalar(unpacked[:, :, j, :], pk, 4 * j, BASE - 1 if j < DIG - 1 else 0xffff,
                                            ALU.arith_shift_right, ALU.bitwise_and)
                ins.then_inc(unpacked_ready, 1)

            def self_loops(t):
                dve.wait_ge(counts_out, t + 1)
                own = CT[:, ds(t, 1), ds(t * R, R)].rearrange("p a r -> p (a r)")
                count(dve.tensor_tensor(own, own, ident[0:R, 0:R], ALU.add))
                dve.tensor_scalar(cb[:, :, :], CT[:, :, ds(t * R, R)], 1.0, None, ALU.min).then_inc(cb_ready, 1)

            def mask_part(t, half):
                dve.wait_ge(maskT, 2 * t + half + 1)
                if half == 0:
                    dve.wait_ge(mask_stored, 16 * (t + 1))
                ins = dve.tensor_scalar(mk[:, half * HALF * R:(half + 1) * HALF * R].rearrange("p (t r) -> p t r", r=R),
                                        p_m[:, 0:HALF * RS].rearrange("p (t r) -> p t r", r=RS)[:, :, 0:R], 1.0, BIG,
                                        ALU.subtract, ALU.mult)
                if half == 0:
                    ins.then_inc(mask_half, 1)
                else:
                    count(ins)
                    dve.sem_inc(mask_ready, 1)

            def see(t, h0, h1):
                for h in range(h0, h1):
                    dve.sem_inc(turns, 1)
                    count(dve.tensor_tensor_reduce(out=junk, in0=a_src[:, h, :], in1=mk[:, :], scale=1.0, scalar=-3.0e38,
                                                   op0=ALU.add, op1=ALU.max, accum_out=peak[:, h:h + 1]))
                if h1 == H:
                    dve.tensor_copy(peaks[:, ds(t, 1), :].rearrange("p a h -> p (a h)"), peak[:, :]).then_inc(scored, 1)

            def steps(t, first=False, last=False):
                if not first:
                    unpack(t - 1)
                onehots(t, 1, first)
                if not first:
                    norm_tail(t - 1)
                    self_loops(t - 1)
                onehots(t, 2, first)
                if not first:
                    mask_part(t - 1, 0)
                    mask_part(t - 1, 1)
                onehots(t, 3, first)
                if not first:
                    out_tail(t - 1)
                    see(t - 1, 0, H // 2)
                heads_out(t, 0)
                if not last:
                    window(t + 1)
                    onehots(t + 1, 0, False)
                if not first:
                    see(t - 1, H // 2, H)
                    assert count.n == COUNT_LINKS

            window(0, True)
            onehots(0, 0, True)
            steps(0, first=True)
            dve.wait_ge(src_loaded, 16 * H)
            with dve.Fori(1, T - 1) as t:
                steps(t)
            steps(T - 1, last=True)
            unpack(T - 1)
            self_loops(T - 1)
            norm_tail(T - 1)
            mask_part(T - 1, 0)
            mask_part(T - 1, 1)
            see(T - 1, 0, H)
            out_tail(T - 1)
            dve.wait_ge(scored, T)

        @block.tensor
        def _(pe):
            def scores(t, p, first):
                n = t * PAIRS + p
                pe.wait_ge(q_ready, n + 1)
                for b, (j0, j1) in enumerate(GROUPS):
                    if not (first and p * UNITS + 2 * b + 2 <= SLOTS):
                        pe.wait_ge(relu_done, n * UNITS + 2 * b + 2 - SLOTS)
                    for j in range(j0, j1):
                        for e in range(2):
                            last = pe.matmul(p_s[(p * UNITS + 2 * b + e) % SLOTS][:, (j - j0) * R:(j - j0 + 1) * R],
                                             QK[e * C:(e + 1) * C, M // 2 + p, j * R:(j + 1) * R],
                                             q[p % 2][e * C:(e + 1) * C, :], start=True, stop=True)
                            if j == j1 - 1:
                                last.then_inc(s_done, 1)

            def values(t, p):
                n = t * PAIRS + p
                pe.wait_ge(relu_done, (n + 1) * UNITS)
                if p % 2 == 0 and not (isinstance(t, int) and t == 0 and p == 0):
                    pe.wait_ge(o_out, 2 * t + p // 2)
                for e in range(2):
                    h = 2 * p + e
                    for j in range(T):
                        last = pe.matmul(p_o[:, h % 4 * 2 * C:(h % 4 + 1) * 2 * C], at[p % 2][e][:, j, :],
                                         V[:, j, 2 * p * C:(2 * p + 2) * C],
                                         start=j == 0, stop=j == T - 1)
                    last.then_inc(pv_done, 1)

            def counts(t, p):
                for k in range(STEP):
                    i = p * STEP + k
                    b = i % (2 * STEP)
                    pe.wait_ge(oh_ready, t * WIN + i + 1)
                    if p == 0 and k == 0 and not (isinstance(t, int) and t == 0):
                        pe.wait_ge(unpacked_ready, t)
                    pe.matmul(p_cnt[:, 0:G * R], oh_s[b], oh_d[b], start=p == 0 and k == 0,
                              stop=p == PAIRS - 1 and k == STEP - 1).then_inc(used, 1)

            def mask_T(t, half):
                pe.wait_ge(cb_ready, t + 1)
                if half == 0:
                    pe.wait_ge(mask_ready, t + 1)
                else:
                    pe.wait_ge(mask_half, t + 1)
                for j in range(HALF):
                    last = pe.transpose(p_m[:, j * RS:j * RS + R], cb[:, half * HALF + j, :], identb[0:R, 0:R])
                last.then_inc(maskT, 1)

            def normed_T(t):
                pe.wait_ge(on_ready, t + 1)
                pe.wait_ge(y_out, t + 1)
                for k in range(KC):
                    last = pe.transpose(p_y[:, k * R:(k + 1) * R], on[:, k * 128:(k + 1) * 128], ident[0:R, 0:R])
                last.then_inc(oT_done, 1)

            def out_product(t):
                pe.wait_ge(loaded, 64)
                pe.wait_ge(oT_out, KC * (t + 1))
                for k in range(KC):
                    last = pe.matmul(p_y[0:R, :], oT[:, k, :], WO[:, k, :], start=k == 0, stop=k == KC - 1)
                last.then_inc(y_done, 1)

            def steps(t, first):
                scores(t, 0, first)
                if not first:
                    values(t - 1, PAIRS - 1)
                counts(t, 0)
                scores(t, 1, first)
                counts(t, 1)
                values(t, 0)
                if not first:
                    mask_T(t - 1, 0)
                    normed_T(t - 1)
                scores(t, 2, first)
                if not first:
                    mask_T(t - 1, 1)
                    out_product(t - 1)
                counts(t, 2)
                values(t, 1)
                scores(t, 3, first)
                counts(t, 3)
                values(t, 2)

            steps(0, True)
            with pe.Fori(1, T) as t:
                steps(t, False)
            values(T - 1, PAIRS - 1)
            mask_T(T - 1, 0)
            normed_T(T - 1)
            mask_T(T - 1, 1)
            out_product(T - 1)


def verify_counts(nc, s, cnt):
    E = s.E
    with ExitStack() as ctx:
        def sb(name, shape, dt=F32):
            return ctx.enter_context(nc.sbuf_tensor(name, shape, dt))

        sem = s.sems.new
        tally, onec, wrong = sb("tally", [R, 2]), sb("ones_column", [R, 1]), sb("wrong", [1, 4])
        p_tal = ctx.enter_context(nc.psum_tensor("p_tally", [1, BANK], F32))
        tally_ready, tally_done, vec_chain = sem("tally_ready"), sem("tally_done"), sem("tally_chain")
        block = ctx.enter_context(nc.Block())

        @block.tensor
        def _(pe):
            pe.wait_ge(tally_ready, 1)
            pe.matmul(p_tal[:, 0:2], onec[:, :], tally[:, :], start=True, stop=True).then_inc(tally_done, 1)

        @block.vector
        def _(dve):
            link = Chain(dve, vec_chain)
            link(dve.memset(onec[:, :], 1.0))
            link(dve.tensor_scalar(cnt.top[:, :], cnt.top[:, :], float(cnt.BASE ** cnt.DIG), None, ALU.is_ge))
            link(dve.reduce_sum(tally[:, 0:1], cnt.found[:, :], AX))
            link(dve.reduce_sum(tally[:, 1:2], cnt.top[:, :], AX))
            dve.sem_inc(tally_ready, 1)
            dve.wait_ge(tally_done, 1)
            link(dve.tensor_scalar(wrong[:, 0:1], p_tal[:, 0:1], float(E), None, ALU.not_equal))
            link(dve.tensor_tensor(wrong[:, 1:2], wrong[:, 0:1], p_tal[:, 1:2], ALU.add))
            link(dve.tensor_scalar(wrong[:, 2:3], wrong[:, 1:2], 0.5, None, ALU.is_ge))
            link(dve.tensor_copy(cnt.wrong_i[:, :], wrong[:, 2:3]))


def general_path(nc, s, cnt, CT, ident, identb, rows_dram, mask_dram, peaks):
    T, ET, N = s.T, s.ET, s.N
    COLS = [(k * 4 * R, min(4 * R, (T - 4 * k) * R)) for k in range(3)]
    flag = cnt.wrong_i[0:1, 0:1]
    with ExitStack() as ctx:
        def sb(name, shape, dt=F32):
            return ctx.enter_context(nc.sbuf_tensor(name, shape, dt))

        sem = s.sems.new
        keyg = sb("general_window", [R, ET])
        oh_s = [sb(f"general_onehot_s{i}", [R, R], BF16) for i in range(2)]
        oh_g = [sb(f"general_onehot_d{i}", [R, T * R], BF16) for i in range(2)]
        iota32, iota_g = sb("iota32_general", [R, T * R], I32), sb("iota_general", [R, T * R], I16)
        zero = sb("zero_bf16", [R, BANK], BF16)
        onehot, used, done, out, key_ready, begun, iotas, pool_chain = (sem(f"general_{n}") for n in (
            "onehot_ready", "onehot_used", "counted", "out", "key_ready", "block_begun", "iota_ready", "pool_chain"))
        p = [ctx.enter_context(nc.psum_tensor(f"p_general{k}", [R, BANK], F32)) for k in range(3)]
        s.sems.begin_at(1, used, out)
        block = ctx.enter_context(nc.Block())

        def bracket(pe, start):
            for k, (c, w) in enumerate(COLS):
                last = pe.matmul(p[k][:, 0:w], zero[:, 0:R], zero[:, 0:w], start=start, stop=not start)
            return last

        @block.gpsimd
        def _(pool):
            def program():
                link = Chain(pool, pool_chain)
                link(pool.memset(zero[:, :], 0.0))
                link(pool.iota(iota32[:, :], [[cnt.TOFF, T], [1, R]], base=0, channel_multiplier=0))
                link(pool.tensor_copy(iota_g[:, :], iota32[:, :]))
                pool.sem_inc(iotas, 1)

            guarded(pool, flag, program)

        @block.tensor
        def _(pe):
            def program():
                pe.wait_ge(iotas, 1)
                with pe.Fori(0, T) as b:
                    pe.wait_ge(out, b + 1)
                    bracket(pe, True)
                    with pe.Fori(0, ET // 2) as v:
                        for i in range(2):
                            pe.wait_ge(onehot, b * ET + v * 2 + i + 1)
                            for k, (c, w) in enumerate(COLS):
                                last = pe.matmul(p[k][:, 0:w], oh_s[i][:, :], oh_g[i][:, c:c + w], start=False, stop=False)
                            last.then_inc(used, 1)
                    bracket(pe, False).then_inc(done, 1)

            guarded(pe, flag, program)

        @block.vector
        def _(dve):
            def program():
                dve.wait_ge(iotas, 1)
                with dve.Fori(0, T) as b:
                    dve.wait_ge(used, b * ET + 1)
                    dve.tensor_scalar(keyg[:, :], cnt.key3[:, :], cnt.first[:, ds(b, 1)], None, ALU.subtract).then_inc(key_ready, 1)
                    dve.wait_ge(key_ready, b + 1)
                    dve.sem_inc(begun, 1)
                    with dve.Fori(0, ET // 2) as v:
                        for i in range(2):
                            dve.wait_ge(used, b * ET + v * 2 + 1)
                            dve.tensor_scalar(oh_s[i][:, :], cnt.iota_s[:, :], cnt.lop[:, ds(v * 2 + i + MARGIN, 1)], None,
                                              ALU.is_equal)
                            dve.tensor_scalar(oh_g[i][:, :], iota_g[:, :], keyg[:, ds(v * 2 + i, 1)], None, ALU.is_equal)\
                               .then_inc(onehot, 1)
                    dve.wait_ge(done, b + 1)
                    for k, (c, w) in enumerate(COLS):
                        ins = dve.tensor_copy(CT[:, 4 * k:4 * k + w // R, ds(b * R, R)],
                                              p[k][:, 0:w].rearrange("p (t r) -> p t r", r=R))
                    ins.then_inc(out, 1)

            guarded(dve, flag, program)

    with ExitStack() as ctx:
        sem = s.sems.new
        PB = 1024
        RS = R + 1
        cb = [ctx.enter_context(nc.sbuf_tensor(f"general_counts_bf16_{i}", [R, T, R], BF16)) for i in range(2)]
        mk = [ctx.enter_context(nc.sbuf_tensor(f"general_mask_{i}", [R, N], BF16)) for i in range(2)]
        loops_ready, cb_ready, ct_done, mask_ready = (sem(f"general_{n}") for n in (
            "loops_ready", "cb_ready", "ct_done", "mask_ready"))
        mask_stored = [sem(f"general_mask_stored{i}") for i in range(2)]
        p_t = [ctx.enter_context(nc.psum_tensor(f"p_general_mask{i}", [R, 2, PB], BF16)) for i in range(2)]
        s.sems.begin_at(1, ct_done, mask_ready)
        s.sems.begin_at(16, *mask_stored)
        block = ctx.enter_context(nc.Block())

        @block.vector
        def _(dve):
            def program():
                for t in range(T):
                    dve.tensor_tensor(CT[:, t, t * R:(t + 1) * R], CT[:, t, t * R:(t + 1) * R], ident[0:R, 0:R], ALU.add)\
                       .then_inc(loops_ready, 1)
                dve.wait_ge(loops_ready, T)
                dve.sem_inc(loops_ready, 1)
                with dve.Fori(0, T // 2) as u:
                    for i in range(2):
                        b = 2 * u + i
                        dve.wait_ge(ct_done, b + 1)
                        dve.tensor_scalar(cb[i][:, :, :], CT[:, :, ds(b * R, R)], 1.0, None, ALU.min).then_inc(cb_ready, 1)
                        dve.wait_ge(ct_done, b + 2)
                        dve.wait_ge(mask_stored[i], 16 * u + 16)
                        for h, (t0, t1) in enumerate(((0, 8), (8, T))):
                            ins = dve.tensor_scalar(mk[i][:, t0 * R:t1 * R].rearrange("p (t r) -> p t r", r=R),
                                                    p_t[i][:, h, 0:(t1 - t0) * RS].rearrange("p (t r) -> p t r", r=RS)[:, :, 0:R],
                                                    1.0, BIG, ALU.subtract, ALU.mult)
                        ins.then_inc(mask_ready, 1)

            guarded(dve, flag, program)

        @block.tensor
        def _(pe):
            def program():
                with pe.Fori(0, T // 2) as u:
                    for i in range(2):
                        b = 2 * u + i
                        pe.wait_ge(cb_ready, b + 1)
                        pe.wait_ge(mask_ready, b + 1)
                        for t in range(T):
                            last = pe.transpose(p_t[i][:, t // 8, t % 8 * RS:t % 8 * RS + R], cb[i][:, t, :], identb[0:R, 0:R])
                        last.then_inc(ct_done, 1)

            guarded(pe, flag, program)

        @block.sync
        def _(sp):
            def program():
                with sp.Fori(0, T // 2) as u:
                    for i in range(2):
                        sp.wait_ge(mask_ready, 2 * u + i + 2)
                        sp.dma_start(mask_dram[ds((2 * u + i) * R, R), :], mk[i][:, :]).then_inc(mask_stored[i], 16)
                for i in range(2):
                    sp.wait_ge(mask_stored[i], 16 * (T // 2) + 16)

            guarded(sp, flag, program)

    see_sources(nc, s, "general", rows_dram, mask_dram, peaks, flag)


def see_sources(nc, s, name, rows_dram, mask_dram, peaks, flag=None, beside=None):
    T, H, N = s.T, s.H, s.N
    with ExitStack() as ctx:
        sem = s.sems.new
        a_src = ctx.enter_context(nc.sbuf_tensor(f"a_src_rows_{name}", [R, H, N], F32))
        mask = [ctx.enter_context(nc.sbuf_tensor(f"mask_{name}{i}", [R, N], BF16)) for i in range(2)]
        peak = [ctx.enter_context(nc.sbuf_tensor(f"peak_{name}{i}", [R, H], F32)) for i in range(2)]
        junk = [ctx.enter_context(nc.sbuf_tensor(f"masked_{name}{i}", [R, N], BF16)) for i in range(2)]
        src_loaded = [sem(f"a_src_loaded_{name}{h}") for h in range(H)]
        mask_loaded = [sem(f"mask_loaded_{name}{i}") for i in range(2)]
        seen, kept, turns, reduced = (sem(f"{n}_{name}") for n in ("seen", "kept", "turns", "reduced"))
        s.sems.begin_at(2, seen)
        block = ctx.enter_context(nc.Block())
        if beside:
            beside(ctx, block)

        @block.sync
        def _(sp):
            def program():
                def load(t, i):
                    sp.wait_ge(seen, t + 1)
                    sp.dma_start(mask[i][:, :], mask_dram[ds(t * R, R), :]).then_inc(mask_loaded[i], 16)

                sp.dma_start(a_src[:, 0, :], rows_dram[0:1, :].to_broadcast([R, N])).then_inc(src_loaded[0], 16)
                for i in range(2):
                    load(i, i)
                for h in range(1, H):
                    sp.dma_start(a_src[:, h, :], rows_dram[h:h + 1, :].to_broadcast([R, N])).then_inc(src_loaded[h], 16)
                with sp.Fori(1, T // 2) as u:
                    for i in range(2):
                        load(2 * u + i, i)

            guarded(sp, flag, program)

        @block.vector
        def _(dve):
            def tile(t, u, i, first):
                dve.wait_ge(mask_loaded[i], 16 * (u + 1))
                for h in range(H):
                    if first:
                        dve.wait_ge(src_loaded[h], 16)
                    if not (first and h < 2):
                        dve.wait_ge(reduced, t * H + h - 1)
                    dve.sem_inc(turns, 1)
                    dve.tensor_tensor_reduce(out=junk[h % 2][:, :], in0=a_src[:, h, :], in1=mask[i][:, :], scale=1.0,
                                             scalar=-3.0e38, op0=ALU.add, op1=ALU.max, accum_out=peak[i][:, h:h + 1])\
                       .then_inc(reduced, 1)
                dve.wait_ge(reduced, (t + 1) * H)
                dve.sem_inc(seen, 1)
                dve.tensor_copy(peaks[:, ds(t, 1), :].rearrange("p a h -> p (a h)"), peak[i][:, :]).then_inc(kept, 1)

            def program():
                for i in range(2):
                    tile(i, 0, i, i == 0)
                with dve.Fori(1, T // 2) as u:
                    for i in range(2):
                        tile(2 * u + i, u, i, False)
                dve.wait_ge(kept, T)

            guarded(dve, flag, program)


def shifts(nc, s, layer, peaks, adcol, ident, as8, as2, shift_dram):
    T, H, N = s.T, s.H, s.N
    with ExitStack() as ctx:
        z, nm = (ctx.enter_context(nc.sbuf_tensor(f"{n}_{layer}", [R, T, H], F32)) for n in ("peak_score", "neg_max"))
        cols = ctx.enter_context(nc.sbuf_tensor(f"shift_columns_{layer}", [R, T, H, 3], F32))
        rows = ctx.enter_context(nc.sbuf_tensor(f"shift_rows_{layer}", [3 * H, N], F32))
        p_row = [ctx.enter_context(nc.psum_tensor(f"p_shift_rows{b}_{layer}", [3 * H, BANK], F32)) for b in range(3)]
        cols_ready, rows_done, rows_out, stored, chain = (s.sems.new(f"{n}_{layer}") for n in (
            "shift_columns_ready", "shift_rows_done", "shift_rows_out", "shift_rows_stored", "shift_chain"))
        block = ctx.enter_context(nc.Block())

        @block.vector
        def _(dve):
            link = Chain(dve, chain)
            a, b = adcol[:, :, 0:H], adcol[:, :, H:2 * H]
            link(dve.scalar_tensor_tensor(z[:, :, :], peaks[:, :, :], -1.0, b, ALU.mult, ALU.subtract))
            link(dve.scalar_tensor_tensor(nm[:, :, :], z[:, :, :], SLOPE, z[:, :, :], ALU.mult, ALU.min))
            link(dve.tensor_tensor(cols[:, :, :, 0], b, nm[:, :, :], ALU.add))
            link(dve.scalar_tensor_tensor(cols[:, :, :, 1], b, SLOPE, nm[:, :, :], ALU.mult, ALU.add))
            link(dve.tensor_scalar(cols[:, :, :, 2], b, 1.0 - SLOPE, None, ALU.mult))
            dve.sem_inc(cols_ready, 1)
            link(dve.tensor_scalar(as8[:, :, :], a, 1.0 - SLOPE, None, ALU.mult))
            link(dve.tensor_scalar(as2[:, :, :], a, SLOPE, None, ALU.mult))
            for b in range(3):
                dve.wait_ge(rows_done, b + 1)
                w = (min(4 * b + 4, T) - 4 * b) * R
                dve.tensor_copy(rows[:, 4 * b * R:4 * b * R + w], p_row[b][:, 0:w]).then_inc(rows_out, 1)

        @block.tensor
        def _(pe):
            pe.wait_ge(cols_ready, 1)
            for t in range(T):
                last = pe.transpose(p_row[t // 4][:, t % 4 * R:(t % 4 + 1) * R], cols[:, t, :, :].rearrange("p h q -> p (h q)"),
                                    ident[0:R, 0:R])
                if t % 4 == 3 or t == T - 1:
                    last.then_inc(rows_done, 1)

        @block.sync
        def _(sp):
            sp.wait_ge(rows_out, 3)
            sp.dma_start(shift_dram.rearrange("h (q n) -> (h q) n", q=3), rows[:, :]).then_inc(stored, 16)
            sp.wait_ge(stored, 16)


def log_counts(nc, s, CT, L, h1_dram, h1, h1_loaded):
    T, H, C1, N = s.T, s.H, s.C1, s.N
    with ExitStack() as ctx:
        logs = [ctx.enter_context(nc.sbuf_tensor(f"count_logs_raw{i}", [R, N], F32)) for i in range(2)]
        tiny = ctx.enter_context(nc.sbuf_tensor("tiny", [R, 1], F32))
        tiny_ready, logs_ready, L_ready = (s.sems.new(n) for n in ("tiny_ready", "count_logs_ready", "count_logs_kept"))
        block = ctx.enter_context(nc.Block())

        @block.sync
        def _(sp):
            for t in range(T):
                sp.dma_start(h1[:, t, :, 0:C1], h1_dram[t * R:(t + 1) * R, :].rearrange("r (h c) -> r h c", h=H))\
                  .then_inc(h1_loaded, 16)

        @block.vector
        def _(dve):
            dve.memset(tiny[:, :], 1.0e-30).then_inc(tiny_ready, 1)
            for t in range(T):
                dve.wait_ge(logs_ready, t + 1)
                dve.scalar_tensor_tensor(L[:, t, :], logs[t % 2][:, :], BIG, logs[t % 2][:, :], ALU.mult, ALU.min)\
                   .then_inc(L_ready, 1)
            dve.wait_ge(L_ready, T)

        @block.scalar
        def _(act):
            act.wait_ge(tiny_ready, 1)
            for t in range(T):
                if t >= 2:
                    act.wait_ge(L_ready, t - 1)
                act.activation(logs[t % 2][:, :], CT[:, t, :], ACT.Ln, bias=tiny[:, 0:1]).then_inc(logs_ready, 1)


def gat_sums(nc, s, layer, C, haug, values_loaded, result_of, as8, as2, shift_dram, L, work):
    T, N, H = s.T, s.N, s.H
    PAIRS = H // 2
    W = C + 1
    BOTH = 2 * W <= BANK // 3
    OW = 2 * W if BOTH else W
    PB = BANK // OW
    NB = -(-T // PB)
    BY_VECTOR = (0, 2, 5, 8)
    BY_OTHERS = tuple(j for j in range(T) if j not in BY_VECTOR)
    NX, NY = len(BY_VECTOR), len(BY_OTHERS)
    WARM_UP = 36
    LA = 4
    banks = [(b * PB, min(T, (b + 1) * PB)) for b in range(NB)]
    p = [work[0:R, j * N:(j + 1) * N] for j in range(T)]
    with ExitStack() as ctx:
        def sb(name, shape, dt=F32):
            return ctx.enter_context(nc.sbuf_tensor(f"{name}_{layer}", shape, dt))

        def sem(name):
            return s.sems.new(f"{name}_{layer}")

        rows = [sb(f"shift_rows_all{i}", [R, 3, N]) for i in range(2)]
        zero = sb("zero", [R, BANK], BF16)
        total, inv = sb("total", [R, T]), sb("inv_total", [R, T])
        p_o = [[ctx.enter_context(nc.psum_tensor(f"p_sums{i}{b}_{layer}", [R, BANK], F32)) for b in range(NB)] for i in range(2)]
        rows_loaded = [sem(f"rows_loaded{i}") for i in range(2)]
        (ones_ready, by_vector, relus, by_others, logits, weights, used, sums_out,
         evac_chain) = (sem(n) for n in (
            "ones_ready", "exponents_by_vector", "relus_ready", "exponents_by_others", "logits_ready",
            "weights_ready", "weights_used", "sums_out", "evac_chain"))
        s.sems.begin_at(T, used)
        s.sems.begin_at(2, sums_out)
        block = ctx.enter_context(nc.Block())

        def term(i, q):
            return rows[i][:, q, :]

        @block.sync
        def _(sp):
            def load(h, i):
                sp.dma_start(rows[i][:, :, :].rearrange("p q n -> p (q n)"), shift_dram[ds(h, 1), :].to_broadcast([R, 3 * N]))\
                  .then_inc(rows_loaded[i], 16)

            for i in range(2):
                load(i, i)
            with sp.Fori(1, PAIRS) as u:
                for i in range(2):
                    sp.wait_ge(logits, (2 * u + i - 1) * T)
                    load(2 * u + i, i)

        @block.vector
        def _(dve):
            link = Chain(dve, evac_chain)
            LINKS = NB + 1

            def exponents(u, i, j):
                h = 2 * u + i
                if j == BY_VECTOR[0]:
                    dve.wait_ge(rows_loaded[i], 16 * (u + 1))
                dve.wait_ge(used, h * T + j + 1)
                dve.scalar_tensor_tensor(p[j], term(i, 0), as8[:, j, ds(h, 1)], term(i, 1), ALU.add, ALU.max)\
                   .then_inc(by_vector, 1)

            def plus_log_count(h, j):
                if j in BY_VECTOR:
                    dve.wait_ge(by_vector, h * NX + BY_VECTOR.index(j) + 1)
                else:
                    dve.wait_ge(by_others, h * NY + BY_OTHERS.index(j) + 1)
                dve.tensor_tensor(p[j], p[j], L[:, j, :], ALU.add).then_inc(logits, 1)

            def result(h, i):
                link.at(h * LINKS)
                own = i * W if BOTH else 0
                dve.wait_ge(used, (h + 2) * T)
                for b, (d0, d1) in enumerate(banks):
                    sums = p_o[i][b][:, 0:(d1 - d0) * OW].rearrange("p (d w) -> p d w", w=OW)[:, :, own:own + W]
                    link(dve.tensor_scalar(total[:, d0:d1], sums[:, :, C], 1e-16, None, ALU.add))
                link(dve.reciprocal(inv[:, :], total[:, :]))
                for b, (d0, d1) in enumerate(banks):
                    sums = p_o[i][b][:, 0:(d1 - d0) * OW].rearrange("p (d w) -> p d w", w=OW)[:, :, own:own + W]
                    ins = dve.tensor_tensor(result_of(d0, d1, h), sums[:, :, 0:C],
                                            inv[:, d0:d1, None].to_broadcast([R, d1 - d0, C]), ALU.mult)
                ins.then_inc(sums_out, 1)
                assert link.n == LINKS

            def pair(u, first=False, last=False):
                for i in range(2):
                    for j in range(T):
                        if j + LA < T:
                            if j + LA in BY_VECTOR:
                                exponents(u, i, j + LA)
                        elif j + LA - T in BY_VECTOR and not (last and i == 1):
                            exponents(u + i, 1 - i, j + LA - T)
                        plus_log_count(2 * u + i, j)
                        if j == 3 and not (first and i == 0):
                            result(2 * u + i - 1, 1 - i)

            dve.memset(haug[:, :, :, C:W], 1.0)
            dve.memset(zero[:, :], 0.0).then_inc(ones_ready, 1)
            for j in BY_VECTOR:
                if j < LA:
                    exponents(0, 0, j)
            pair(0, first=True)
            with dve.Fori(1, PAIRS - 1) as u:
                pair(u)
            pair(PAIRS - 1, last=True)
            result(H - 1, 1)
            dve.wait_ge(sums_out, H + 2)

        @block.scalar
        def _(act):
            def relu(u, i, j):
                h = 2 * u + i
                if j == BY_OTHERS[0]:
                    act.wait_ge(rows_loaded[i], 16 * (u + 1))
                act.wait_ge(used, h * T + j + 1)
                act.activation(p[j], term(i, 2), ACT.Relu, bias=as8[:, j, ds(h, 1)]).then_inc(relus, 1)

            def exp(h, j):
                act.wait_ge(logits, h * T + j + 1)
                act.activation(p[j], p[j], ACT.Exp, bias=as2[:, j, ds(h, 1)]).then_inc(weights, 1)

            def pair(u, last=False):
                for i in range(2):
                    for j in range(T):
                        if j + LA < T:
                            if j + LA in BY_OTHERS:
                                relu(u, i, j + LA)
                        elif j + LA - T in BY_OTHERS and not (last and i == 1):
                            relu(u + i, 1 - i, j + LA - T)
                        exp(2 * u + i, j)

            for j in BY_OTHERS:
                if j < LA:
                    relu(0, 0, j)
            with act.Fori(0, PAIRS - 1) as u:
                pair(u)
            pair(PAIRS - 1, last=True)

        @block.gpsimd
        def _(pool):
            with pool.Fori(0, PAIRS) as u:
                for i in range(2):
                    pool.wait_ge(rows_loaded[i], 16 * (u + 1))
                    for k, j in enumerate(BY_OTHERS):
                        pool.wait_ge(relus, (2 * u + i) * NY + k + 1)
                        pool.tensor_tensor(p[j], p[j], term(i, 1), ALU.add).then_inc(by_others, 1)

        @block.tensor
        def _(pe):
            pe.wait_ge(ones_ready, 1)
            if values_loaded is not None:
                pe.wait_ge(values_loaded, 16 * T)
            for _ in range(WARM_UP):
                pe.matmul(p_o[0][0][:, :], zero[:, 0:R], zero[:, :], start=True, stop=True)
            with pe.Fori(0, PAIRS) as u:
                for i in range(2):
                    h = 2 * u + i
                    pe.wait_ge(sums_out, h + 1)
                    for j in range(T):
                        pe.wait_ge(weights, h * T + j + 1)
                        values = haug[:, j, ds(2 * u, 2) if BOTH else ds(h, 1), :]
                        for d in range(T):
                            last = pe.matmul(p_o[i][d // PB][:, d % PB * OW:(d % PB + 1) * OW], p[j][:, d * R:(d + 1) * R],
                                             values.rearrange("p a w -> p (a w)"), start=j == 0 and d % PB == 0,
                                             stop=j == T - 1 and (d % PB == PB - 1 or d == T - 1))
                        last.then_inc(used, 1)


def second_scores(nc, s, h1, b1, w2att, work, ident, adcol, rows_dram):
    T, H, N, C1, HC = s.T, s.H, s.N, s.C1, s.HC
    K = HC // 128
    hT = work[:, 0:K * N].rearrange("p (k n) -> p k n", k=K)
    CB = [(4 * b * R, (min(4 * b + 4, T) - 4 * b) * R) for b in range(3)]
    with ExitStack() as ctx:
        b1c = ctx.enter_context(nc.sbuf_tensor("b1_columns", [128, K], F32))
        rows = ctx.enter_context(nc.sbuf_tensor("att2_rows_sb", [2 * H, N], F32))
        p_t = [[ctx.enter_context(nc.psum_tensor(f"p_h1_T{i}{b}", [128, BANK], F32)) for b in range(3)] for i in range(2)]
        p_c = ctx.enter_context(nc.psum_tensor("p_att2_columns", [R, T * 2 * H], F32))
        loaded, T_done, T_vec, T_act, row_done, row_out, col_done, col_out, stored = (s.sems.new(f"second_{n}") for n in (
            "loaded", "T_done", "T_out_by_vector", "T_out_by_scalar", "row_done", "row_out", "columns_done", "columns_out",
            "rows_stored"))
        block = ctx.enter_context(nc.Block())

        @block.sync
        def _(sp):
            with nc.allow_non_contiguous_dma(reason="one short vector, once"):
                sp.dma_start(b1c[:, :], b1.rearrange("(k p) -> p k", p=128)).then_inc(loaded, 16)
            sp.wait_ge(row_out, 3)
            sp.dma_start(rows_dram, rows[0:H, :]).then_inc(stored, 16)
            sp.wait_ge(stored, 16)

        @block.tensor
        def _(pe):
            for k in range(K):
                if k >= 2:
                    pe.wait_ge(T_act, k - 1)
                    pe.wait_ge(T_vec, k - 1)
                for t in range(T):
                    last = pe.transpose(p_t[k % 2][t // 4][:, t % 4 * R:(t % 4 + 1) * R], h1[:, t, k, 0:C1], ident[0:R, 0:R])
                last.then_inc(T_done, 1)
            pe.wait_ge(T_act, K)
            pe.wait_ge(T_vec, K)
            for b, (c0, w) in enumerate(CB):
                for k in range(K):
                    last = pe.matmul(p_t[0][b][0:2 * H, 0:w], w2att[:, k, :], hT[:, k, c0:c0 + w], start=k == 0, stop=k == K - 1)
                last.then_inc(row_done, 1)
            pe.wait_ge(row_out, 3)
            for t in range(T):
                last = pe.transpose(p_c[:, t * 2 * H:(t + 1) * 2 * H], rows[:, t * R:(t + 1) * R], ident[0:2 * H, 0:2 * H])
            last.then_inc(col_done, 1)

        @block.scalar
        def _(act):
            act.wait_ge(loaded, 16)
            for k in range(K):
                act.wait_ge(T_done, k + 1)
                (c0, w), (c2, w2) = CB[0], CB[2]
                act.activation(hT[:, k, c0:c0 + w], p_t[k % 2][0][:, 0:w], ACT.Relu, bias=b1c[:, k:k + 1])
                act.activation(hT[:, k, c2:c2 + w2], p_t[k % 2][2][:, 0:w2], ACT.Relu, bias=b1c[:, k:k + 1]).then_inc(T_act, 1)

        @block.vector
        def _(dve):
            dve.wait_ge(loaded, 16)
            c1, w = CB[1]
            for k in range(K):
                dve.wait_ge(T_done, k + 1)
                dve.tensor_scalar(hT[:, k, c1:c1 + w], p_t[k % 2][1][:, 0:w], b1c[:, k:k + 1], 0.0, ALU.add, ALU.max)\
                   .then_inc(T_vec, 1)
            for b, (c0, w) in enumerate(CB):
                dve.wait_ge(row_done, b + 1)
                dve.tensor_copy(rows[:, c0:c0 + w], p_t[0][b][0:2 * H, 0:w]).then_inc(row_out, 1)
            dve.wait_ge(col_done, 1)
            dve.tensor_copy(adcol[:, :, :], p_c[:, :].rearrange("p (t h) -> p t h", t=T)).then_inc(col_out, 1)
            dve.wait_ge(col_out, 1)


def second_values(nc, s, w2, w2_sb, work, haug):
    T, H, N, C2, K = s.T, s.H, s.N, s.C2, s.HC // 128
    D2 = H * C2
    hT = work[:, 0:K * N].rearrange("p (k n) -> p k n", k=K)

    def beside(ctx, block):
        p_h = [ctx.enter_context(nc.psum_tensor(f"p_h2_{i}", [R, BANK], F32)) for i in range(2)]
        w2_loaded, h2_done, h2_out = s.sems.new("w2_loaded"), s.sems.new("h2_done"), s.sems.new("h2_out")

        @block.scalar
        def _(act):
            act.dma_start(w2_sb, w2.rearrange("(k p) n -> p k n", p=128)).then_inc(w2_loaded, 16)
            for t in range(T):
                act.wait_ge(h2_done, t + 1)
                act.activation(haug[:, t, :, 0:C2], p_h[t % 2][:, 0:D2].rearrange("p (h c) -> p h c", h=H), ACT.Copy)\
                   .then_inc(h2_out, 1)
            act.wait_ge(h2_out, T)

        @block.tensor
        def _(pe):
            pe.wait_ge(w2_loaded, 16)
            for t in range(T):
                if t >= 2:
                    pe.wait_ge(h2_out, t - 1)
                for k in range(K):
                    last = pe.matmul(p_h[t % 2][:, 0:D2], hT[:, k, t * R:(t + 1) * R], w2_sb[:, k, :], start=k == 0, stop=k == K - 1)
                last.then_inc(h2_done, 1)

    return beside




def residual_and_ffn(nc, s, x1, gnn_bias, mix_dram, router_w, w1, b1, w2, b2, ident, out):
    T, D, KC, N, NE, F = s.T, s.D, s.KC, s.N, s.NE, s.F
    KF = F // 128
    CB = [(k * BANK, min(N - k * BANK, BANK)) for k in range(3)]
    with ExitStack() as ctx:
        def sb(name, shape, dt=F32):
            return ctx.enter_context(nc.sbuf_tensor(f"ffn_{name}", shape, dt))

        def ps(name, shape, dt=F32):
            return ctx.enter_context(nc.psum_tensor(f"p_ffn_{name}", shape, dt))

        def sem(name):
            return s.sems.new(f"ffn_{name}")

        gnn_bias_rows, mix = sb("gnn_bias_rows", [R, D]), sb("x_plus_mix", [R, T, D])
        junk = [sb(f"log_softmax_exps{i}", [R, D]) for i in range(2)]
        ls_peak, ls_neg_peak, ls_sums, ls_logs = (sb(f"log_softmax_{n}", [R, T]) for n in ("peak", "neg_peak", "sums", "logs"))
        r_raw, w1_raw, w2_raw = sb("router", [NE, D]), sb("w1", [128, KF, D]), sb("w2", [128, KC, F])
        rT, w1T, w2T = sb("router_T", [128, KC, NE]), sb("w1_T", [128, KC, F]), sb("w2_T", [128, KF, D])
        b1c, b2b = sb("b1", [128, KF]), sb("b2", [R, D])
        xn = [sb(f"xn{i}", [R, D]) for i in range(2)]
        xT = [sb(f"xT{i}", [128, KC, R]) for i in range(2)]
        xT_all, hT = sb("xT_all", [128, KC, N]), sb("hT", [128, KF, N])
        stat, mv = sb("stat", [R, T, 6]), sb("mean_var", [R, T, 2])
        ve, std, rstd, scratch = (sb(n, [R, T]) for n in ("var_eps", "std", "rstd", "scratch"))
        logits, probs, sel, kept = (sb(n, [R, T, NE]) for n in ("logits", "probs", "chosen", "kept"))
        one = sb("one_chosen", [R, T, NE])
        selb = sb("chosen_bf16", [R, T, NE], BF16)
        peak, total, inv, gate = (sb(n, [R, T]) for n in ("peak", "total", "inv_total", "gate"))
        best = sb("best", [R, T, 8])
        best_i = sb("best_index", [R, T, 8], U32)
        best_f = sb("best_index_f", [R, T, 2])
        iota_i, iota_e = sb("iota_i", [R, NE], I32), sb("iota_e", [R, NE])
        upper, onesb = sb("earlier", [R, R], BF16), sb("ones_bf16", [R, R], BF16)
        yb = sb("y_plus_b2", [R, D])
        fin = [sb(f"result{i}", [R, D]) for i in range(2)]
        p_w = [ps(f"weights{i}", [128, BANK]) for i in range(2)]
        p_l = ps("logits", [R, BANK])
        p_h = [ps(f"h{i}", [128, BANK]) for i in range(2)]
        p_x = p_h
        p_y = [ps(f"y{i}", [R, BANK]) for i in range(2)]

        (loaded, wT_done, wT_out, var_ready, std_ready, xn_ready, xT_done, xT_out, xT_kept, logits_done, logits_out,
         shifted, exps, consts, chosen, pos_done, h_done, h_out, y_done, y_out, fin_ready, chain, pool_chain) = (sem(n) for n in (
            "loaded", "wT_done", "wT_out", "var_ready", "std_ready", "xn_ready", "xT_done", "xT_out", "xT_kept",
            "logits_done", "logits_out", "logits_shifted", "exps_ready", "constants_ready", "chosen_ready", "positions_done",
            "h_done", "h_out", "y_done", "y_out", "result_ready", "vec_chain", "pool_chain"))
        stored = [sem(f"stored{i}") for i in range(2)]
        summed, x1_ready = sem("summed"), sem("x1_ready")
        gnn_bias_loaded, mix_loaded, ls_peak_ready, ls_exps_done, ls_logs_ready = (sem(n) for n in (
            "gnn_bias_loaded", "mix_loaded", "log_softmax_peak_ready", "log_softmax_exps_done", "log_softmax_logs_ready"))
        TURNS = ([[(rT[:, k, :], r_raw[:, k * 128:(k + 1) * 128], NE) for k in range(KC)]]
                 + [[(w1T[:, k, f * 128:(f + 1) * 128], w1_raw[:, f, k * 128:(k + 1) * 128], 128) for k in range(KC)]
                    for f in range(KF)]
                 + [[(w2T[:, f, k * 128:(k + 1) * 128], w2_raw[:, k, f * 128:(f + 1) * 128], 128) for k in range(KC)]
                    for f in range(KF)])
        s.sems.begin_at(1, logits_out)
        s.sems.begin_at(2, xT_done, xT_out, xT_kept, logits_done)
        block = ctx.enter_context(nc.Block())

        @block.sync
        def _(sp):
            sp.dma_start(gnn_bias_rows[:, :], gnn_bias[None, :].to_broadcast([R, D])).then_inc(gnn_bias_loaded, 16)
            with nc.allow_non_contiguous_dma(reason="one short vector, once"):
                sp.dma_start(b1c[:, :], b1.rearrange("(f p) -> p f", p=128)).then_inc(loaded, 16)
            sp.dma_start(b2b[:, :], b2[None, :].to_broadcast([R, D])).then_inc(loaded, 16)
            sp.wait_ge(loaded, 16 * 5)
            for t in range(T):
                sp.dma_start(mix[:, t, :], mix_dram[t * R:(t + 1) * R, :]).then_inc(mix_loaded, 16)
            for t in range(T):
                sp.wait_ge(fin_ready, t + 1)
                sp.dma_start(out[t * R:(t + 1) * R, :], fin[t % 2][:, :]).then_inc(stored[t % 2], 16)
            for i in range(2):
                sp.wait_ge(stored[i], 16 * (T // 2))

        @block.gpsimd
        def _(pool):
            link = Chain(pool, pool_chain)
            link(pool.iota(iota_i[:, :], [[1, NE]], base=0, channel_multiplier=0))
            link(pool.tensor_copy(iota_e[:, :], iota_i[:, :]))
            link(pool.memset(onesb[:, :], 1.0))
            link(pool.affine_select(out=upper[:, :], in_=onesb[:, :], compare_op=ALU.is_gt, fill=0.0, base=0,
                                    pattern=[[1, R]], channel_multiplier=-1))
            pool.sem_inc(consts, 1)
            pool.wait_ge(ls_logs_ready, 1)
            pool.wait_ge(xn_ready, T)
            for t in range(T):
                pool.tensor_scalar(x1[:, t, :], x1[:, t, :], ls_logs[:, t:t + 1], None, ALU.subtract).then_inc(x1_ready, 1)

        @block.tensor
        def _(pe):
            pe.wait_ge(loaded, 16 * 5)
            for n, turn in enumerate(TURNS):
                if n >= 2:
                    pe.wait_ge(wT_out, n - 1)
                for k, (_, src, w) in enumerate(turn):
                    K = src.shape[0]
                    last = pe.transpose(p_w[n % 2][:, k * w:k * w + K], src, ident[0:K, 0:K])
                last.then_inc(wT_done, 1)
            pe.wait_ge(wT_out, len(TURNS))

            def turn_tile(t, i):
                pe.wait_ge(xn_ready, t + 1)
                pe.wait_ge(xT_out, t + 1)
                for k in range(KC):
                    last = pe.transpose(p_x[i][:, k * R:(k + 1) * R], xn[i][:, k * 128:(k + 1) * 128], ident[0:R, 0:R])
                last.then_inc(xT_done, 1)

            def logits_of(t, i):
                pe.wait_ge(xT_out, t + 2 + 1)
                pe.wait_ge(logits_out, t + 1)
                for k in range(KC):
                    last = pe.matmul(p_l[:, 0:NE], xT[i][:, k, :], rT[:, k, :], start=k == 0, stop=k == KC - 1)
                last.then_inc(logits_done, 1)

            turn_tile(0, 0)
            with pe.Fori(0, T // 2 - 1) as u:
                for i in range(2):
                    turn_tile(2 * u + i + 1, 1 - i)
                    logits_of(2 * u + i, i)
            turn_tile(T - 1, 1)
            logits_of(T - 2, 0)
            logits_of(T - 1, 1)
            pe.wait_ge(xT_kept, T + 2)
            n = 0
            for c0, w in CB:
                for f in range(KF):
                    if n >= 2:
                        pe.wait_ge(h_out, n - 1)
                    for k in range(KC):
                        last = pe.matmul(p_h[n % 2][:, 0:w], w1T[:, k, f * 128:(f + 1) * 128], xT_all[:, k, c0:c0 + w],
                                         start=k == 0, stop=k == KC - 1)
                    last.then_inc(h_done, 1)
                    n += 1
            pe.wait_ge(consts, 1)
            pe.wait_ge(chosen, 1)
            for t in range(T):
                to = p_w[t // 8][0:R, t % 8 * NE:(t % 8 + 1) * NE]
                for e in range(t + 1):
                    last = pe.matmul(to, (onesb if e < t else upper)[:, :], selb[:, e, :], start=e == 0, stop=e == t)
            last.then_inc(pos_done, 1)
            pe.wait_ge(h_out, n)
            for t in range(T):
                if t >= 2:
                    pe.wait_ge(y_out, t - 1)
                for f in range(KF):
                    last = pe.matmul(p_y[t % 2][:, :], hT[:, f, t * R:(t + 1) * R], w2T[:, f, :], start=f == 0, stop=f == KF - 1)
                last.then_inc(y_done, 1)

        @block.scalar
        def _(act):
            act.dma_start(r_raw[:, :], router_w).then_inc(loaded, 16)
            act.dma_start(w1_raw[:, :, :], w1.rearrange("(f p) n -> p f n", p=128)).then_inc(loaded, 16)
            act.dma_start(w2_raw[:, :, :], w2.rearrange("(k p) n -> p k n", p=128)).then_inc(loaded, 16)
            for t in range(T):
                act.wait_ge(ls_peak_ready, t + 1)
                if t >= 2:
                    act.wait_ge(ls_exps_done, t - 1)
                act.activation(junk[t % 2][:, :], x1[:, t, :], ACT.Exp, bias=ls_neg_peak[:, t:t + 1],
                               accum_out=ls_sums[:, t:t + 1]).then_inc(ls_exps_done, 1)
            act.wait_ge(ls_exps_done, T)
            act.activation(ls_logs[:, :], ls_sums[:, :], ACT.Ln).then_inc(ls_logs_ready, 1)
            act.wait_ge(var_ready, 1)
            act.activation(std[:, :], ve[:, :], ACT.Sqrt).then_inc(std_ready, 1)

            def keep_xT(t, i):
                act.wait_ge(xT_done, t + 2 + 1)
                act.wait_ge(xT_kept, t + 1)
                act.wait_ge(logits_done, t + 1)
                act.activation(xT[i][:, :, :].rearrange("p k r -> p (k r)"), p_x[i][:, 0:KC * R], ACT.Copy).then_inc(xT_out, 1)

            def keep_logits(t):
                act.wait_ge(logits_done, t + 2 + 1)
                act.activation(logits[:, ds(t, 1), :].rearrange("p a n -> p (a n)"), p_l[:, 0:NE], ACT.Copy)\
                   .then_inc(logits_out, 1)

            keep_xT(0, 0)
            with act.Fori(0, T // 2 - 1) as u:
                for i in range(2):
                    keep_xT(2 * u + i + 1, 1 - i)
                    keep_logits(2 * u + i)
            keep_xT(T - 1, 1)
            keep_logits(T - 2)
            keep_logits(T - 1)
            act.wait_ge(shifted, 1)
            act.activation(probs[:, :, :], logits[:, :, :], ACT.Exp).then_inc(exps, 1)
            n = 0
            for c0, w in CB:
                for f in range(KF):
                    act.wait_ge(h_done, n + 1)
                    act.activation(hT[:, f, c0:c0 + w], p_h[n % 2][:, 0:w], ACT.Gelu, bias=b1c[:, f:f + 1]).then_inc(h_out, 1)
                    n += 1

        @block.vector
        def _(dve):
            link = Chain(dve, chain)
            dve.wait_ge(gnn_bias_loaded, 16)
            for t in range(T):
                link(dve.tensor_tensor_reduce(out=x1[:, t, :], in0=x1[:, t, :], in1=gnn_bias_rows[:, :], scale=1.0,
                                              scalar=-3.0e38, op0=ALU.add, op1=ALU.max, accum_out=ls_peak[:, t:t + 1]))
                dve.tensor_scalar(ls_neg_peak[:, t:t + 1], ls_peak[:, t:t + 1], -1.0, None, ALU.mult).then_inc(ls_peak_ready, 1)
            for n, turn in enumerate(TURNS):
                dve.wait_ge(wT_done, n + 1)
                for k, (to, src, w) in enumerate(turn):
                    ins = dve.tensor_copy(to, p_w[n % 2][:, k * w:k * w + src.shape[0]])
                ins.then_inc(wT_out, 1)
            dve.wait_ge(mix_loaded, 16 * T)
            for t in range(T):
                dve.wait_ge(ls_exps_done, t + 1)
                dve.scalar_tensor_tensor(x1[:, t, :], x1[:, t, :], ls_neg_peak[:, t:t + 1], mix[:, t, :], ALU.add, ALU.add)\
                   .then_inc(summed, 1)
            for t in range(T):
                dve.wait_ge(summed, t + 1)
                ins = dve.bn_stats(stat[:, t, :], x1[:, t, :])
            link(ins)
            for t in range(T):
                ins = dve.bn_aggr(mv[:, t, :], stat[:, t, :])
            link(ins)
            dve.tensor_scalar(ve[:, :], mv[:, :, 1], LN_EPS, None, ALU.add).then_inc(var_ready, 1)
            dve.wait_ge(var_ready, 1)
            one_over_sqrt(dve, link, std[:, :], ve[:, :], rstd[:, :], std_ready, 1, scratch[:, :])

            def normalise(t, i):
                dve.wait_ge(xT_done, t + 1)
                dve.tensor_scalar(xn[i][:, :], x1[:, ds(t, 1), :].rearrange("p a n -> p (a n)"), mv[:, ds(t, 1), 0],
                                  rstd[:, ds(t, 1)], ALU.subtract, ALU.mult).then_inc(xn_ready, 1)

            def keep(t, i):
                dve.wait_ge(xT_out, t + 2 + 1)
                dve.tensor_copy(xT_all[:, :, ds(t * R, R)], xT[i][:, :, :]).then_inc(xT_kept, 1)

            normalise(0, 0)
            with dve.Fori(0, T // 2 - 1) as u:
                for i in range(2):
                    normalise(2 * u + i + 1, 1 - i)
                    keep(2 * u + i, i)
            normalise(T - 1, 1)
            keep(T - 2, 0)
            keep(T - 1, 1)
            dve.wait_ge(logits_out, T + 1)
            link(dve.tensor_reduce(peak[:, :], logits[:, :, :], AX, ALU.max))
            link(dve.tensor_tensor(logits[:, :, :], logits[:, :, :], peak[:, :, None].to_broadcast([R, T, NE]), ALU.subtract))
            dve.sem_inc(shifted, 1)
            dve.wait_ge(exps, 1)
            link(dve.tensor_reduce(total[:, :], probs[:, :, :], AX, ALU.add))
            link(dve.reciprocal(inv[:, :], total[:, :]))
            link(dve.tensor_tensor(probs[:, :, :], probs[:, :, :], inv[:, :, None].to_broadcast([R, T, NE]), ALU.mult))
            for t in range(T):
                ins = dve.max(best[:, t, :], probs[:, t, :])
            link(ins)
            for t in range(T):
                ins = dve.max_index(best_i[:, t, :], best[:, t, :], probs[:, t, :])
            link(ins)
            link(dve.tensor_copy(best_f[:, :, :], best_i[:, :, 0:2]))
            dve.wait_ge(consts, 1)
            which = iota_e[:, None, :].to_broadcast([R, T, NE])
            dve.tensor_tensor(sel[:, :, :], which, best_f[:, :, 0:1].to_broadcast([R, T, NE]), ALU.is_equal)
            link(dve.tensor_tensor(one[:, :, :], which, best_f[:, :, 1:2].to_broadcast([R, T, NE]), ALU.is_equal))
            link(dve.tensor_tensor(sel[:, :, :], sel[:, :, :], one[:, :, :], ALU.add))
            link(dve.tensor_copy(selb[:, :, :], sel[:, :, :]))
            dve.sem_inc(chosen, 1)
            link(dve.tensor_tensor(probs[:, :, :], probs[:, :, :], sel[:, :, :], ALU.mult))
            dve.wait_ge(pos_done, 1)
            for b, (t0, t1) in enumerate(((0, 8), (8, T))):
                ins = dve.tensor_scalar(kept[:, t0:t1, :].rearrange("p t n -> p (t n)"), p_w[b][0:R, 0:(t1 - t0) * NE], float(CAP), None,
                                        ALU.is_lt)
            link(ins)
            link(dve.tensor_tensor(kept[:, :, :], kept[:, :, :], probs[:, :, :], ALU.mult))
            link(dve.tensor_reduce(gate[:, :], kept[:, :, :], AX, ALU.add))
            for t in range(T):
                dve.wait_ge(y_done, t + 1)
                if t >= 1:
                    dve.wait_ge(fin_ready, t)
                dve.tensor_tensor(yb[:, :], p_y[t % 2][:, :], b2b[:, :], ALU.add).then_inc(y_out, 1)
                dve.wait_ge(y_out, t + 1)
                dve.wait_ge(x1_ready, t + 1)
                if t >= 2:
                    dve.wait_ge(stored[t % 2], 16 * (t // 2))
                dve.scalar_tensor_tensor(fin[t % 2][:, :], yb[:, :], gate[:, t:t + 1], x1[:, t, :], ALU.mult, ALU.add)\
                   .then_inc(fin_ready, 1)


def gps_layer(nc, a, out):
    s = Shapes(nc, a["x"], a["src"], a["L0_gnn_W1"], a["L0_gnn_att_src1"], a["L0_gnn_att_src2"], a["L0_mix_w_out"],
               a["L0_ffn_router_w"], a["L0_ffn_w1"])
    N, D, T, H = s.N, s.D, s.T, s.H

    def scratch(name, shape, dt=F32):
        return nc.dram_tensor(name, shape, dt, kind="Internal").ap()

    rows1, rows2 = scratch("a_src1_rows", [H, N]), scratch("a_src2_rows", [H, N])
    mask, mix = scratch("mask", [N, N], BF16), scratch("x_plus_mix", [N, D])
    h1_dram = scratch("h1_rows", [N, s.HC])
    shift_rows = scratch("shift_rows", [H, 3 * N])
    with ExitStack() as ctx:
        def sb(name, shape, dt=F32):
            return ctx.enter_context(nc.sbuf_tensor(name, shape, dt))

        ident, identb = sb("ident", [128, 128]), sb("ident_bf16", [128, 128], BF16)
        adcol1, adcol2 = sb("att1_columns", [R, T, 2 * H]), sb("att2_columns", [R, T, 2 * H])
        w2att = sb("w2_att", [128, s.HC // 128, 2 * H])
        weights = sb("weights_counts_x1", [128, max(s.KC * 3 * D, T * N // 2)])
        w2_sb = weights[:, 0:s.HC // 128 * H * s.C2].rearrange("p (k n) -> p k n", k=s.HC // 128)
        x1 = weights[0:R, 0:T * D].rearrange("p (t n) -> p t n", t=T)
        CT = weights[0:R, 0:T * N // 2].bitcast(U16).rearrange("p (t n) -> p t n", t=T)
        peaks = sb("largest_a_src", [R, T, H])
        constants(nc, s, ident, identb)
        with ExitStack() as counting, ExitStack() as attention:
            cnt = Counting(s, counting, nc)
            W1 = attention.enter_context(nc.sbuf_tensor("w1_then_spare", [128, s.KC * s.HC], F32))
            RB = attention.enter_context(nc.sbuf_tensor("qkv", [128, 8 * N + T * D], F32))
            project(nc, s, cnt, a["src"], a["dst"], a["x"], a["L0_gnn_W1"], a["L0_mix_w_qkv"], a["L0_gnn_att_src1"], a["L0_gnn_att_dst1"],
                    a["L0_gnn_W2"], a["L0_gnn_att_src2"], a["L0_gnn_att_dst2"], W1, weights, RB, ident, adcol1, w2att, h1_dram,
                    rows1)
            s.sems.start_over()
            attend_and_count(nc, s, cnt, a["x"], a["L0_mix_ln_gamma"], a["L0_mix_ln_beta"], a["L0_mix_w_out"],
                             a["L0_mix_b_out"], RB, CT, W1, ident, identb, rows1, mask, mix, peaks)
            attention.close()
            verify_counts(nc, s, cnt)
            s.sems.start_over()
            general_path(nc, s, cnt, CT, ident, identb, rows1, mask, peaks)
        s.sems.start_over()
        as8, as2 = sb("a_src_times_rest", [R, T, H]), sb("a_src_times_slope", [R, T, H])
        with nc.sbuf_tensor("count_logs", [R, T, N], F32) as L, nc.sbuf_tensor("work", [128, T * N], F32) as work:
            with nc.sbuf_tensor("h1", [R, T, H, s.C1 + 1], F32) as h1:
                h1_loaded = s.sems.new("h1_loaded")
                log_counts(nc, s, CT, L, h1_dram, h1, h1_loaded)
                shifts(nc, s, 1, peaks, adcol1, ident, as8, as2, shift_rows)
                gat_sums(nc, s, 1, s.C1, h1, h1_loaded,
                         lambda d0, d1, h: h1[:, d0:d1, ds(h, 1), 0:s.C1].rearrange("p d a c -> p d (a c)"),
                         as8, as2, shift_rows, L, work)
                second_scores(nc, s, h1, a["L0_gnn_b1"], w2att, work, ident, adcol2, rows2)
            s.sems.start_over()
            with nc.sbuf_tensor("h2", [R, T, H, s.C2 + 1], F32) as h2:
                see_sources(nc, s, "layer2", rows2, mask, peaks, beside=second_values(nc, s, a["L0_gnn_W2"], w2_sb, work, h2))
                shifts(nc, s, 2, peaks, adcol2, ident, as8, as2, shift_rows)
                s.sems.start_over()
                gat_sums(nc, s, 2, s.C2, h2, None, lambda d0, d1, h: x1[:, d0:d1, ds(h * s.C2, s.C2)],
                         as8, as2, shift_rows, L, work)
        residual_and_ffn(nc, s, x1, a["L0_gnn_b2"], mix, a["L0_ffn_router_w"], a["L0_ffn_w1"], a["L0_ffn_b1"],
                         a["L0_ffn_w2"], a["L0_ffn_b2"], ident, out)


_INS = ["x", "src", "dst", "L0_gnn_W1", "L0_gnn_att_src1", "L0_gnn_att_dst1", "L0_gnn_b1", "L0_gnn_W2",
        "L0_gnn_att_src2", "L0_gnn_att_dst2", "L0_gnn_b2", "L0_mix_w_qkv", "L0_mix_ln_gamma", "L0_mix_ln_beta",
        "L0_mix_w_out", "L0_mix_b_out", "L0_ffn_router_w", "L0_ffn_w1", "L0_ffn_b1", "L0_ffn_w2", "L0_ffn_b2"]


def kernel(**inputs):
    import numpy as _np
    import concourse.bacc as _bacc
    from concourse.bass_utils import run_bass_kernel_spmd as _run

    nc = _bacc.Bacc("TRN2", target_bir_lowering=False, num_devices=1)
    arrays, args = {}, {}
    for name in _INS:
        a = _np.ascontiguousarray(inputs[name])
        arrays[f"in_{name}"] = a
        args[name] = nc.dram_tensor(f"in_{name}", a.shape, mybir.dt.from_np(a.dtype), kind="ExternalInput").ap()
    out = nc.dram_tensor("out_0", inputs["x"].shape, F32, kind="ExternalOutput").ap()
    gps_layer(nc, args, out)
    return _run(nc, [arrays], core_ids=[0]).results[0]["out_0"]
```
